# Optimizing a Trainium2 kernel written in Bass

```python
import numpy as np
import jax
import jax.numpy as jnp

def _softmax(x, axis=-1):
    return jax.nn.softmax(x, axis=axis)

def _gelu(x):
    return jax.nn.gelu(x, approximate=True)

def _silu(x):
    return jax.nn.silu(x)

def _sigmoid(x):
    return jax.nn.sigmoid(x)

def _layernorm(x, axis=-1, eps=1e-05):
    m = jnp.mean(x, axis=axis, keepdims=True)
    v = jnp.var(x, axis=axis, keepdims=True)
    return (x - m) / jnp.sqrt(v + eps)

def _scatter_add(tgt, idx, src, axis=0):
    return tgt.at[idx].add(src)

def _segment_sum(src, seg, n):
    return jax.ops.segment_sum(src, seg, n)
kernel_name = 'mk_cond_seq_d4_seqx_r4_cd12ad'

def setup_inputs(seed: int=0):
    np.random.seed(seed)
    _w = jnp.asarray

    def _rec_inputs():
        import jax
        import jax.numpy as jnp
        _rk = jax.random.key(seed)
        x = -0.0002928 + 1 * jax.random.normal(jax.random.fold_in(_rk, 1), (8, 512, 256), jnp.float32)
        _lenS = 512 - jax.random.randint(jax.random.fold_in(_rk, 7), (8,), 0, max(1, 512 // 4) + 1, jnp.int32)
        _lenS2 = 512 - jax.random.randint(jax.random.fold_in(_rk, 8), (8,), 0, max(1, 512 // 4) + 1, jnp.int32)
        cond_1024 = 0.0061147 + 1.02565 * jax.random.normal(jax.random.fold_in(_rk, 11), (8, 256), jnp.float32)
        _validS = jnp.arange(512)[None, :] < _lenS[:, None]
        _validS2 = jnp.arange(512)[None, :] < _lenS2[:, None]
        _causal = jnp.tril(jnp.ones((512, 512), dtype=bool))
        mask_BxS_bk1 = jnp.broadcast_to(_validS[:, :], (8, 512))
        return (x, cond_1024, mask_BxS_bk1)
    x, cond_1024, mask_BxS_bk1 = _rec_inputs()

    def _L0_cond_setup():
        import jax, jax.numpy as jnp
        import numpy as np
        D = 256
        H = 16
        HD = D // H
        EPS = 1e-05

        def _ln(x):
            mu = jnp.mean(x, axis=-1, keepdims=True)
            var = jnp.var(x, axis=-1, keepdims=True)
            return (x - mu) * jax.lax.rsqrt(var + EPS)

        def _ada_ln(x, cond, W, b):
            h = _ln(x)
            ss = cond @ W + b
            scale, shift = jnp.split(ss[:, None, :], 2, axis=-1)
            return h * (1.0 + scale) + shift

        def _attn(x, Wq, bq, Wk, bk, Wv, bv, Wo, bo):
            B, L, _ = x.shape

            def heads(y):
                return y.reshape(B, L, H, HD).transpose(0, 2, 1, 3)
            q = heads(x @ Wq + bq)
            k = heads(x @ Wk + bk)
            v = heads(x @ Wv + bv)
            scores = jnp.einsum('bhqd,bhkd->bhqk', q, k) / np.sqrt(HD).astype(x.dtype)
            attn = jax.nn.softmax(scores, axis=-1)
            out = jnp.einsum('bhqk,bhkd->bhqd', attn, v)
            out = out.transpose(0, 2, 1, 3).reshape(B, L, D)
            return out @ Wo + bo
        key = jax.random.key(seed)
        ks = jax.random.split(key, 20)
        s = 0.02
        inp = {'x': jax.random.normal(ks[0], (4, 256, D), jnp.float32), 'cond': jax.random.normal(ks[1], (4, D), jnp.float32), 'Wq': jax.random.normal(ks[2], (D, D), jnp.float32) * s, 'bq': jnp.zeros((D,), jnp.float32), 'Wk': jax.random.normal(ks[3], (D, D), jnp.float32) * s, 'bk': jnp.zeros((D,), jnp.float32), 'Wv': jax.random.normal(ks[4], (D, D), jnp.float32) * s, 'bv': jnp.zeros((D,), jnp.float32), 'Wo': jax.random.normal(ks[5], (D, D), jnp.float32) * s, 'bo': jnp.zeros((D,), jnp.float32), 'Wln1': jax.random.normal(ks[6], (D, 2 * D), jnp.float32) * s, 'bln1': jnp.zeros((2 * D,), jnp.float32), 'Wln2': jax.random.normal(ks[7], (D, 2 * D), jnp.float32) * s, 'bln2': jnp.zeros((2 * D,), jnp.float32), 'W1': jax.random.normal(ks[8], (D, 4 * D), jnp.float32) * s, 'b1': jnp.zeros((4 * D,), jnp.float32), 'W2': jax.random.normal(ks[9], (4 * D, D), jnp.float32) * s, 'b2': jnp.zeros((D,), jnp.float32)}
        return inp
    _L0_cond_all = _L0_cond_setup()
    _L0_cond_in = {k: v for k, v in _L0_cond_all.items() if k in ('Wq', 'bq', 'Wk', 'bk', 'Wv', 'bv', 'Wo', 'bo', 'Wln1', 'bln1', 'Wln2', 'bln2', 'W1', 'b1', 'W2', 'b2')}
    del _L0_cond_all

    def _L1_cond_setup():
        import jax, jax.numpy as jnp
        import numpy as np
        B, T, DIM = (4, 256, 256)
        COND = 256
        HEADS, DH = (16, 64)
        INNER = HEADS * DH
        MLP = 1024
        EPS = 1e-05

        def _layernorm(x):
            mu = jnp.mean(x, axis=-1, keepdims=True)
            var = jnp.mean(jnp.square(x - mu), axis=-1, keepdims=True)
            return (x - mu) * jax.lax.rsqrt(var + EPS)

        def _modulate(x, shift, scale):
            return x * (1.0 + scale) + shift

        def _attention(x, W_qkv, W_out, b_out):
            Bq, Tq, _ = x.shape
            qkv = x @ W_qkv
            q, k, v = jnp.split(qkv, 3, axis=-1)
            q = q.reshape(Bq, Tq, HEADS, DH)
            k = k.reshape(Bq, Tq, HEADS, DH)
            v = v.reshape(Bq, Tq, HEADS, DH)
            scale = DH ** (-0.5)
            attn = jnp.einsum('bqhd,bkhd->bhqk', q, k) * scale
            attn = jax.nn.softmax(attn, axis=-1)
            out = jnp.einsum('bhqk,bkhd->bqhd', attn, v).reshape(Bq, Tq, INNER)
            return out @ W_out + b_out

        def _ff(x, W1, b1, W2, b2):
            return jax.nn.gelu(x @ W1 + b1, approximate=False) @ W2 + b2
        key = jax.random.key(seed)
        ks = jax.random.split(key, 12)
        s = 0.02
        return {'x': jax.random.normal(ks[0], (B, T, DIM), jnp.float32), 'c': jax.random.normal(ks[1], (B, 1, COND), jnp.float32), 'W_mod': jax.random.normal(ks[2], (COND, 6 * DIM), jnp.float32) * s, 'b_mod': jax.random.normal(ks[3], (6 * DIM,), jnp.float32) * s, 'W_qkv': jax.random.normal(ks[4], (DIM, 3 * INNER), jnp.float32) * s, 'W_out': jax.random.normal(ks[5], (INNER, DIM), jnp.float32) * s, 'b_out': jax.random.normal(ks[6], (DIM,), jnp.float32) * s, 'W1': jax.random.normal(ks[7], (DIM, MLP), jnp.float32) * s, 'b1': jax.random.normal(ks[8], (MLP,), jnp.float32) * s, 'W2': jax.random.normal(ks[9], (MLP, DIM), jnp.float32) * s, 'b2': jax.random.normal(ks[10], (DIM,), jnp.float32) * s}
    _L1_cond_all = _L1_cond_setup()
    _L1_cond_in = {k: v for k, v in _L1_cond_all.items() if k in ('W_mod', 'b_mod', 'W_qkv', 'W_out', 'b_out', 'W1', 'b1', 'W2', 'b2')}
    del _L1_cond_all

    def _L2_cond_setup():
        import jax, jax.numpy as jnp
        import numpy as np
        B, N, C = (8, 256, 256)
        H = 16
        HD = C // H
        MLP = 4 * C
        EPS = 1e-06

        def _layernorm(x):
            mu = jnp.mean(x, axis=-1, keepdims=True)
            var = jnp.mean((x - mu) ** 2, axis=-1, keepdims=True)
            return (x - mu) * jax.lax.rsqrt(var + EPS)

        def _modulate(x, shift, scale):
            return x * (1.0 + scale[:, None, :]) + shift[:, None, :]

        def _attention(x, padding_mask, qkv_w, qkv_b, proj_w, proj_b):
            b, n, cdim = x.shape
            qkv = x @ qkv_w.T + qkv_b
            qkv = qkv.reshape(b, n, 3, H, HD).transpose(2, 0, 3, 1, 4)
            q, k, v = (qkv[0], qkv[1], qkv[2])
            scale = HD ** (-0.5)
            attn = jnp.einsum('bhnd,bhmd->bhnm', q, k) * scale
            mask = padding_mask[:, None, :] & padding_mask[:, :, None]
            attn = jnp.where(mask[:, None, :, :], attn, -1000000000.0)
            attn = jax.nn.softmax(attn, axis=-1)
            out = jnp.einsum('bhnm,bhmd->bhnd', attn, v)
            out = out.transpose(0, 2, 1, 3).reshape(b, n, cdim)
            return out @ proj_w.T + proj_b
        key = jax.random.key(seed)
        ks = jax.random.split(key, 12)
        x = jax.random.normal(ks[0], (B, N, C), dtype=jnp.float32)
        c = jax.random.normal(ks[1], (B, C), dtype=jnp.float32)
        lengths = jax.random.randint(ks[2], (B,), N // 2, N + 1)
        padding_mask = jnp.arange(N)[None, :] < lengths[:, None]
        s = 0.02
        qkv_w = jax.random.normal(ks[3], (3 * C, C), dtype=jnp.float32) * s
        qkv_b = jnp.zeros((3 * C,), dtype=jnp.float32)
        proj_w = jax.random.normal(ks[4], (C, C), dtype=jnp.float32) * s
        proj_b = jnp.zeros((C,), dtype=jnp.float32)
        fc1_w = jax.random.normal(ks[5], (MLP, C), dtype=jnp.float32) * s
        fc1_b = jnp.zeros((MLP,), dtype=jnp.float32)
        fc2_w = jax.random.normal(ks[6], (C, MLP), dtype=jnp.float32) * s
        fc2_b = jnp.zeros((C,), dtype=jnp.float32)
        ada_w = jax.random.normal(ks[7], (6 * C, C), dtype=jnp.float32) * s
        ada_b = jnp.zeros((6 * C,), dtype=jnp.float32)
        return {'x': x, 'c': c, 'padding_mask': padding_mask, 'qkv_w': qkv_w, 'qkv_b': qkv_b, 'proj_w': proj_w, 'proj_b': proj_b, 'fc1_w': fc1_w, 'fc1_b': fc1_b, 'fc2_w': fc2_w, 'fc2_b': fc2_b, 'ada_w': ada_w, 'ada_b': ada_b}
    _L2_cond_all = _L2_cond_setup()
    _L2_cond_in = {k: v for k, v in _L2_cond_all.items() if k in ('qkv_w', 'qkv_b', 'proj_w', 'proj_b', 'fc1_w', 'fc1_b', 'fc2_w', 'fc2_b', 'ada_w', 'ada_b')}
    del _L2_cond_all

    def _L3_cond_setup():
        import jax, jax.numpy as jnp
        import numpy as np
        B, L = (2, 256)
        D_MODEL = 256
        D_STATE = 32
        D_CONV = 4
        D_INNER = 2 * D_MODEL
        DT_RANK = D_MODEL // 16
        HIDDEN = (int(2 / 3 * 2 * D_MODEL) + 63) // 64 * 64
        COND = D_MODEL

        def _silu(x):
            return x * jax.nn.sigmoid(x)

        def _ln(x, w, b):
            m = x.mean(-1, keepdims=True)
            v = ((x - m) ** 2).mean(-1, keepdims=True)
            return (x - m) / jnp.sqrt(v + 1e-05) * w + b

        def _mamba(h, in_proj_W, conv_w, conv_b, x_proj_W, dt_proj_W, dt_proj_b, A_log, Dp, out_proj_W):
            xz = h @ in_proj_W
            x, z = jnp.split(xz, 2, axis=-1)
            xc = jnp.transpose(x, (0, 2, 1))
            xc = jax.lax.conv_general_dilated(xc, conv_w, (1,), [(D_CONV - 1, 0)], feature_group_count=D_INNER, dimension_numbers=('NCH', 'OIH', 'NCH'))
            x = _silu(jnp.transpose(xc, (0, 2, 1)) + conv_b)
            xdbl = x @ x_proj_W
            dt = jax.nn.softplus(xdbl[..., :DT_RANK] @ dt_proj_W + dt_proj_b)
            Bm = xdbl[..., DT_RANK:DT_RANK + D_STATE]
            Cm = xdbl[..., DT_RANK + D_STATE:]
            A = -jnp.exp(A_log)

            def step(hst, inp):
                dt_t, B_t, C_t, x_t = inp
                dA = jnp.exp(dt_t[:, :, None] * A)
                hst = hst * dA + dt_t[:, :, None] * B_t[:, None, :] * x_t[:, :, None]
                y = jnp.einsum('bdn,bn->bd', hst, C_t)
                return (hst, y)
            h0 = jnp.zeros((h.shape[0], D_INNER, D_STATE), h.dtype)
            seq = (jnp.swapaxes(dt, 0, 1), jnp.swapaxes(Bm, 0, 1), jnp.swapaxes(Cm, 0, 1), jnp.swapaxes(x, 0, 1))
            _, ys = jax.lax.scan(step, h0, seq)
            y = jnp.swapaxes(ys, 0, 1) + Dp * x
            return y * _silu(z) @ out_proj_W
        key = jax.random.key(seed)
        ks = jax.random.split(key, 16)
        f = lambda k, s, sc=0.02: jax.random.normal(k, s, jnp.float32) * sc
        return {'x': jax.random.normal(ks[0], (B, L, D_MODEL), jnp.float32), 'cond': jax.random.normal(ks[1], (B, COND), jnp.float32), 'norm1_w': jnp.ones((D_MODEL,), jnp.float32), 'norm1_b': jnp.zeros((D_MODEL,), jnp.float32), 'norm2_w': jnp.ones((D_MODEL,), jnp.float32), 'norm2_b': jnp.zeros((D_MODEL,), jnp.float32), 'adaln1_W': f(ks[2], (COND, 3 * D_MODEL)), 'adaln1_b': jnp.zeros((3 * D_MODEL,), jnp.float32), 'adaln2_W': f(ks[3], (COND, 3 * D_MODEL)), 'adaln2_b': jnp.zeros((3 * D_MODEL,), jnp.float32), 'in_proj_W': f(ks[4], (D_MODEL, 2 * D_INNER)), 'conv_w': f(ks[5], (D_INNER, 1, D_CONV), 0.1), 'conv_b': jnp.zeros((D_INNER,), jnp.float32), 'x_proj_W': f(ks[6], (D_INNER, DT_RANK + 2 * D_STATE)), 'dt_proj_W': f(ks[7], (DT_RANK, D_INNER), 0.1), 'dt_proj_b': jnp.full((D_INNER,), float(np.log(np.expm1(0.01))), jnp.float32), 'A_log': jnp.log(jnp.tile(jnp.arange(1, D_STATE + 1, dtype=jnp.float32), (D_INNER, 1))), 'Dp': jnp.ones((D_INNER,), jnp.float32), 'out_proj_W': f(ks[8], (D_INNER, D_MODEL)), 'w1': f(ks[9], (D_MODEL, HIDDEN)), 'w2': f(ks[10], (D_MODEL, HIDDEN)), 'w3': f(ks[11], (HIDDEN, D_MODEL))}
    _L3_cond_all = _L3_cond_setup()
    _L3_cond_in = {k: v for k, v in _L3_cond_all.items() if k in ('norm1_w', 'norm1_b', 'norm2_w', 'norm2_b', 'adaln1_W', 'adaln1_b', 'adaln2_W', 'adaln2_b', 'in_proj_W', 'conv_w', 'conv_b', 'x_proj_W', 'dt_proj_W', 'dt_proj_b', 'A_log', 'Dp', 'out_proj_W', 'w1', 'w2', 'w3')}
    del _L3_cond_all
    return {'x': x, 'cond_1024': cond_1024, 'mask_BxS_bk1': mask_BxS_bk1, 'L0_cond_Wq': _L0_cond_in['Wq'], 'L0_cond_bq': _L0_cond_in['bq'], 'L0_cond_Wk': _L0_cond_in['Wk'], 'L0_cond_bk': _L0_cond_in['bk'], 'L0_cond_Wv': _L0_cond_in['Wv'], 'L0_cond_bv': _L0_cond_in['bv'], 'L0_cond_Wo': _L0_cond_in['Wo'], 'L0_cond_bo': _L0_cond_in['bo'], 'L0_cond_Wln1': _L0_cond_in['Wln1'], 'L0_cond_bln1': _L0_cond_in['bln1'], 'L0_cond_Wln2': _L0_cond_in['Wln2'], 'L0_cond_bln2': _L0_cond_in['bln2'], 'L0_cond_W1': _L0_cond_in['W1'], 'L0_cond_b1': _L0_cond_in['b1'], 'L0_cond_W2': _L0_cond_in['W2'], 'L0_cond_b2': _L0_cond_in['b2'], 'L1_cond_W_mod': _L1_cond_in['W_mod'], 'L1_cond_b_mod': _L1_cond_in['b_mod'], 'L1_cond_W_qkv': _L1_cond_in['W_qkv'], 'L1_cond_W_out': _L1_cond_in['W_out'], 'L1_cond_b_out': _L1_cond_in['b_out'], 'L1_cond_W1': _L1_cond_in['W1'], 'L1_cond_b1': _L1_cond_in['b1'], 'L1_cond_W2': _L1_cond_in['W2'], 'L1_cond_b2': _L1_cond_in['b2'], 'L2_cond_qkv_w': _L2_cond_in['qkv_w'], 'L2_cond_qkv_b': _L2_cond_in['qkv_b'], 'L2_cond_proj_w': _L2_cond_in['proj_w'], 'L2_cond_proj_b': _L2_cond_in['proj_b'], 'L2_cond_fc1_w': _L2_cond_in['fc1_w'], 'L2_cond_fc1_b': _L2_cond_in['fc1_b'], 'L2_cond_fc2_w': _L2_cond_in['fc2_w'], 'L2_cond_fc2_b': _L2_cond_in['fc2_b'], 'L2_cond_ada_w': _L2_cond_in['ada_w'], 'L2_cond_ada_b': _L2_cond_in['ada_b'], 'L3_cond_norm1_w': _L3_cond_in['norm1_w'], 'L3_cond_norm1_b': _L3_cond_in['norm1_b'], 'L3_cond_norm2_w': _L3_cond_in['norm2_w'], 'L3_cond_norm2_b': _L3_cond_in['norm2_b'], 'L3_cond_adaln1_W': _L3_cond_in['adaln1_W'], 'L3_cond_adaln1_b': _L3_cond_in['adaln1_b'], 'L3_cond_adaln2_W': _L3_cond_in['adaln2_W'], 'L3_cond_adaln2_b': _L3_cond_in['adaln2_b'], 'L3_cond_in_proj_W': _L3_cond_in['in_proj_W'], 'L3_cond_conv_w': _L3_cond_in['conv_w'], 'L3_cond_conv_b': _L3_cond_in['conv_b'], 'L3_cond_x_proj_W': _L3_cond_in['x_proj_W'], 'L3_cond_dt_proj_W': _L3_cond_in['dt_proj_W'], 'L3_cond_dt_proj_b': _L3_cond_in['dt_proj_b'], 'L3_cond_A_log': _L3_cond_in['A_log'], 'L3_cond_Dp': _L3_cond_in['Dp'], 'L3_cond_out_proj_W': _L3_cond_in['out_proj_W'], 'L3_cond_w1': _L3_cond_in['w1'], 'L3_cond_w2': _L3_cond_in['w2'], 'L3_cond_w3': _L3_cond_in['w3']}

def reference(x, cond_1024, mask_BxS_bk1, L0_cond_Wq, L0_cond_bq, L0_cond_Wk, L0_cond_bk, L0_cond_Wv, L0_cond_bv, L0_cond_Wo, L0_cond_bo, L0_cond_Wln1, L0_cond_bln1, L0_cond_Wln2, L0_cond_bln2, L0_cond_W1, L0_cond_b1, L0_cond_W2, L0_cond_b2, L1_cond_W_mod, L1_cond_b_mod, L1_cond_W_qkv, L1_cond_W_out, L1_cond_b_out, L1_cond_W1, L1_cond_b1, L1_cond_W2, L1_cond_b2, L2_cond_qkv_w, L2_cond_qkv_b, L2_cond_proj_w, L2_cond_proj_b, L2_cond_fc1_w, L2_cond_fc1_b, L2_cond_fc2_w, L2_cond_fc2_b, L2_cond_ada_w, L2_cond_ada_b, L3_cond_norm1_w, L3_cond_norm1_b, L3_cond_norm2_w, L3_cond_norm2_b, L3_cond_adaln1_W, L3_cond_adaln1_b, L3_cond_adaln2_W, L3_cond_adaln2_b, L3_cond_in_proj_W, L3_cond_conv_w, L3_cond_conv_b, L3_cond_x_proj_W, L3_cond_dt_proj_W, L3_cond_dt_proj_b, L3_cond_A_log, L3_cond_Dp, L3_cond_out_proj_W, L3_cond_w1, L3_cond_w2, L3_cond_w3):
    import jax
    import jax.numpy as jnp

    def _L0_cond_ref(x, cond, Wq, bq, Wk, bk, Wv, bv, Wo, bo, Wln1, bln1, Wln2, bln2, W1, b1, W2, b2):
        import jax, jax.numpy as jnp
        import numpy as np
        D = 256
        H = 16
        HD = D // H
        EPS = 1e-05

        def _ln(x):
            mu = jnp.mean(x, axis=-1, keepdims=True)
            var = jnp.var(x, axis=-1, keepdims=True)
            return (x - mu) * jax.lax.rsqrt(var + EPS)

        def _ada_ln(x, cond, W, b):
            h = _ln(x)
            ss = cond @ W + b
            scale, shift = jnp.split(ss[:, None, :], 2, axis=-1)
            return h * (1.0 + scale) + shift

        def _attn(x, Wq, bq, Wk, bk, Wv, bv, Wo, bo):
            B, L, _ = x.shape

            def heads(y):
                return y.reshape(B, L, H, HD).transpose(0, 2, 1, 3)
            q = heads(x @ Wq + bq)
            k = heads(x @ Wk + bk)
            v = heads(x @ Wv + bv)
            scores = jnp.einsum('bhqd,bhkd->bhqk', q, k) / np.sqrt(HD).astype(x.dtype)
            attn = jax.nn.softmax(scores, axis=-1)
            out = jnp.einsum('bhqk,bhkd->bhqd', attn, v)
            out = out.transpose(0, 2, 1, 3).reshape(B, L, D)
            return out @ Wo + bo
        h = _ada_ln(x, cond, Wln1, bln1)
        x = x + _attn(h, Wq, bq, Wk, bk, Wv, bv, Wo, bo)
        h = _ada_ln(x, cond, Wln2, bln2)
        mlp = jax.nn.gelu(h @ W1 + b1, approximate=False) @ W2 + b2
        return x + mlp

    def _L1_cond_ref(x, c, W_mod, b_mod, W_qkv, W_out, b_out, W1, b1, W2, b2):
        import jax, jax.numpy as jnp
        import numpy as np
        B, T, DIM = (4, 256, 256)
        COND = 256
        HEADS, DH = (16, 64)
        INNER = HEADS * DH
        MLP = 1024
        EPS = 1e-05

        def _layernorm(x):
            mu = jnp.mean(x, axis=-1, keepdims=True)
            var = jnp.mean(jnp.square(x - mu), axis=-1, keepdims=True)
            return (x - mu) * jax.lax.rsqrt(var + EPS)

        def _modulate(x, shift, scale):
            return x * (1.0 + scale) + shift

        def _attention(x, W_qkv, W_out, b_out):
            Bq, Tq, _ = x.shape
            qkv = x @ W_qkv
            q, k, v = jnp.split(qkv, 3, axis=-1)
            q = q.reshape(Bq, Tq, HEADS, DH)
            k = k.reshape(Bq, Tq, HEADS, DH)
            v = v.reshape(Bq, Tq, HEADS, DH)
            scale = DH ** (-0.5)
            attn = jnp.einsum('bqhd,bkhd->bhqk', q, k) * scale
            attn = jax.nn.softmax(attn, axis=-1)
            out = jnp.einsum('bhqk,bkhd->bqhd', attn, v).reshape(Bq, Tq, INNER)
            return out @ W_out + b_out

        def _ff(x, W1, b1, W2, b2):
            return jax.nn.gelu(x @ W1 + b1, approximate=False) @ W2 + b2
        mod = jax.nn.silu(c) @ W_mod + b_mod
        sh_msa, sc_msa, g_msa, sh_mlp, sc_mlp, g_mlp = jnp.split(mod, 6, axis=-1)
        x = x + g_msa * _attention(_modulate(_layernorm(x), sh_msa, sc_msa), W_qkv, W_out, b_out)
        x = x + g_mlp * _ff(_modulate(_layernorm(x), sh_mlp, sc_mlp), W1, b1, W2, b2)
        return x

    def _L2_cond_ref(x, c, padding_mask, qkv_w, qkv_b, proj_w, proj_b, fc1_w, fc1_b, fc2_w, fc2_b, ada_w, ada_b):
        import jax, jax.numpy as jnp
        import numpy as np
        B, N, C = (8, 256, 256)
        H = 16
        HD = C // H
        MLP = 4 * C
        EPS = 1e-06

        def _layernorm(x):
            mu = jnp.mean(x, axis=-1, keepdims=True)
            var = jnp.mean((x - mu) ** 2, axis=-1, keepdims=True)
            return (x - mu) * jax.lax.rsqrt(var + EPS)

        def _modulate(x, shift, scale):
            return x * (1.0 + scale[:, None, :]) + shift[:, None, :]

        def _attention(x, padding_mask, qkv_w, qkv_b, proj_w, proj_b):
            b, n, cdim = x.shape
            qkv = x @ qkv_w.T + qkv_b
            qkv = qkv.reshape(b, n, 3, H, HD).transpose(2, 0, 3, 1, 4)
            q, k, v = (qkv[0], qkv[1], qkv[2])
            scale = HD ** (-0.5)
            attn = jnp.einsum('bhnd,bhmd->bhnm', q, k) * scale
            mask = padding_mask[:, None, :] & padding_mask[:, :, None]
            attn = jnp.where(mask[:, None, :, :], attn, -1000000000.0)
            attn = jax.nn.softmax(attn, axis=-1)
            out = jnp.einsum('bhnm,bhmd->bhnd', attn, v)
            out = out.transpose(0, 2, 1, 3).reshape(b, n, cdim)
            return out @ proj_w.T + proj_b
        mod = jax.nn.silu(c) @ ada_w.T + ada_b
        shift_msa, scale_msa, gate_msa, shift_mlp, scale_mlp, gate_mlp = jnp.split(mod, 6, axis=1)
        h = _modulate(_layernorm(x), shift_msa, scale_msa)
        x = x + gate_msa[:, None, :] * _attention(h, padding_mask, qkv_w, qkv_b, proj_w, proj_b)
        h = _modulate(_layernorm(x), shift_mlp, scale_mlp)
        h = jax.nn.gelu(h @ fc1_w.T + fc1_b, approximate=True) @ fc2_w.T + fc2_b
        x = x + gate_mlp[:, None, :] * h
        return x

    def _L3_cond_ref(x, cond, norm1_w, norm1_b, norm2_w, norm2_b, adaln1_W, adaln1_b, adaln2_W, adaln2_b, in_proj_W, conv_w, conv_b, x_proj_W, dt_proj_W, dt_proj_b, A_log, Dp, out_proj_W, w1, w2, w3):
        import jax, jax.numpy as jnp
        import numpy as np
        B, L = (2, 256)
        D_MODEL = 256
        D_STATE = 32
        D_CONV = 4
        D_INNER = 2 * D_MODEL
        DT_RANK = D_MODEL // 16
        HIDDEN = (int(2 / 3 * 2 * D_MODEL) + 63) // 64 * 64
        COND = D_MODEL

        def _silu(x):
            return x * jax.nn.sigmoid(x)

        def _ln(x, w, b):
            m = x.mean(-1, keepdims=True)
            v = ((x - m) ** 2).mean(-1, keepdims=True)
            return (x - m) / jnp.sqrt(v + 1e-05) * w + b

        def _mamba(h, in_proj_W, conv_w, conv_b, x_proj_W, dt_proj_W, dt_proj_b, A_log, Dp, out_proj_W):
            xz = h @ in_proj_W
            x, z = jnp.split(xz, 2, axis=-1)
            xc = jnp.transpose(x, (0, 2, 1))
            xc = jax.lax.conv_general_dilated(xc, conv_w, (1,), [(D_CONV - 1, 0)], feature_group_count=D_INNER, dimension_numbers=('NCH', 'OIH', 'NCH'))
            x = _silu(jnp.transpose(xc, (0, 2, 1)) + conv_b)
            xdbl = x @ x_proj_W
            dt = jax.nn.softplus(xdbl[..., :DT_RANK] @ dt_proj_W + dt_proj_b)
            Bm = xdbl[..., DT_RANK:DT_RANK + D_STATE]
            Cm = xdbl[..., DT_RANK + D_STATE:]
            A = -jnp.exp(A_log)

            def step(hst, inp):
                dt_t, B_t, C_t, x_t = inp
                dA = jnp.exp(dt_t[:, :, None] * A)
                hst = hst * dA + dt_t[:, :, None] * B_t[:, None, :] * x_t[:, :, None]
                y = jnp.einsum('bdn,bn->bd', hst, C_t)
                return (hst, y)
            h0 = jnp.zeros((h.shape[0], D_INNER, D_STATE), h.dtype)
            seq = (jnp.swapaxes(dt, 0, 1), jnp.swapaxes(Bm, 0, 1), jnp.swapaxes(Cm, 0, 1), jnp.swapaxes(x, 0, 1))
            _, ys = jax.lax.scan(step, h0, seq)
            y = jnp.swapaxes(ys, 0, 1) + Dp * x
            return y * _silu(z) @ out_proj_W
        sc = _silu(cond)
        sh1, s1, g1 = jnp.split(sc @ adaln1_W + adaln1_b, 3, axis=-1)
        sh2, s2, g2 = jnp.split(sc @ adaln2_W + adaln2_b, 3, axis=-1)
        mp = (in_proj_W, conv_w, conv_b, x_proj_W, dt_proj_W, dt_proj_b, A_log, Dp, out_proj_W)
        h = _ln(x, norm1_w, norm1_b)
        h = h * (1.0 + s1[:, None, :]) + sh1[:, None, :]
        fwd = _mamba(h, *mp)
        bwd = jnp.flip(_mamba(jnp.flip(h, 1), *mp), 1)
        x = x + g1[:, None, :] * (fwd + bwd)
        h = _ln(x, norm2_w, norm2_b)
        h = h * (1.0 + s2[:, None, :]) + sh2[:, None, :]
        mlp = _silu(h @ w1) * (h @ w2) @ w3
        return x + g2[:, None, :] * mlp
    x = _L0_cond_ref(x, cond_1024, L0_cond_Wq, L0_cond_bq, L0_cond_Wk, L0_cond_bk, L0_cond_Wv, L0_cond_bv, L0_cond_Wo, L0_cond_bo, L0_cond_Wln1, L0_cond_bln1, L0_cond_Wln2, L0_cond_bln2, L0_cond_W1, L0_cond_b1, L0_cond_W2, L0_cond_b2)
    x = _L1_cond_ref(x, cond_1024[:, None, :], L1_cond_W_mod, L1_cond_b_mod, L1_cond_W_qkv, L1_cond_W_out, L1_cond_b_out, L1_cond_W1, L1_cond_b1, L1_cond_W2, L1_cond_b2)
    x = _L2_cond_ref(x, cond_1024, mask_BxS_bk1, L2_cond_qkv_w, L2_cond_qkv_b, L2_cond_proj_w, L2_cond_proj_b, L2_cond_fc1_w, L2_cond_fc1_b, L2_cond_fc2_w, L2_cond_fc2_b, L2_cond_ada_w, L2_cond_ada_b)
    x = _L3_cond_ref(x, cond_1024, L3_cond_norm1_w, L3_cond_norm1_b, L3_cond_norm2_w, L3_cond_norm2_b, L3_cond_adaln1_W, L3_cond_adaln1_b, L3_cond_adaln2_W, L3_cond_adaln2_b, L3_cond_in_proj_W, L3_cond_conv_w, L3_cond_conv_b, L3_cond_x_proj_W, L3_cond_dt_proj_W, L3_cond_dt_proj_b, L3_cond_A_log, L3_cond_Dp, L3_cond_out_proj_W, L3_cond_w1, L3_cond_w2, L3_cond_w3)
    return x

_drawn_inputs = setup_inputs


def setup_inputs(seed=0):
    import zlib

    import numpy as np

    out = dict(_drawn_inputs(seed))
    spreads = {'L0_cond_bq': (0.0, 0.1),
     'L0_cond_bk': (0.0, 0.1),
     'L0_cond_bv': (0.0, 0.1),
     'L0_cond_bo': (0.0, 0.1),
     'L0_cond_bln1': (0.0, 0.1),
     'L0_cond_bln2': (0.0, 0.1),
     'L0_cond_b1': (0.0, 0.1),
     'L0_cond_b2': (0.0, 0.1),
     'L2_cond_qkv_b': (0.0, 0.1),
     'L2_cond_proj_b': (0.0, 0.1),
     'L2_cond_fc1_b': (0.0, 0.1),
     'L2_cond_fc2_b': (0.0, 0.1),
     'L2_cond_ada_b': (0.0, 0.1),
     'L3_cond_norm1_w': (1.0, 0.2),
     'L3_cond_norm1_b': (0.0, 0.1),
     'L3_cond_norm2_w': (1.0, 0.2),
     'L3_cond_norm2_b': (0.0, 0.1),
     'L3_cond_adaln1_b': (0.0, 0.1),
     'L3_cond_adaln2_b': (0.0, 0.1),
     'L3_cond_conv_b': (0.0, 0.1),
     'L3_cond_dt_proj_b': (-4.600165843963623, 0.2),
     'L3_cond_Dp': (1.0, 0.2)}
    factors = {}
    for name, (base, spread) in spreads.items():
        noise = np.random.default_rng([zlib.crc32(name.encode()), seed]).standard_normal(out[name].shape)
        drawn = base * np.exp(spread * noise) if base else spread * noise
        out[name] = jnp.asarray(drawn.astype(out[name].dtype))
    for name, factor in factors.items():
        out[name] = (out[name] * factor).astype(out[name].dtype)
    return out
```

```python
import concourse.bass as bass
from concourse import mybir
from contextlib import ExitStack

FP32 = mybir.dt.float32
BF16 = mybir.dt.bfloat16
U8 = mybir.dt.uint8
ALU = mybir.AluOpType
ACT = mybir.ActivationFunctionType
AX = mybir.AxisListType

P = 128
B, T, D = 8, 512, 256
TT = T // P
DC = D // P
H = 16
GH = 4
NG = H // GH
MLP = 4 * D
MC = MLP // P
SPLIT = 3
Q_PART = (0, 0, 1, 1, 0, 2)
K_PART = (0, 1, 0, 1, 2, 0)
HD = 16
STACK = HD * len(Q_PART)
HD1 = 64
INNER1 = H * HD1
DI = 2 * D
IC = DI // P
NS = 32
DTR = D // 16
DPU = P // NS
UB = NS // DPU
NB = P // NS
TAPS = 4
HID = (int(2 / 3 * 2 * D) + 63) // 64 * 64
HC = HID // P

MOD0, MOD1, MOD2, MOD3 = 0, 4 * DC, 10 * DC, 16 * DC
MODS = 22 * DC


class Semaphores:

    def __init__(self, pool, names):
        assert len(set(names)) == len(names) <= len(pool)
        self.range = range(pool[0].num, pool[0].num + len(pool))
        assert [s.num for s in pool] == list(self.range)
        self.of = dict(zip(names, pool))

    def __getitem__(self, name):
        return self.of[name]


LN_SEMS = ["stats", "aggr", "var_eps", "rstd", "xn", "hT_filled", "hT"]


class Norm:

    def __init__(self, sb, S, x, cur, ident, half, banks, eps):
        self.S, self.x, self.cur, self.ident, self.half, self.banks, self.eps = S, x, cur, ident, half, banks, eps
        self.st = sb("ln_stats", [P, TT, 6], FP32)
        self.mv = sb("ln_mean_var", [P, TT, 2], FP32)
        self.ve = sb("ln_var_eps", [P, TT], FP32)
        self.rs = sb("ln_rstd", [P, TT], FP32)
        self.xn = sb("ln_xn", [P, TT, D], FP32)
        self.hT = sb("ln_hT", [P, DC, T], FP32)

    def vector(self, nc, dve, b, n):
        S = self.S
        for t in range(TT):
            nc.vector.bn_stats(self.st[:, t, :], self.x(b)[:, t, :]).then_inc(S["stats"], 1)
        dve.wait_ge(S["stats"], TT * (n + 1))
        for t in range(TT):
            nc.vector.bn_aggr(self.mv[:, t, :], self.st[:, t, :]).then_inc(S["aggr"], 1)
        dve.wait_ge(S["rstd"], n + 1)
        for t in range(TT):
            nc.vector.tensor_scalar(self.xn[:, t, :], self.x(b)[:, t, :], self.mv[:, t, 0:1], self.rs[:, t:t + 1],
                                    ALU.subtract, ALU.mult).then_inc(S["xn"], 1)

    def gpsimd(self, nc, pool, n):
        S = self.S
        pool.wait_ge(S["aggr"], TT * (n + 1))
        nc.gpsimd.tensor_scalar(self.ve[:, :], self.mv[:, :, 1], self.eps, None, ALU.add).then_inc(S["var_eps"], 1)
        pool.wait_ge(S["var_eps"], n + 1)
        nc.gpsimd.tensor_tensor(self.rs[:, :], self.ve[:, :], self.half[:, :], ALU.pow).then_inc(S["rstd"], 1)

    def tensor(self, nc, pe, n):
        S = self.S
        pe.wait_ge(S["xn"], TT * (n + 1))
        for c in range(DC):
            for t in range(TT):
                last = nc.tensor.transpose(self.banks[c][:, t * P:(t + 1) * P], self.xn[:, t, c * P:(c + 1) * P],
                                           self.ident[:, :])
            last.then_inc(S["hT_filled"], 1)

    def scalar(self, nc, act, n, scale, shift):
        S = self.S
        for c in range(DC):
            act.wait_ge(S["hT_filled"], DC * n + c + 1)
            nc.scalar.activation(self.hT[:, c, :], self.banks[c][:, :], ACT.Identity,
                                 bias=self.cur[:, shift + c:shift + c + 1],
                                 scale=self.cur[:, scale + c:scale + c + 1]).then_inc(S["hT"], 1)


class Gates:

    def __init__(self, sb, S, cur, ident, ones, bank, columns):
        self.S, self.cur, self.ident, self.ones, self.bank, self.columns = S, cur, ident, ones, bank, columns
        self.diag = sb("gate_diag", [P, len(columns), D], FP32)
        self.rows = sb("gate_rows", [P, len(columns), D], FP32)

    def vector(self, nc, dve):
        for k, column in enumerate(self.columns):
            for c in range(DC):
                nc.vector.tensor_scalar(self.diag[:, k, c * P:(c + 1) * P], self.ident[:, :],
                                        self.cur[:, column + c:column + c + 1], None,
                                        ALU.mult).then_inc(self.S["gate_diag"], 1)

    def tensor(self, nc, pe):
        pe.wait_ge(self.S["gate_diag"], DC * len(self.columns))
        for k in range(len(self.columns)):
            last = nc.tensor.matmul(self.bank[:, k * D:(k + 1) * D], self.ones[:, :], self.diag[:, k, :],
                                    start=True, stop=True)
        last.then_inc(self.S["gate_filled"], 1)

    def scalar(self, nc, act):
        act.wait_ge(self.S["gate_filled"], 1)
        nc.scalar.activation(self.rows[:, :, :].rearrange("p k n -> p (k n)"), self.bank[:, 0:len(self.columns) * D],
                             ACT.Copy).then_inc(self.S["gate_rows"], 1)


def residual(nc, dve, S, banks, bias, gate, tmp, x_b, n, filled):
    steps = (bias is not None) + (gate is not None) + 1
    for k in range(2):
        done = 2 * steps * n + steps * k
        dve.wait_ge(S[filled], k + 1)
        y = banks[k][:, :].rearrange("p (t n) -> p t n", t=2)
        over = lambda row: row.unsqueeze(1).broadcast_to([P, 2, D])
        rows = [(row, op) for row, op in ((bias, ALU.add), (gate, ALU.mult)) if row is not None]
        for n_row, (row, op) in enumerate(rows):
            nc.vector.tensor_tensor(tmp[:, k, :, :], tmp[:, k, :, :] if n_row else y, over(row), op)\
                .then_inc(S["res"], 1)
            dve.wait_ge(S["res"], done + n_row + 1)
        x = x_b[:, 2 * k:2 * k + 2, :]
        nc.vector.tensor_tensor(x, x, tmp[:, k, :, :], ALU.add).then_inc(S["res"], 1)
    dve.wait_ge(S["res"], 2 * steps * (n + 1))


def mlp_tensor(nc, pe, S, banks, hT, w1, w2, g, n_hT):
    pe.wait_ge(S["hT"], n_hT)
    for j in range(MC):
        if j >= 4:
            pe.wait_ge(S["gelu"], j - 3)
        for c in range(DC):
            last = nc.tensor.matmul(banks[2 + j % 4][:, :], w1[:, c, j * P:(j + 1) * P], hT[:, c, :],
                                    start=(c == 0), stop=(c == DC - 1))
        last.then_inc(S["up_filled"], 1)
    pe.wait_ge(S["gelu"], MC)
    for t in range(TT):
        for j in range(MC):
            last = nc.tensor.matmul(banks[6 + t // 2][:, (t % 2) * D:(t % 2 + 1) * D], g[:, j, t * P:(t + 1) * P],
                                    w2[:, j, :], start=(j == 0), stop=(j == MC - 1))
        if t % 2:
            last.then_inc(S["down_filled"], 1)


def mlp_scalar(nc, act, S, banks, b1, g, func):
    for j in range(MC):
        act.wait_ge(S["up_filled"], j + 1)
        nc.scalar.activation(g[:, j, :], banks[2 + j % 4][:, :], func, bias=b1[:, j:j + 1]).then_inc(S["gelu"], 1)


def modulation(nc, consts, io):
    ident, ones, mod = consts["ident"], consts["ones"], consts["mod"]
    with ExitStack() as ctx:
        sb = lambda n, s, d: ctx.enter_context(nc.sbuf_tensor(n, s, d))
        w = sb("mod_w", [P, DC, MODS * P], FP32)
        bias = sb("mod_bias", [P, MODS], FP32)
        nw = sb("mod_norm_w", [P, 2 * DC], FP32)
        nb = sb("mod_norm_b", [P, 2 * DC], FP32)
        cT = sb("mod_cT", [P, DC, B], FP32)
        scT = sb("mod_silu_cT", [P, DC, B], FP32)
        acc = ctx.enter_context(nc.psum_tensor("mod_acc", [P, MODS, B], FP32))
        s_in = ctx.enter_context(nc.semaphore("mod_in"))
        s_w = [ctx.enter_context(nc.semaphore(f"mod_w{n}")) for n in range(2)]
        s_x = ctx.enter_context(nc.semaphore("mod_x"))
        s_sc = ctx.enter_context(nc.semaphore("mod_silu"))
        s_mm = ctx.enter_context(nc.semaphore("mod_filled"))
        s_v = ctx.enter_context(nc.semaphore("mod_steps"))
        s_c = ctx.enter_context(nc.semaphore("mod_consts"))
        half_cols = MODS // 2 * P
        with nc.Block() as block:

            @block.sync
            def _(sp):
                sp.dma_start(cT[:, :, :], io["condT"].rearrange("(c p) b -> p c b", p=P)).then_inc(s_in, 16)
                sp.dma_start(bias[:, :], io["mod_b"]).then_inc(s_in, 16)
                sp.dma_start(nw[:, :], io["norm_w"]).then_inc(s_in, 16)
                sp.dma_start(nb[:, :], io["norm_b"]).then_inc(s_in, 16)
                wv = io["mod_w"].rearrange("(c p) n -> p c n", p=P)
                for n in range(2):
                    sp.dma_start(w[:, :, n * half_cols:(n + 1) * half_cols],
                                 wv[:, :, n * half_cols:(n + 1) * half_cols]).then_inc(s_w[n], 16)
                sp.dma_start(consts["x"][:, :, :, :].rearrange("p b t d -> p (b t) d"),
                             io["x"].rearrange("b (t p) d -> p (b t) d", p=P)).then_inc(s_x, 16)
                sp.wait_ge(s_x, 16)

            @block.gpsimd
            def _(pool):
                nc.gpsimd.memset(ident[:, :], 0.0).then_inc(s_c, 1)
                pool.wait_ge(s_c, 1)
                nc.gpsimd.affine_select(out=ident[:, :], in_=ident[:, :], compare_op=ALU.not_equal, fill=1.0,
                                        base=0, pattern=[[-1, P]], channel_multiplier=1).then_inc(s_c, 1)
                nc.gpsimd.memset(ones[:, :], 1.0).then_inc(s_c, 1)
                nc.gpsimd.memset(consts["half"][:, :], -0.5).then_inc(s_c, 1)

            @block.scalar
            def _(act):
                act.wait_ge(s_in, 64)
                nc.scalar.activation(scT[:, :, :], cT[:, :, :], ACT.Silu).then_inc(s_sc, 1)

            @block.tensor
            def _(pe):
                pe.wait_ge(s_in, 64)
                pe.wait_ge(s_sc, 1)
                for m in range(MODS):
                    if m % (MODS // 2) == 0:
                        pe.wait_ge(s_w[m // (MODS // 2)], 16)
                    c_in = cT if m < MOD1 else scT
                    for c in range(DC):
                        last = nc.tensor.matmul(acc[:, m, :], w[:, c, m * P:(m + 1) * P], c_in[:, c, :],
                                                start=(c == 0), stop=(c == DC - 1))
                last.then_inc(s_mm, 1)

            @block.vector
            def _(dve):
                dve.wait_ge(s_mm, 1)
                done = [0]

                def step(instruction):
                    instruction.then_inc(s_v, 1)
                    done[0] += 1

                step(nc.vector.tensor_tensor(mod[:, :, :].rearrange("p b m -> p m b"), acc[:, :, :],
                                             bias[:, :].unsqueeze(2).broadcast_to([P, MODS, B]), ALU.add))
                dve.wait_ge(s_v, done[0])
                scales = [MOD0, MOD0 + 2 * DC] + [m + k * DC for m in (MOD1, MOD2, MOD3) for k in (1, 4)]
                for col in scales:
                    step(nc.vector.tensor_scalar(mod[:, :, col:col + DC], mod[:, :, col:col + DC], 1.0, None, ALU.add))
                dve.wait_ge(s_v, done[0])
                for k in range(2):
                    for c in range(DC):
                        sh, sc = MOD3 + 3 * k * DC + c, MOD3 + (3 * k + 1) * DC + c
                        n = k * DC + c
                        step(nc.vector.scalar_tensor_tensor(mod[:, :, sh], mod[:, :, sc], nb[:, n:n + 1],
                                                            mod[:, :, sh], ALU.mult, ALU.add))
                        dve.wait_ge(s_v, done[0])
                        step(nc.vector.tensor_scalar(mod[:, :, sc], mod[:, :, sc], nw[:, n:n + 1], None, ALU.mult))
    nc.all_engine_barrier()


def narrow_attention_layer(nc, consts, io, tag, mod0, eps, masked):
    ident, ones, mod = consts["ident"], consts["ones"], consts["mod"]
    x = consts["x"]
    gated = masked
    k_max = STACK + (1 if masked else 0)
    k_all = k_max + 2
    if masked:
        scale1, shift1, gate1, scale2, shift2, gate2 = DC, 0, 2 * DC, 4 * DC, 3 * DC, 5 * DC
    else:
        scale1, shift1, gate1, scale2, shift2, gate2 = 0, DC, None, 2 * DC, 3 * DC, None
    n_mod = 6 * DC if gated else 4 * DC
    with ExitStack() as ctx:
        def sb(name, shape, dt):
            return ctx.enter_context(nc.sbuf_tensor(f"{tag}_{name}", shape, dt))

        wq, wk, wv = (sb(f"w{n}", [P, DC, D], FP32) for n in "qkv")
        wo = sb("wo", [P, NG, D], FP32)
        w1 = sb("w1", [P, DC, MLP], FP32)
        w2 = sb("w2", [P, MC, D], FP32)
        bqk = sb("bqk", [P, 2 * DC], FP32)
        bv, bo, b2 = (sb(n, [P, D], FP32) for n in ("bv", "bo", "b2"))
        b1 = sb("b1", [P, MC], FP32)
        cur = sb("cur", [P, n_mod], FP32)
        qk = sb("qk", [P, 2 * DC, T], FP32)
        parts = sb("parts", [P, 2 * DC, SPLIT, T], BF16)
        qs = sb("q_stack", [k_all, H, T], BF16)
        ks = sb("k_stack", [k_all, H, T], BF16)
        va = sb("v_and_ones", [P, TT, H, 2 * HD], FP32)
        mx = sb("row_max", [P, NG, TT, GH], FP32)
        mrow = sb("max_rows", [GH, 2, T], BF16)
        probs = sb("probs", [P, 2 * GH, T], FP32)
        oT = sb("oT", [P, NG, T], FP32)
        rec = sb("rec", [P, T], FP32)
        sel_sum = sb("sel_sum", [P, NG, H], FP32)
        sel_head = sb("sel_head", [P, NG, P], FP32)
        g = sb("g", [P, MC, T], FP32)
        tmp = sb("res_tmp", [P, 2, 2, D], FP32)
        pm = sb("q_valid", [P, T], FP32) if masked else None
        scratch = nc.dram_tensor(f"{tag}_parts_dram", (2, DC, P, SPLIT, T), BF16, kind="Internal").ap()
        bank = [ctx.enter_context(nc.psum_tensor(f"{tag}_bank{n}", [P, T], FP32)) for n in range(8)]
        S = Semaphores(consts["pool"], LN_SEMS + [
            "cur", "gate_diag", "gate_filled", "gate_rows", "qk_filled", "v_filled", "qk", "part1", "rest", "part2",
            "part3", "v", "parts_out0", "parts_out1", "parts_out2", "parts_out3", "stacks", "mask_in", "max_filled", "max_taken",
            "maxT_filled", "max_part1", "max_part2", "max_rows", "st_filled", "exp", "av", "oT", "sum_filled", "rec",
            "head_filled", "oT_norm", "y_filled", "res", "up_filled", "gelu", "down_filled"])
        s_w, s_i, s_p, s_a = consts["init_sems"]
        norm = Norm(sb, S, lambda b: x[:, bass.ds(b, 1), :, :].rearrange("p b t d -> p (b t) d"), cur, ident,
                    consts["half"], bank, eps)
        gates = Gates(sb, S, cur, ident, ones, bank[7], [gate1, gate2]) if gated else None

        with nc.Block() as block:

            @block.sync
            def _(sp):
                n = 0
                for to, of in ((wq, "wq"), (wk, "wk"), (wv, "wv"), (w1, "w1"), (w2, "w2")):
                    sp.dma_start(to[:, :, :], io[tag + of].rearrange("(c p) n -> p c n", p=P)).then_inc(s_w, 16)
                    n += 1
                for to, of in ((bv, "bv"), (bo, "bo"), (b2, "b2")):
                    sp.dma_start(to[:, :], io[tag + of].unsqueeze(0).broadcast_to([P, D])).then_inc(s_w, 16)
                    n += 1
                sp.dma_start(b1[:, :], io[tag + "b1"]).then_inc(s_w, 16)
                sp.dma_start(bqk[:, 0:DC], io[tag + "bq"]).then_inc(s_w, 16)
                sp.dma_start(bqk[:, DC:2 * DC], io[tag + "bk"]).then_inc(s_w, 16)
                sp.wait_ge(s_i, 1)
                wo_v = io[tag + "wo"].rearrange("(g j d) n -> j d g n", j=GH, d=HD)
                for j in range(GH):
                    sp.dma_start(wo[j * 2 * HD:j * 2 * HD + HD, :, :], wo_v[j]).then_inc(s_w, 16)
                sp.wait_ge(s_w, 16 * (n + 3 + GH))

            @block.vector
            def _(dve):
                nc.vector.memset(wo[:, :, :], 0.0).then_inc(s_i, 1)
                nc.vector.memset(rec[:, :], 0.0).then_inc(s_i, 1)
                nc.vector.memset(va[:, :, :, HD:2 * HD], 1.0).then_inc(s_i, 1)
                nc.vector.memset(ks[STACK:k_all, :, :], 1.0).then_inc(s_i, 1)

            @block.gpsimd
            def _(pool):
                nc.gpsimd.memset(sel_sum[:, :, :], 0.0).then_inc(s_p, 1)
                nc.gpsimd.memset(sel_head[:, :, :], 0.0).then_inc(s_p, 1)
                pool.wait_ge(s_p, 2)
                for gg in range(NG):
                    nc.gpsimd.affine_select(
                        out=sel_sum[:, gg, gg * GH:(gg + 1) * GH], in_=sel_sum[:, gg, gg * GH:(gg + 1) * GH],
                        compare_op=ALU.not_equal, fill=1.0, base=-HD, pattern=[[-2 * HD, GH]], channel_multiplier=1)
                    nc.gpsimd.affine_select(
                        out=sel_head[:, gg, :].rearrange("p (j r) -> p j r", j=GH),
                        in_=sel_head[:, gg, :].rearrange("p (j r) -> p j r", j=GH),
                        compare_op=ALU.not_equal, fill=1.0, base=-gg * GH, pattern=[[-1, GH], [0, 2 * HD]],
                        channel_multiplier=1)

        nc.all_engine_barrier(sems_to_clear=range(s_w.num, s_a.num + 1))

        with nc.Fori(0, B) as b:
            x_b = x[:, bass.ds(b, 1), :, :].rearrange("p b t d -> p (b t) d")
            with nc.Block() as block:

                @block.sync
                def _(sp):
                    if masked:
                        valid, valid16, bar16 = io["valid"], io["valid16"], io["bar16"]
                        sp.dma_start(pm[:, :], valid[bass.ds(b, 1), :].broadcast_to([P, T])).then_inc(S["mask_in"], 16)
                        row = lambda a: a[bass.ds(b, 1), :].unsqueeze(1).broadcast_to([1, H, T])
                        sp.dma_start(qs[STACK:STACK + 1, :, :], row(valid16)).then_inc(S["mask_in"], 16)
                        sp.dma_start(ks[STACK:STACK + 1, :, :], row(bar16)).then_inc(S["mask_in"], 16)
                    for m in range(2 * DC):
                        sp.wait_ge(S["part3"], m + 1)
                        sp.dma_start(scratch[m // DC, m % DC, :, :, :], parts[:, m, :, :])\
                            .then_inc(S[f"parts_out{m}"], 16)
                    for which, stack, part in ((0, qs, Q_PART), (1, ks, K_PART)):
                        for m in range(DC):
                            sp.wait_ge(S[f"parts_out{which * DC + m}"], 16)
                        for s, p_ in enumerate(part):
                            of = scratch[which, :, :, p_, :].rearrange("m (h d) t -> d (m h) t", d=HD)
                            sp.dma_start(stack[s * HD:(s + 1) * HD, :, :], of).then_inc(S["stacks"], 16)
                    for gg in range(NG):
                        sp.wait_ge(S["max_part2"], gg + 1)
                        for k in range(2):
                            sp.dma_start(qs[k_max + k:k_max + k + 1, gg * GH:(gg + 1) * GH, :],
                                         mrow[:, k, :]).then_inc(S["max_rows"], 16)
                        sp.wait_ge(S["max_rows"], 32 * (gg + 1))

                @block.gpsimd
                def _(pool):
                    norm.gpsimd(nc, pool, 0)
                    norm.gpsimd(nc, pool, 1)

                @block.vector
                def _(dve):
                    nc.vector.tensor_copy(cur[:, :], mod[:, bass.ds(b, 1), mod0:mod0 + n_mod]
                                          .rearrange("p b m -> p (b m)")).then_inc(S["cur"], 1)
                    norm.vector(nc, dve, b, 0)
                    if gated:
                        dve.wait_ge(S["cur"], 1)
                        gates.vector(nc, dve)
                    if masked:
                        dve.wait_ge(S["mask_in"], 48)
                    for m in range(2 * DC):
                        dve.wait_ge(S["qk_filled"], m + 1)
                        if masked and m < DC:
                            nc.vector.scalar_tensor_tensor(qk[:, m, :], bank[2 + m][:, :], bqk[:, m:m + 1], pm[:, :],
                                                           ALU.add, ALU.mult).then_inc(S["qk"], 1)
                        else:
                            nc.vector.tensor_scalar(qk[:, m, :], bank[2 + m][:, :], bqk[:, m:m + 1], None,
                                                    ALU.add).then_inc(S["qk"], 1)
                    for k in range(2):
                        dve.wait_ge(S["v_filled"], k + 1)
                        nc.vector.tensor_tensor(
                            va[:, 2 * k:2 * k + 2, :, 0:HD],
                            bank[6 + k][:, :].rearrange("p (t h d) -> p t h d", t=2, h=H),
                            bv[:, :].rearrange("p (h d) -> p h d", h=H).unsqueeze(1).broadcast_to([P, 2, H, HD]),
                            ALU.add).then_inc(S["v"], 1)
                    for m in range(2 * DC):
                        dve.wait_ge(S["part1"], m + 1)
                        nc.vector.tensor_tensor(qk[:, m, :], qk[:, m, :], parts[:, m, 0, :],
                                                ALU.subtract).then_inc(S["rest"], 1)
                    for m in range(2 * DC):
                        dve.wait_ge(S["part2"], m + 1)
                        nc.vector.tensor_tensor(parts[:, m, 2, :], qk[:, m, :], parts[:, m, 1, :],
                                                ALU.subtract).then_inc(S["part3"], 1)

                    def take_max(gg, j):
                        for t in range(TT):
                            n = (gg * GH + j) * TT + t
                            dve.wait_ge(S["max_filled"], n + 1)
                            nc.vector.tensor_reduce(mx[:, gg, t, j:j + 1], bank[n % 2][:, :], AX.X, ALU.max)\
                                .then_inc(S["max_taken"], 1)

                    def max_rows(gg):
                        dve.wait_ge(S["maxT_filled"], gg + 1)
                        if gg:
                            dve.wait_ge(S["max_rows"], 32 * gg)
                        nc.vector.tensor_scalar(mrow[:, 0, :], bank[6][0:GH, :], -1.0, None,
                                                ALU.mult).then_inc(S["max_part1"], 1)
                        dve.wait_ge(S["max_part1"], gg + 1)
                        nc.vector.scalar_tensor_tensor(mrow[:, 1, :], bank[6][0:GH, :], -1.0, mrow[:, 0, :],
                                                       ALU.mult, ALU.subtract).then_inc(S["max_part2"], 1)

                    for j in range(GH):
                        take_max(0, j)
                    max_rows(0)
                    for gg in range(NG):
                        for k in range(TT):
                            if gg + 1 < NG:
                                take_max(gg + 1, k)
                        if gg + 1 < NG:
                            max_rows(gg + 1)
                        dve.wait_ge(S["av"], TT * (gg + 1))
                        nc.vector.tensor_copy(oT[:, gg, :], bank[4 + gg % 2][:, :]).then_inc(S["oT"], 1)
                    dve.wait_ge(S["sum_filled"], 1)
                    nc.vector.reciprocal(rec[0:H, :], bank[6][0:H, :]).then_inc(S["rec"], 1)
                    for gg in range(NG):
                        dve.wait_ge(S["head_filled"], gg + 1)
                        nc.vector.tensor_tensor(oT[:, gg, :], oT[:, gg, :], bank[gg][:, :],
                                                ALU.mult).then_inc(S["oT_norm"], 1)
                    if gated:
                        dve.wait_ge(S["gate_rows"], 1)
                    residual(nc, dve, S, bank[4:6], bo[:, :], gates.rows[:, 0, :] if gated else None, tmp, x_b, 0,
                             "y_filled")
                    norm.vector(nc, dve, b, 1)
                    residual(nc, dve, S, bank[6:8], b2[:, :], gates.rows[:, 1, :] if gated else None, tmp, x_b, 1,
                             "down_filled")

                @block.scalar
                def _(act):
                    act.wait_ge(S["cur"], 1)
                    norm.scalar(nc, act, 0, scale1, shift1)
                    if gated:
                        gates.scalar(nc, act)
                    for m in range(2 * DC):
                        act.wait_ge(S["qk"], m + 1)
                        nc.scalar.activation(parts[:, m, 0, :], qk[:, m, :], ACT.Copy).then_inc(S["part1"], 1)
                    for m in range(2 * DC):
                        act.wait_ge(S["rest"], m + 1)
                        nc.scalar.activation(parts[:, m, 1, :], qk[:, m, :], ACT.Copy).then_inc(S["part2"], 1)
                    for gg in range(NG):
                        for k in range(TT):
                            for j in range(GH):
                                n = (gg * TT + k) * GH + j
                                act.wait_ge(S["st_filled"], n + 1)
                                if n >= 2 * GH:
                                    act.wait_ge(S["av"], n // GH - 1)
                                nc.scalar.activation(probs[:, n % (2 * GH), :], bank[2 + n % 2][:, :], ACT.Exp,
                                                     scale=float(HD) ** -0.5).then_inc(S["exp"], 1)
                    norm.scalar(nc, act, 1, scale2, shift2)
                    mlp_scalar(nc, act, S, bank, b1, g, ACT.Gelu_apprx_tanh if masked else ACT.Gelu)

                @block.tensor
                def _(pe):
                    norm.tensor(nc, pe, 0)
                    if gated:
                        gates.tensor(nc, pe)
                    pe.wait_ge(S["hT"], DC)
                    for m in range(2 * DC):
                        w = (wq, wk)[m // DC]
                        for c in range(DC):
                            last = nc.tensor.matmul(bank[2 + m][:, :], w[:, c, (m % DC) * P:(m % DC + 1) * P],
                                                    norm.hT[:, c, :], start=(c == 0), stop=(c == DC - 1))
                        last.then_inc(S["qk_filled"], 1)
                    if gated:
                        pe.wait_ge(S["gate_rows"], 1)
                    for t in range(TT):
                        for c in range(DC):
                            last = nc.tensor.matmul(bank[6 + t // 2][:, (t % 2) * D:(t % 2 + 1) * D],
                                                    norm.hT[:, c, t * P:(t + 1) * P], wv[:, c, :],
                                                    start=(c == 0), stop=(c == DC - 1))
                        if t % 2:
                            last.then_inc(S["v_filled"], 1)

                    def scores(gg, j):
                        h = gg * GH + j
                        for t in range(TT):
                            n = h * TT + t
                            if n >= 2:
                                pe.wait_ge(S["max_taken"], n - 1)
                            nc.tensor.matmul(bank[n % 2][:, :], qs[0:k_max, h, t * P:(t + 1) * P], ks[0:k_max, h, :],
                                             start=True, stop=True).then_inc(S["max_filled"], 1)

                    def max_rows(gg):
                        pe.wait_ge(S["max_taken"], TT * GH * (gg + 1))
                        if gg:
                            pe.wait_ge(S["max_part2"], gg)
                        for t in range(TT):
                            last = nc.tensor.transpose(bank[6][0:GH, t * P:(t + 1) * P], mx[:, gg, t, :], ident[:, :])
                        last.then_inc(S["maxT_filled"], 1)

                    def scores_T(gg, k):
                        for j in range(GH):
                            h, n = gg * GH + j, (gg * TT + k) * GH + j
                            if n >= 2:
                                pe.wait_ge(S["exp"], n - 1)
                            nc.tensor.matmul(bank[2 + n % 2][:, :], ks[0:k_all, h, k * P:(k + 1) * P],
                                             qs[0:k_all, h, :], start=True, stop=True).then_inc(S["st_filled"], 1)

                    def values(gg, k):
                        if k == 0 and gg >= 2:
                            pe.wait_ge(S["oT"], gg - 1)
                        pe.wait_ge(S["exp"], GH * (gg * TT + k + 1))
                        for j in range(GH):
                            n = (gg * TT + k) * GH + j
                            last = nc.tensor.matmul(bank[4 + gg % 2][2 * HD * j:2 * HD * (j + 1), :],
                                                    va[:, k, gg * GH + j, :], probs[:, n % (2 * GH), :],
                                                    start=(k == 0), stop=(k == TT - 1))
                        last.then_inc(S["av"], 1)

                    pe.wait_ge(S["stacks"], 16 * 2 * len(Q_PART))
                    pe.wait_ge(S["v"], 2)
                    if masked:
                        pe.wait_ge(S["mask_in"], 48)
                    for j in range(GH):
                        scores(0, j)
                    max_rows(0)
                    for gg in range(NG):
                        pe.wait_ge(S["max_rows"], 32 * (gg + 1))
                        for k in range(TT):
                            if gg + 1 < NG:
                                scores(gg + 1, k)
                            scores_T(gg, k)
                            if k:
                                values(gg, k - 1)
                        if gg + 1 < NG:
                            max_rows(gg + 1)
                        values(gg, TT - 1)
                    pe.wait_ge(S["oT"], NG)
                    pe.wait_ge(S["max_part2"], NG)
                    for gg in range(NG):
                        last = nc.tensor.matmul(bank[6][0:H, :], sel_sum[:, gg, :], oT[:, gg, :],
                                                start=(gg == 0), stop=(gg == NG - 1))
                    last.then_inc(S["sum_filled"], 1)
                    pe.wait_ge(S["rec"], 1)
                    for gg in range(NG):
                        nc.tensor.matmul(bank[gg][:, :], sel_head[:, gg, :], rec[:, :], start=True, stop=True)\
                            .then_inc(S["head_filled"], 1)
                    pe.wait_ge(S["oT_norm"], NG)
                    for t in range(TT):
                        for gg in range(NG):
                            last = nc.tensor.matmul(bank[4 + t // 2][:, (t % 2) * D:(t % 2 + 1) * D],
                                                    oT[:, gg, t * P:(t + 1) * P], wo[:, gg, :],
                                                    start=(gg == 0), stop=(gg == NG - 1))
                        if t % 2:
                            last.then_inc(S["y_filled"], 1)
                    norm.tensor(nc, pe, 1)
                    mlp_tensor(nc, pe, S, bank, norm.hT, w1, w2, g, 2 * DC)

            nc.all_engine_barrier(sems_to_clear=S.range)


def wide_attention_layer(nc, consts, io, tag, mod0, eps):
    ident, ones, mod, x = consts["ident"], consts["ones"], consts["mod"], consts["x"]
    shift1, scale1, gate1, shift2, scale2, gate2 = (k * DC for k in range(6))
    n_mod = 6 * DC
    PG = GH // 2
    GW = GH * HD1
    with ExitStack() as ctx:
        def sb(name, shape, dt):
            return ctx.enter_context(nc.sbuf_tensor(f"{tag}_{name}", shape, dt))

        wq, wk, wv = (sb(f"w{n}", [P, DC, INNER1], FP32) for n in "qkv")
        wo = sb("wo", [P, INNER1 // P, D], FP32)
        w1 = sb("w1", [P, DC, MLP], FP32)
        w2 = sb("w2", [P, MC, D], FP32)
        bo, b2 = (sb(n, [P, D], FP32) for n in ("bo", "b2"))
        b1 = sb("b1", [P, MC], FP32)
        cur = sb("cur", [P, n_mod], FP32)
        qz = sb("q_heads", [P, 2, GH, T], FP32)
        kz = sb("k_heads", [P, 2, GH, T], FP32)
        v = sb("v", [P, 2, TT, GW], FP32)
        mx = sb("row_max", [P, NG, TT, GH], FP32)
        mrow = sb("max_rows", [GH, T], FP32)
        probs = sb("probs", [P, 2 * GH, T], FP32)
        oT = sb("oT", [P, INNER1 // P, T], FP32)
        rec = sb("rec", [P, T], FP32)
        sel = sb("sel_pair", [P, PG, P], FP32)
        g = sb("g", [P, MC, T], FP32)
        tmp = sb("res_tmp", [P, 2, 2, D], FP32)
        bank = [ctx.enter_context(nc.psum_tensor(f"{tag}_bank{n}", [P, T], FP32)) for n in range(8)]
        S = Semaphores(consts["pool"], LN_SEMS + [
            "cur", "gate_diag", "gate_filled", "gate_rows", "proj_filled", "proj", "no_max", "max_filled", "max_taken",
            "maxT_filled", "max_neg", "max_rows", "st_filled", "exp", "av", "oT", "rec", "head_filled", "oT_norm",
            "y_filled", "res", "up_filled", "gelu", "down_filled"])
        s_w, s_i, s_p, s_a = consts["init_sems"]
        norm = Norm(sb, S, lambda b: x[:, bass.ds(b, 1), :, :].rearrange("p b t d -> p (b t) d"), cur, ident,
                    consts["half"], bank, eps)
        gates = Gates(sb, S, cur, ident, ones, bank[7], [gate1, gate2])
        own = lambda j: slice(HD1 * (j % 2), HD1 * (j % 2) + HD1)
        aux = lambda j: HD1 * (1 - j % 2)

        with nc.Block() as block:

            @block.sync
            def _(sp):
                n = 0
                for to, of in ((wq, "wq"), (wk, "wk"), (wv, "wv"), (wo, "wo"), (w1, "w1"), (w2, "w2")):
                    sp.dma_start(to[:, :, :], io[tag + of].rearrange("(c p) n -> p c n", p=P)).then_inc(s_w, 16)
                    n += 1
                for to, of in ((bo, "bo"), (b2, "b2")):
                    sp.dma_start(to[:, :], io[tag + of].unsqueeze(0).broadcast_to([P, D])).then_inc(s_w, 16)
                    n += 1
                sp.dma_start(b1[:, :], io[tag + "b1"]).then_inc(s_w, 16)
                sp.wait_ge(s_w, 16 * (n + 1))

            @block.vector
            def _(dve):
                nc.vector.memset(qz[:, :, :, :], 0.0).then_inc(s_i, 1)
                nc.vector.memset(kz[:, :, :, :], 0.0).then_inc(s_i, 1)
                dve.wait_ge(s_i, 2)
                for j in range(GH):
                    nc.vector.memset(kz[aux(j):aux(j) + 1, :, j, :], 1.0).then_inc(s_i, 1)

            @block.gpsimd
            def _(pool):
                nc.gpsimd.memset(sel[:, :, :], 0.0).then_inc(s_p, 1)
                pool.wait_ge(s_p, 1)
                view = sel[:, :, :].rearrange("p q (a r) -> p q a r", a=2)
                nc.gpsimd.affine_select(out=view, in_=view, compare_op=ALU.not_equal, fill=1.0, base=0,
                                        pattern=[[-HD1, PG], [-HD1 // 2, 2], [0, HD1]], channel_multiplier=1)

        nc.all_engine_barrier(sems_to_clear=range(s_w.num, s_a.num + 1))

        with nc.Fori(0, B) as b:
            x_b = x[:, bass.ds(b, 1), :, :].rearrange("p b t d -> p (b t) d")
            PROJ = 2 * PG + 2
            PRING = (7, 0, 1)
            with nc.Block() as block:

                @block.sync
                def _(sp):
                    for gg in range(NG):
                        sp.wait_ge(S["max_neg"], gg + 1)
                        for j in range(GH):
                            sp.dma_start(qz[aux(j):aux(j) + 1, gg % 2, j, :], mrow[j:j + 1, :])\
                                .then_inc(S["max_rows"], 16)
                        sp.wait_ge(S["max_rows"], 16 * GH * (gg + 1))

                @block.gpsimd
                def _(pool):
                    norm.gpsimd(nc, pool, 0)
                    pool.wait_ge(S["rstd"], 1)
                    for gg in range(NG):
                        if gg >= 2:
                            pool.wait_ge(S["st_filled"], GH * TT * (gg - 1))
                        for j in range(GH):
                            if gg or j:
                                pool.wait_ge(S["no_max"], gg * GH + j)
                            nc.gpsimd.memset(qz[aux(j):aux(j) + 1, gg % 2, j, :], 0.0).then_inc(S["no_max"], 1)
                    norm.gpsimd(nc, pool, 1)

                @block.vector
                def _(dve):
                    nc.vector.tensor_copy(cur[:, :], mod[:, bass.ds(b, 1), mod0:mod0 + n_mod]
                                          .rearrange("p b m -> p (b m)")).then_inc(S["cur"], 1)
                    norm.vector(nc, dve, b, 0)
                    dve.wait_ge(S["cur"], 1)
                    gates.vector(nc, dve)

                    def take_max(gg, j):
                        for t in range(TT):
                            n = (gg * GH + j) * TT + t
                            dve.wait_ge(S["max_filled"], n + 1)
                            nc.vector.tensor_reduce(mx[:, gg, t, j:j + 1], bank[n % 2][:, :], AX.X, ALU.max)\
                                .then_inc(S["max_taken"], 1)

                    def max_rows(gg):
                        dve.wait_ge(S["maxT_filled"], gg + 1)
                        if gg:
                            dve.wait_ge(S["max_rows"], 16 * GH * gg)
                        nc.vector.tensor_scalar(mrow[:, :], bank[7][0:GH, :], -1.0, None,
                                                ALU.mult).then_inc(S["max_neg"], 1)

                    def normalise(gg, p):
                        dve.wait_ge(S["head_filled"], PG * gg + p + 1)
                        dve.wait_ge(S["oT"], PG * gg + p + 1)
                        nc.vector.tensor_tensor(oT[:, PG * gg + p, :], oT[:, PG * gg + p, :], bank[7][:, :],
                                                ALU.mult).then_inc(S["oT_norm"], 1)

                    for j in range(GH):
                        take_max(0, j)
                    max_rows(0)
                    for gg in range(NG):
                        for k in range(TT):
                            if gg + 1 < NG:
                                take_max(gg + 1, k)
                            if gg and 1 <= k <= PG:
                                normalise(gg - 1, k - 1)
                        if gg + 1 < NG:
                            max_rows(gg + 1)
                        dve.wait_ge(S["av"], TT * (gg + 1))
                        nc.vector.reciprocal(rec[:, :], bank[6][:, :]).then_inc(S["rec"], 1)
                    for p in range(PG):
                        normalise(NG - 1, p)
                    dve.wait_ge(S["gate_rows"], 1)
                    residual(nc, dve, S, bank[4:6], bo[:, :], gates.rows[:, 0, :], tmp, x_b, 0, "y_filled")
                    norm.vector(nc, dve, b, 1)
                    residual(nc, dve, S, bank[6:8], b2[:, :], gates.rows[:, 1, :], tmp, x_b, 1, "down_filled")

                @block.scalar
                def _(act):
                    act.wait_ge(S["cur"], 1)
                    norm.scalar(nc, act, 0, scale1, shift1)
                    gates.scalar(nc, act)

                    def projected(gg):
                        for m in range(PROJ):
                            n = gg * PROJ + m
                            act.wait_ge(S["proj_filled"], n + 1)
                            src = bank[PRING[m % 3]]
                            if m < 2 * PG:
                                to, pair = (qz, kz)[m // PG], m % PG
                                for j in (2 * pair, 2 * pair + 1):
                                    nc.scalar.activation(to[own(j), gg % 2, j, :], src[own(j), :],
                                                         ACT.Copy).then_inc(S["proj"], 1)
                            else:
                                t = 2 * (m - 2 * PG)
                                nc.scalar.activation(v[:, gg % 2, t:t + 2, :].rearrange("p t n -> p (t n)"), src[:, :],
                                                     ACT.Copy).then_inc(S["proj"], 2)

                    projected(0)
                    for gg in range(NG):
                        for k in range(TT):
                            if gg + 1 < NG and k == 0:
                                projected(gg + 1)
                            for j in range(GH):
                                n = (gg * TT + k) * GH + j
                                act.wait_ge(S["st_filled"], n + 1)
                                if n >= 2 * GH:
                                    act.wait_ge(S["av"], n // GH - 1)
                                nc.scalar.activation(probs[:, n % (2 * GH), :], bank[2 + n % 2][:, :], ACT.Exp,
                                                     scale=float(HD1) ** -0.5).then_inc(S["exp"], 1)
                        act.wait_ge(S["av"], TT * (gg + 1))
                        for p in range(PG):
                            nc.scalar.activation(oT[:, PG * gg + p, :], bank[4 + p][:, :],
                                                 ACT.Copy).then_inc(S["oT"], 1)
                    norm.scalar(nc, act, 1, scale2, shift2)
                    mlp_scalar(nc, act, S, bank, b1, g, ACT.Gelu)

                @block.tensor
                def _(pe):
                    norm.tensor(nc, pe, 0)
                    gates.tensor(nc, pe)
                    pe.wait_ge(S["hT"], DC)
                    pe.wait_ge(S["gate_rows"], 1)

                    def project(gg):
                        for m in range(PROJ):
                            if m == 0 and gg:
                                pe.wait_ge(S["max_neg"], gg)
                            if m == 0 and gg >= 3:
                                pe.wait_ge(S["oT_norm"], PG * (gg - 2))
                            if m == 1 and gg:
                                pe.wait_ge(S["max_taken"], TT * GH * gg)
                            if m >= 3:
                                pe.wait_ge(S["proj"], 2 * (gg * PROJ + m - 2))
                            to = bank[PRING[m % 3]]
                            if m < 2 * PG:
                                w, cols = (wq, wk)[m // PG], gg * GW + (m % PG) * P
                                for c in range(DC):
                                    last = nc.tensor.matmul(to[:, :], w[:, c, cols:cols + P], norm.hT[:, c, :],
                                                            start=(c == 0), stop=(c == DC - 1))
                            else:
                                for u in range(2):
                                    t = 2 * (m - 2 * PG) + u
                                    for c in range(DC):
                                        last = nc.tensor.matmul(to[:, u * GW:(u + 1) * GW],
                                                                norm.hT[:, c, t * P:(t + 1) * P],
                                                                wv[:, c, gg * GW:(gg + 1) * GW],
                                                                start=(c == 0), stop=(c == DC - 1))
                            last.then_inc(S["proj_filled"], 1)

                    def scores(gg, j):
                        if j == 0:
                            pe.wait_ge(S["proj"], 2 * PROJ * (gg + 1))
                            pe.wait_ge(S["no_max"], GH * (gg + 1))
                        for t in range(TT):
                            n = (gg * GH + j) * TT + t
                            if n >= 2:
                                pe.wait_ge(S["max_taken"], n - 1)
                            nc.tensor.matmul(bank[n % 2][:, :], qz[:, gg % 2, j, t * P:(t + 1) * P],
                                             kz[:, gg % 2, j, :], start=True, stop=True).then_inc(S["max_filled"], 1)

                    def max_rows(gg):
                        pe.wait_ge(S["max_taken"], TT * GH * (gg + 1))
                        if gg >= 2:
                            pe.wait_ge(S["oT_norm"], PG * (gg - 1))
                        for t in range(TT):
                            last = nc.tensor.transpose(bank[7][0:GH, t * P:(t + 1) * P], mx[:, gg, t, :], ident[:, :])
                        last.then_inc(S["maxT_filled"], 1)

                    def scores_T(gg, k):
                        for j in range(GH):
                            n = (gg * TT + k) * GH + j
                            if n >= 2:
                                pe.wait_ge(S["exp"], n - 1)
                            nc.tensor.matmul(bank[2 + n % 2][:, :], kz[:, gg % 2, j, k * P:(k + 1) * P],
                                             qz[:, gg % 2, j, :], start=True, stop=True).then_inc(S["st_filled"], 1)

                    def values(gg, k):
                        if k == 0 and gg:
                            pe.wait_ge(S["oT"], PG * gg)
                            pe.wait_ge(S["rec"], gg)
                        pe.wait_ge(S["exp"], GH * (gg * TT + k + 1))
                        slot = lambda j: ((gg * TT + k) * GH + j) % (2 * GH)
                        for j in range(GH):
                            nc.tensor.matmul(bank[4 + j // 2][own(j), :], v[:, gg % 2, k, j * HD1:(j + 1) * HD1],
                                             probs[:, slot(j), :], start=(k == 0), stop=(k == TT - 1))
                        for j in range(GH):
                            last = nc.tensor.matmul(bank[6][32 * j:32 * (j + 1), :], ones[:, 0:32],
                                                    probs[:, slot(j), :], start=(k == 0), stop=(k == TT - 1))
                        last.then_inc(S["av"], 1)

                    def spread(gg, p):
                        pe.wait_ge(S["rec"], gg + 1)
                        if p:
                            pe.wait_ge(S["oT_norm"], PG * gg + p)
                        nc.tensor.matmul(bank[7][:, :], sel[:, p, :], rec[:, :], start=True, stop=True)\
                            .then_inc(S["head_filled"], 1)

                    project(0)
                    for j in range(GH):
                        scores(0, j)
                    max_rows(0)
                    for gg in range(NG):
                        for k in range(TT):
                            if gg + 1 < NG and k == 0:
                                project(gg + 1)
                            if gg + 1 < NG:
                                scores(gg + 1, k)
                            if k == 0:
                                pe.wait_ge(S["max_rows"], 16 * GH * (gg + 1))
                            scores_T(gg, k)
                            if gg and 1 <= k <= PG:
                                spread(gg - 1, k - 1)
                            if k:
                                values(gg, k - 1)
                        if gg + 1 < NG:
                            max_rows(gg + 1)
                        values(gg, TT - 1)
                    for p in range(PG):
                        spread(NG - 1, p)
                    pe.wait_ge(S["oT"], PG * NG)
                    pe.wait_ge(S["oT_norm"], PG * NG)
                    for t in range(TT):
                        for c in range(INNER1 // P):
                            last = nc.tensor.matmul(bank[4 + t // 2][:, (t % 2) * D:(t % 2 + 1) * D],
                                                    oT[:, c, t * P:(t + 1) * P], wo[:, c, :],
                                                    start=(c == 0), stop=(c == INNER1 // P - 1))
                        if t % 2:
                            last.then_inc(S["y_filled"], 1)
                    norm.tensor(nc, pe, 1)
                    mlp_tensor(nc, pe, S, bank, norm.hT, w1, w2, g, 2 * DC)

            nc.all_engine_barrier(sems_to_clear=S.range)


def mask_rows(nc, io):
    with ExitStack() as ctx:
        sb = lambda n, s, d: ctx.enter_context(nc.sbuf_tensor(n, s, d))
        m8, v32 = sb("mask_u8", [B, T], U8), sb("mask_f32", [B, T], FP32)
        v16, bar = sb("mask_bf16", [B, T], BF16), sb("mask_bar", [B, T], BF16)
        s_in = ctx.enter_context(nc.semaphore("mask_in"))
        s_v = ctx.enter_context(nc.semaphore("mask_steps"))
        s_out = ctx.enter_context(nc.semaphore("mask_out"))
        with nc.Block() as block:

            @block.sync
            def _(sp):
                sp.dma_start(m8[:, :], io["mask"]).then_inc(s_in, 16)
                sp.wait_ge(s_v, 3)
                sp.dma_start(io["valid"], v32[:, :]).then_inc(s_out, 16)
                sp.dma_start(io["valid16"], v16[:, :]).then_inc(s_out, 16)
                sp.dma_start(io["bar16"], bar[:, :]).then_inc(s_out, 16)
                sp.wait_ge(s_out, 48)

            @block.vector
            def _(dve):
                dve.wait_ge(s_in, 16)
                nc.vector.tensor_copy(v32[:, :], m8[:, :]).then_inc(s_v, 1)
                nc.vector.tensor_copy(v16[:, :], m8[:, :]).then_inc(s_v, 1)
                nc.vector.tensor_scalar(bar[:, :], m8[:, :], 1.0, 1e9, ALU.subtract, ALU.mult).then_inc(s_v, 1)
    nc.all_engine_barrier()


def mamba_layer(nc, consts, io, tag, mod0, eps):
    ident, ones, mod, x = consts["ident"], consts["ones"], consts["mod"], consts["x"]
    shift1, scale1, gate1, shift2, scale2, gate2 = (k * DC for k in range(6))
    n_mod = 6 * DC
    PAD = TAPS - 1
    UNITS = IC * UB * NB
    SLOTS = 2 * NB
    with ExitStack() as ctx:
        def sb(name, shape, dt, where=ctx):
            return where.enter_context(nc.sbuf_tensor(f"{tag}_{name}", shape, dt))

        win = sb("win", [P, DC, 2 * DI], FP32)
        x_dt = sb("xproj_dt", [P, IC, P], FP32)
        x_b4 = sb("xproj_b", [P, IC, DPU, NS], FP32)
        x_c4 = sb("xproj_c", [P, IC, DPU, NS], FP32)
        dtw = sb("dtw", [P, DI], FP32)
        wout = sb("wout", [P, IC, D], FP32)
        w1, w2 = sb("w1", [P, DC, HID], FP32), sb("w2", [P, DC, HID], FP32)
        w3 = sb("w3", [P, HC, D], FP32)
        cw = sb("conv_w", [P, IC, TAPS], FP32)
        cb, dtb, dp = (sb(n, [P, IC], FP32) for n in ("conv_b", "dtb", "dp"))
        a_log = sb("a_log", [P, UNITS], FP32)
        a_neg = sb("a_neg", [P, UNITS], FP32)
        spread = sb("spread", [SPLIT * NS, UB, P], BF16)
        gather = sb("gather", [P, UB * NS], FP32)
        cur = sb("cur", [P, n_mod], FP32)
        sz = sb("silu_z", [P, IC, T], FP32)
        xs = sb("xs", [P, IC, 2, T], FP32)
        b_rep, c_rep = sb("b_rep", [P, 2, T], FP32), sb("c_rep", [P, 2, T], FP32)
        g = sb("g", [P, IC, T], FP32)
        tmp = sb("res_tmp", [P, 2, 2, D], FP32)
        S = Semaphores(consts["pool"], LN_SEMS + [
            "cur", "gate_diag", "gate_filled", "gate_rows", "pads", "in_filled", "in_taken", "tap0", "taps", "xs",
            "xp_filled", "xp", "dt_filled", "abs", "exp_abs", "ln", "relu", "dt", "dtx", "part1", "rest",
            "part2", "part3", "parts_out0", "parts_out1", "parts_out2", "parts_out3", "stacks", "e_filled", "x_filled",
            "decay", "bx", "scan", "hc", "y_sum", "combine", "y_filled", "res", "up1_filled", "up2_filled", "silu",
            "prod", "down_filled"])
        s_w, s_i, s_p, s_a = consts["init_sems"]
        psum = ctx.enter_context(nc.psum_tensor(f"{tag}_psum", [P, 8, T], FP32))
        bank = [psum[:, n, :] for n in range(8)]
        decay = lambda i: psum[:, 2 * (i % 2):2 * (i % 2) + 2, :]
        x_psum = psum[:, 4:6, :]
        y_psum = psum[:, 6:8, :]
        norm = Norm(sb, S, lambda b: x[:, bass.ds(b, 1), :, :].rearrange("p b t d -> p (b t) d"), cur, ident,
                    consts["half"], bank, eps)
        gates = Gates(sb, S, cur, ident, ones, bank[7], [gate1, gate2])
        scratch = nc.dram_tensor(f"{tag}_parts_dram", (IC, SPLIT, P, 2, 2, T), BF16, kind="Internal").ap()
        with ExitStack() as late:
            hid = sb("hid", [P, HC, T], FP32, late)
        with ExitStack() as early:
            xp = sb("x_padded", [P, IC, T + 2 * PAD], FP32, early)
            dtl = sb("dt_low", [P, 2, T], FP32, early)
            lg = sb("softplus", [P, IC, 2, T], FP32, early)
            dd = sb("dt_and_dtx", [P, 2, 2, 2, T], FP32, early)
            parts = sb("parts", [P, 2, SPLIT, 2, 2, T], BF16, early)
        stack = sb("stack", [SPLIT * NS, 2, NB, 2, 2, T], BF16)
        bx = sb("bx", [P, 2, 2, T], FP32)
        h = sb("h", [P, 2, 2, T], FP32)
        hc = sb("hc", [P, SLOTS, 2, T], FP32)

        with nc.Block() as block:

            @block.sync
            def _(sp):
                n = 0
                for to, of in ((win, "win"), (wout, "wout"), (w1, "w1"), (w2, "w2"), (w3, "w3")):
                    sp.dma_start(to[:, :, :], io[tag + of].rearrange("(c p) n -> p c n", p=P)).then_inc(s_w, 16)
                    n += 1
                xpv = io[tag + "xp"].rearrange("(c p) n -> p c n", p=P)
                for r in range(DPU):
                    sp.dma_start(x_b4[:, :, r, :], xpv[:, :, DTR:DTR + NS]).then_inc(s_w, 16)
                    sp.dma_start(x_c4[:, :, r, :], xpv[:, :, DTR + NS:DTR + 2 * NS]).then_inc(s_w, 16)
                    n += 2
                sp.dma_start(cw[:, :, :], io[tag + "conv_w"].rearrange("(c p) k -> p c k", p=P)).then_inc(s_w, 16)
                for to, of in ((cb, "conv_b"), (dtb, "dtb"), (dp, "dp")):
                    sp.dma_start(to[:, :], io[tag + of]).then_inc(s_w, 16)
                sp.wait_ge(s_i, 2)
                sp.dma_start(x_dt[:, :, 0:DTR], xpv[:, :, 0:DTR]).then_inc(s_w, 16)
                sp.dma_start(dtw[0:DTR, :], io[tag + "dtw"]).then_inc(s_w, 16)
                sp.wait_ge(s_w, 16 * (n + 6))

            @block.vector
            def _(dve):
                nc.vector.memset(x_dt[:, :, :], 0.0).then_inc(s_i, 1)
                nc.vector.memset(dtw[:, :], 0.0).then_inc(s_i, 1)
                nc.vector.memset(gather[:, :], 0.0).then_inc(s_i, 1)
                dve.wait_ge(s_i, 3)
                for a in range(DPU):
                    nc.vector.memset(gather[NS * a:NS * (a + 1), a::NS + DPU], 1.0).then_inc(s_i, 1)
                dve.wait_ge(s_a, 17)
                nc.vector.tensor_scalar(a_neg[:, :], a_neg[:, :], -1.0, None, ALU.mult).then_inc(s_i, 1)

            @block.scalar
            def _(act):
                act.dma_start(a_log[:, :], io[tag + "alog"]).then_inc(s_a, 16)
                act.wait_ge(s_a, 16)
                nc.scalar.activation(a_neg[:, :], a_log[:, :], ACT.Exp).then_inc(s_a, 1)

            @block.gpsimd
            def _(pool):
                nc.gpsimd.memset(spread[:, :, :], 0.0).then_inc(s_p, 1)
                view = spread[:, :, :].rearrange("p u (a n) -> p u a n", a=DPU)
                for j in range(SPLIT):
                    pool.wait_ge(s_p, j + 1)
                    nc.gpsimd.affine_select(out=view, in_=view, compare_op=ALU.not_equal, fill=1.0, base=-NS * j,
                                            pattern=[[-DPU, UB], [-1, DPU], [0, NS]],
                                            channel_multiplier=1).then_inc(s_p, 1)

        nc.all_engine_barrier(sems_to_clear=range(s_w.num, s_a.num + 1))

        with nc.Fori(0, B) as b:
            x_of_b = x[:, bass.ds(b, 1), :, :].rearrange("p b t d -> p (b t) d")
            with nc.Block() as block:

                @block.sync
                def _(sp):
                    for c in range(IC):
                        sp.wait_ge(S["part3"], c + 1)
                        sp.dma_start(scratch[c].rearrange("s p q w t -> p s (q w t)"),
                                     parts[:, c % 2, :, :, :, :].rearrange("p s q w t -> p s (q w t)"))\
                            .then_inc(S[f"parts_out{c}"], 16)
                    for c in range(IC):
                        sp.wait_ge(S[f"parts_out{c}"], 16)
                        if c == 0:
                            for k in range(1, IC):
                                sp.wait_ge(S[f"parts_out{k}"], 16)
                            sp.wait_ge(S["dtx"], IC)
                        if c >= 2:
                            sp.wait_ge(S["x_filled"], UB * NB * (c - 1))
                        for j in range(SPLIT):
                            sp.dma_start(stack[NS * j:NS * (j + 1), c % 2, :, :, :, :]
                                         .rearrange("d k q w t -> d k (q w t)"),
                                         scratch[c, j].rearrange("(k d) q w t -> d k (q w t)", d=NS))\
                                .then_inc(S["stacks"], 16)
                        sp.wait_ge(S["stacks"], 16 * SPLIT * (c + 1))

                @block.gpsimd
                def _(pool):
                    nc.gpsimd.memset(xp[:, :, 0:PAD], 0.0).then_inc(S["pads"], 1)
                    pool.wait_ge(S["pads"], 1)
                    nc.gpsimd.memset(xp[:, :, PAD + T:], 0.0).then_inc(S["pads"], 1)
                    pool.wait_ge(S["pads"], 2)
                    norm.gpsimd(nc, pool, 0)
                    for i in range(UNITS):
                        pool.wait_ge(S["scan"], 2 * (i + 1))
                        if i >= SLOTS:
                            pool.wait_ge(S["y_sum"], i // NB - 1)
                        nc.gpsimd.tensor_tensor(hc[:, i % SLOTS, :, :], h[:, i % 2, :, :], c_rep[:, :, :],
                                                ALU.mult).then_inc(S["hc"], 1)
                    norm.gpsimd(nc, pool, 1)

                @block.vector
                def _(dve):
                    nc.vector.tensor_copy(cur[:, :], mod[:, bass.ds(b, 1), mod0:mod0 + n_mod]
                                          .rearrange("p b m -> p (b m)")).then_inc(S["cur"], 1)
                    norm.vector(nc, dve, b, 0)
                    dve.wait_ge(S["cur"], 1)
                    gates.vector(nc, dve)
                    dve.wait_ge(S["pads"], 2)
                    for j in range(1, TAPS):
                        for c in range(IC):
                            for w in range(2):
                                n = 2 * c + w
                                if j == 1:
                                    dve.wait_ge(S["tap0"], n + 1)
                                else:
                                    dve.wait_ge(S["taps"], 2 * IC * (j - 2) + n + 1)
                                src = xp[:, c, j:j + T] if w == 0 else xp[:, c, T + 2 * PAD - 1 - j:2 * PAD - 1 - j:-1]
                                nc.vector.scalar_tensor_tensor(xs[:, c, w, :], src, cw[:, c, j:j + 1], xs[:, c, w, :],
                                                               ALU.mult, ALU.add).then_inc(S["taps"], 1)
                    for c in range(IC):
                        dve.wait_ge(S["abs"], c + 1)
                        if c >= 2:
                            dve.wait_ge(S["part3"], c - 1)
                        nc.vector.tensor_scalar(dd[:, c % 2, 0, :, :], psum[:, 2 * c:2 * c + 2, :], dtb[:, c:c + 1],
                                                0.0, ALU.add, ALU.max).then_inc(S["relu"], 1)
                        dve.wait_ge(S["ln"], c + 1)
                        dve.wait_ge(S["relu"], c + 1)
                        nc.vector.tensor_tensor(dd[:, c % 2, 0, :, :], dd[:, c % 2, 0, :, :], lg[:, c, :, :],
                                                ALU.add).then_inc(S["dt"], 1)
                        dve.wait_ge(S["dt"], c + 1)
                        nc.vector.tensor_tensor(dd[:, c % 2, 1, :, :], dd[:, c % 2, 0, :, :], xs[:, c, :, :],
                                                ALU.mult).then_inc(S["dtx"], 1)
                        dve.wait_ge(S["part1"], c + 1)
                        nc.vector.tensor_tensor(dd[:, c % 2, :, :, :], dd[:, c % 2, :, :, :],
                                                parts[:, c % 2, 0, :, :, :], ALU.subtract).then_inc(S["rest"], 1)
                        dve.wait_ge(S["part2"], c + 1)
                        nc.vector.tensor_tensor(parts[:, c % 2, 2, :, :, :], dd[:, c % 2, :, :, :],
                                                parts[:, c % 2, 1, :, :, :], ALU.subtract).then_inc(S["part3"], 1)
                    for k in range(IC):
                        dve.wait_ge(S[f"parts_out{k}"], 16)
                    dve.wait_ge(S["xp"], 6)

                    def scan_unit(i):
                        dve.wait_ge(S["decay"], i + 1)
                        dve.wait_ge(S["bx"], i + 1)
                        if i >= 2:
                            dve.wait_ge(S["hc"], i - 1)
                        for w in range(2):
                            nc.vector.tensor_tensor_scan(h[:, i % 2, w, :], decay(i)[:, w, :], bx[:, i % 2, w, :], 0.0,
                                                         ALU.mult, ALU.add).then_inc(S["scan"], 1)

                    def combine(c):
                        dve.wait_ge(S["y_sum"], UB * (c + 1))
                        y = g[:, c, :]
                        steps = (
                            lambda: nc.vector.scalar_tensor_tensor(y, xs[:, c, 0, :], dp[:, c:c + 1], y_psum[:, 0, :],
                                                                   ALU.mult, ALU.add),
                            lambda: nc.vector.scalar_tensor_tensor(y, xs[:, c, 1, ::-1], dp[:, c:c + 1], y,
                                                                   ALU.mult, ALU.add),
                            lambda: nc.vector.tensor_tensor(y, y_psum[:, 1, ::-1], y, ALU.add),
                            lambda: nc.vector.tensor_tensor(y, y, sz[:, c, :], ALU.mult))
                        for k, step in enumerate(steps):
                            if k:
                                dve.wait_ge(S["combine"], len(steps) * c + k)
                            step().then_inc(S["combine"], 1)

                    per_chunk = UB * NB
                    for i in range(UNITS + 1):
                        if i < UNITS:
                            dve.wait_ge(S["x_filled"], i + 1)
                            if i >= 2:
                                dve.wait_ge(S["scan"], 2 * (i - 1))
                            nc.vector.tensor_tensor(bx[:, i % 2, :, :], x_psum, b_rep[:, :, :],
                                                    ALU.mult).then_inc(S["bx"], 1)
                        if i:
                            scan_unit(i - 1)
                        if i > per_chunk and i % per_chunk == 5:
                            combine(i // per_chunk - 1)
                    combine(IC - 1)
                    dve.wait_ge(S["gate_rows"], 1)
                    residual(nc, dve, S, bank[0:2], None, gates.rows[:, 0, :], tmp, x_of_b, 0, "y_filled")
                    norm.vector(nc, dve, b, 1)
                    for j in range(HC):
                        dve.wait_ge(S["silu"], j + 1)
                        dve.wait_ge(S["up2_filled"], j + 1)
                        nc.vector.tensor_tensor(hid[:, j, :], hid[:, j, :], bank[5 + j], ALU.mult)\
                            .then_inc(S["prod"], 1)
                    residual(nc, dve, S, bank[0:2], None, gates.rows[:, 1, :], tmp, x_of_b, 1, "down_filled")

                @block.scalar
                def _(act):
                    act.wait_ge(S["cur"], 1)
                    norm.scalar(nc, act, 0, scale1, shift1)
                    gates.scalar(nc, act)
                    for m in range(2 * IC):
                        act.wait_ge(S["in_filled"], m + 1)
                        if m < IC:
                            nc.scalar.activation(xp[:, m, PAD:PAD + T], bank[2 + m % 4], ACT.Copy)\
                                .then_inc(S["in_taken"], 1)
                        else:
                            nc.scalar.activation(sz[:, m - IC, :], bank[2 + m % 4], ACT.Silu)\
                                .then_inc(S["in_taken"], 1)
                    act.wait_ge(S["pads"], 2)
                    act.wait_ge(S["in_taken"], IC)
                    for c in range(IC):
                        for w in range(2):
                            src = xp[:, c, 0:T] if w == 0 else xp[:, c, T + 2 * PAD - 1:2 * PAD - 1:-1]
                            nc.scalar.activation(xs[:, c, w, :], src, ACT.Identity, bias=cb[:, c:c + 1],
                                                 scale=cw[:, c, 0:1]).then_inc(S["tap0"], 1)
                    for c in range(IC):
                        for w in range(2):
                            act.wait_ge(S["taps"], 2 * IC * (TAPS - 2) + 2 * c + w + 1)
                            nc.scalar.activation(xs[:, c, w, :], xs[:, c, w, :], ACT.Silu).then_inc(S["xs"], 1)
                    for n, to in enumerate((dtl, dtl, b_rep, b_rep, c_rep, c_rep)):
                        act.wait_ge(S["xp_filled"], n + 1)
                        nc.scalar.activation(to[:, n % 2, :], bank[2 + n % 4], ACT.Copy).then_inc(S["xp"], 1)
                    for c in range(IC):
                        act.wait_ge(S["dt_filled"], c + 1)
                        nc.scalar.activation(lg[:, c, :, :], psum[:, 2 * c:2 * c + 2, :], ACT.Abs,
                                             bias=dtb[:, c:c + 1]).then_inc(S["abs"], 1)
                    for c in range(IC):
                        act.wait_ge(S["abs"], c + 1)
                        nc.scalar.activation(lg[:, c, :, :], lg[:, c, :, :], ACT.Exp, scale=-1.0)\
                            .then_inc(S["exp_abs"], 1)
                    for c in range(IC):
                        act.wait_ge(S["exp_abs"], c + 1)
                        nc.scalar.activation(lg[:, c, :, :], lg[:, c, :, :], ACT.Ln, bias=1.0).then_inc(S["ln"], 1)
                    for c in range(IC):
                        act.wait_ge(S["dtx"], c + 1)
                        if c >= 2:
                            act.wait_ge(S[f"parts_out{c - 2}"], 16)
                        nc.scalar.activation(parts[:, c % 2, 0, :, :, :], dd[:, c % 2, :, :, :], ACT.Copy)\
                            .then_inc(S["part1"], 1)
                        act.wait_ge(S["rest"], c + 1)
                        nc.scalar.activation(parts[:, c % 2, 1, :, :, :], dd[:, c % 2, :, :, :], ACT.Copy)\
                            .then_inc(S["part2"], 1)
                    for i in range(UNITS):
                        unit = (i // (UB * NB)) * UB * NB + (i % NB) * UB + (i // NB) % UB
                        act.wait_ge(S["e_filled"], i + 1)
                        nc.scalar.activation(decay(i), decay(i), ACT.Exp, scale=a_neg[:, unit:unit + 1])\
                            .then_inc(S["decay"], 1)
                    norm.scalar(nc, act, 1, scale2, shift2)
                    for j in range(HC):
                        act.wait_ge(S["up1_filled"], j + 1)
                        nc.scalar.activation(hid[:, j, :], bank[2 + j], ACT.Silu).then_inc(S["silu"], 1)

                @block.tensor
                def _(pe):
                    norm.tensor(nc, pe, 0)
                    gates.tensor(nc, pe)
                    pe.wait_ge(S["hT"], DC)
                    for m in range(2 * IC):
                        if m >= 4:
                            pe.wait_ge(S["in_taken"], m - 3)
                        for c in range(DC):
                            last = nc.tensor.matmul(bank[2 + m % 4], win[:, c, m * P:(m + 1) * P], norm.hT[:, c, :],
                                                    start=(c == 0), stop=(c == DC - 1))
                        last.then_inc(S["in_filled"], 1)
                    pe.wait_ge(S["in_taken"], 2 * IC)
                    pe.wait_ge(S["xs"], 2 * IC)
                    for n, w in enumerate((x_dt, x_dt, x_b4, x_b4, x_c4, x_c4)):
                        if n >= 4:
                            pe.wait_ge(S["xp"], n - 3)
                        for c in range(IC):
                            stat = w[:, c, :] if w is x_dt else w[:, c, :, :].rearrange("p a n -> p (a n)")
                            last = nc.tensor.matmul(bank[2 + n % 4], stat, xs[:, c, n % 2, :],
                                                    start=(c == 0), stop=(c == IC - 1))
                        last.then_inc(S["xp_filled"], 1)
                    pe.wait_ge(S["gate_rows"], 1)
                    pe.wait_ge(S["xp"], 6)
                    for c in range(IC):
                        for w in range(2):
                            last = nc.tensor.matmul(bank[2 * c + w], dtw[:, c * P:(c + 1) * P], dtl[:, w, :],
                                                    start=True, stop=True)
                        last.then_inc(S["dt_filled"], 1)
                    pe.wait_ge(S["relu"], IC)
                    pe.wait_ge(S["abs"], IC)

                    def y_sum(k):
                        c, u = k // UB, k % UB
                        if u == 0 and c:
                            pe.wait_ge(S["combine"], 4 * c)
                        pe.wait_ge(S["hc"], NB * (k + 1))
                        for w in range(2):
                            for j in range(NB):
                                last = nc.tensor.matmul(y_psum[NS * j:NS * (j + 1), w, :],
                                                        gather[:, NS * u:NS * (u + 1)],
                                                        hc[:, (NB * k + j) % SLOTS, w, :],
                                                        start=(u == 0), stop=(u == UB - 1))
                        last.then_inc(S["y_sum"], 1)

                    for i in range(UNITS):
                        c, u, j = i // (UB * NB), (i // NB) % UB, i % NB
                        if i % (UB * NB) == 0:
                            pe.wait_ge(S["stacks"], 16 * SPLIT * (c + 1))
                        if i >= 2:
                            pe.wait_ge(S["scan"], 2 * (i - 1))
                        for w in range(2):
                            last = nc.tensor.matmul(decay(i)[:, w, :], spread[:, u, :], stack[:, c % 2, j, 0, w, :],
                                                    start=True, stop=True)
                        last.then_inc(S["e_filled"], 1)
                        if i:
                            pe.wait_ge(S["bx"], i)
                        for w in range(2):
                            last = nc.tensor.matmul(x_psum[:, w, :], spread[:, u, :], stack[:, c % 2, j, 1, w, :],
                                                    start=True, stop=True)
                        last.then_inc(S["x_filled"], 1)
                        if i % NB == 3 and i > NB:
                            y_sum(i // NB - 1)
                    y_sum(UNITS // NB - 1)
                    pe.wait_ge(S["combine"], 4 * IC)
                    for t in range(TT):
                        for c in range(IC):
                            last = nc.tensor.matmul(bank[t // 2][:, (t % 2) * D:(t % 2 + 1) * D],
                                                    g[:, c, t * P:(t + 1) * P], wout[:, c, :],
                                                    start=(c == 0), stop=(c == IC - 1))
                        if t % 2:
                            last.then_inc(S["y_filled"], 1)
                    norm.tensor(nc, pe, 1)
                    pe.wait_ge(S["hT"], 2 * DC)
                    for base, w, filled in ((2, w1, "up1_filled"), (5, w2, "up2_filled")):
                        for j in range(HC):
                            for c in range(DC):
                                last = nc.tensor.matmul(bank[base + j], w[:, c, j * P:(j + 1) * P], norm.hT[:, c, :],
                                                        start=(c == 0), stop=(c == DC - 1))
                            last.then_inc(S[filled], 1)
                    pe.wait_ge(S["prod"], HC)
                    for t in range(TT):
                        for j in range(HC):
                            last = nc.tensor.matmul(bank[t // 2][:, (t % 2) * D:(t % 2 + 1) * D],
                                                    hid[:, j, t * P:(t + 1) * P], w3[:, j, :],
                                                    start=(j == 0), stop=(j == HC - 1))
                        if t % 2:
                            last.then_inc(S["down_filled"], 1)

            nc.all_engine_barrier(sems_to_clear=S.range)


_INPUTS = {
    "x": lambda a: a["x"],
    "condT": lambda a: a["cond_1024"].T,
    "mask": lambda a: a["mask_BxS_bk1"],
    "mod_w": lambda a: _join(1, a["L0_cond_Wln1"], a["L0_cond_Wln2"], a["L1_cond_W_mod"], a["L2_cond_ada_w"].T,
                             a["L3_cond_adaln1_W"], a["L3_cond_adaln2_W"]),
    "mod_b": lambda a: _columns(_join(0, a["L0_cond_bln1"], a["L0_cond_bln2"], a["L1_cond_b_mod"], a["L2_cond_ada_b"],
                                      a["L3_cond_adaln1_b"], a["L3_cond_adaln2_b"])),
    "norm_w": lambda a: _columns(_join(0, a["L3_cond_norm1_w"], a["L3_cond_norm2_w"])),
    "norm_b": lambda a: _columns(_join(0, a["L3_cond_norm1_b"], a["L3_cond_norm2_b"])),
    "l0_wq": lambda a: a["L0_cond_Wq"], "l0_wk": lambda a: a["L0_cond_Wk"], "l0_wv": lambda a: a["L0_cond_Wv"],
    "l0_wo": lambda a: a["L0_cond_Wo"], "l0_w1": lambda a: a["L0_cond_W1"], "l0_w2": lambda a: a["L0_cond_W2"],
    "l0_bq": lambda a: _columns(a["L0_cond_bq"]), "l0_bk": lambda a: _columns(a["L0_cond_bk"]), "l0_bv": lambda a: a["L0_cond_bv"],
    "l0_bo": lambda a: a["L0_cond_bo"], "l0_b1": lambda a: _columns(a["L0_cond_b1"]), "l0_b2": lambda a: a["L0_cond_b2"],
    "l1_wq": lambda a: a["L1_cond_W_qkv"][:, 0:INNER1], "l1_wk": lambda a: a["L1_cond_W_qkv"][:, INNER1:2 * INNER1],
    "l1_wv": lambda a: a["L1_cond_W_qkv"][:, 2 * INNER1:], "l1_wo": lambda a: a["L1_cond_W_out"],
    "l1_bo": lambda a: a["L1_cond_b_out"], "l1_w1": lambda a: a["L1_cond_W1"], "l1_b1": lambda a: _columns(a["L1_cond_b1"]),
    "l1_w2": lambda a: a["L1_cond_W2"], "l1_b2": lambda a: a["L1_cond_b2"],
    "l2_wq": lambda a: a["L2_cond_qkv_w"][0:D].T, "l2_wk": lambda a: a["L2_cond_qkv_w"][D:2 * D].T,
    "l2_wv": lambda a: a["L2_cond_qkv_w"][2 * D:].T, "l2_wo": lambda a: a["L2_cond_proj_w"].T,
    "l2_w1": lambda a: a["L2_cond_fc1_w"].T, "l2_w2": lambda a: a["L2_cond_fc2_w"].T,
    "l2_bq": lambda a: _columns(a["L2_cond_qkv_b"][0:D]), "l2_bk": lambda a: _columns(a["L2_cond_qkv_b"][D:2 * D]),
    "l2_bv": lambda a: a["L2_cond_qkv_b"][2 * D:], "l2_bo": lambda a: a["L2_cond_proj_b"],
    "l2_b1": lambda a: _columns(a["L2_cond_fc1_b"]), "l2_b2": lambda a: a["L2_cond_fc2_b"],
    "l3_win": lambda a: a["L3_cond_in_proj_W"], "l3_conv_w": lambda a: a["L3_cond_conv_w"].reshape(DI, TAPS),
    "l3_conv_b": lambda a: _columns(a["L3_cond_conv_b"]), "l3_xp": lambda a: a["L3_cond_x_proj_W"],
    "l3_dtw": lambda a: a["L3_cond_dt_proj_W"], "l3_dtb": lambda a: _columns(a["L3_cond_dt_proj_b"]),
    "l3_alog": lambda a: _columns(a["L3_cond_A_log"]), "l3_dp": lambda a: _columns(a["L3_cond_Dp"]),
    "l3_wout": lambda a: a["L3_cond_out_proj_W"], "l3_w1": lambda a: a["L3_cond_w1"],
    "l3_w2": lambda a: a["L3_cond_w2"], "l3_w3": lambda a: a["L3_cond_w3"],
}


def _columns(v):
    return v.reshape(-1, P).T


def _join(axis, *arrays):
    import numpy as np
    return np.concatenate(arrays, axis=axis)


LAYERS = 4
BODY_SEMS = 56


def program(nc, io, out):
    for name, dt in (("valid", FP32), ("valid16", BF16), ("bar16", BF16)):
        io[name] = nc.dram_tensor(f"{name}_dram", (B, T), dt, kind="Internal").ap()
    with ExitStack() as ctx:
        sb = lambda n, s, d: ctx.enter_context(nc.sbuf_tensor(n, s, d))
        consts = {"x": sb("x_sb", [P, B, TT, D], FP32), "ident": sb("ident", [P, P], FP32),
                  "ones": sb("ones", [P, P], FP32), "mod": sb("mod", [P, B, MODS], FP32),
                  "half": sb("minus_half", [P, TT], FP32)}
        consts["init_sems"] = [ctx.enter_context(nc.semaphore(n)) for n in ("weights", "init", "init_sel", "init_a")]
        consts["pool"] = [ctx.enter_context(nc.semaphore(f"body{n}")) for n in range(BODY_SEMS)]
        modulation(nc, consts, io)
        if LAYERS >= 1:
            narrow_attention_layer(nc, consts, io, "l0_", MOD0, 1e-5, masked=False)
        if LAYERS >= 2:
            wide_attention_layer(nc, consts, io, "l1_", MOD1, 1e-5)
        if LAYERS >= 3:
            mask_rows(nc, io)
            narrow_attention_layer(nc, consts, io, "l2_", MOD2, 1e-6, masked=True)
        if LAYERS >= 4:
            mamba_layer(nc, consts, io, "l3_", MOD3, 1e-5)
        store(nc, consts, out)


def store(nc, consts, out):
    s_out = nc.alloc_semaphore("out")
    with nc.Block() as block:

        @block.sync
        def _(sp):
            sp.dma_start(out.rearrange("b (t p) d -> p (b t) d", p=P),
                         consts["x"][:, :, :, :].rearrange("p b t d -> p (b t) d")).then_inc(s_out, 16)
            sp.wait_ge(s_out, 16)


def kernel(**inputs):
    import numpy as np
    import concourse.bacc as bacc
    from concourse.bass_utils import run_bass_kernel_spmd

    nc = bacc.Bacc("TRN2", target_bir_lowering=False, num_devices=1)
    given = {k: np.asarray(v) for k, v in inputs.items()}
    arrays, io = {}, {}
    for name, lay in _INPUTS.items():
        a = np.ascontiguousarray(lay(given))
        arrays[f"in_{name}"] = a
        io[name] = nc.dram_tensor(f"in_{name}", a.shape, mybir.dt.from_np(a.dtype), kind="ExternalInput").ap()
    out = nc.dram_tensor("out_x", (B, T, D), FP32, kind="ExternalOutput").ap()
    program(nc, io, out)
    r = run_bass_kernel_spmd(nc, [arrays], core_ids=[0])
    return r.results[0]["out_x"]
```

```python
import concourse.bass as bass
from concourse import mybir
from contextlib import ExitStack

FP32 = mybir.dt.float32
BF16 = mybir.dt.bfloat16
U8 = mybir.dt.uint8
ALU = mybir.AluOpType
ACT = mybir.ActivationFunctionType
AX = mybir.AxisListType

P = 128
B, T, D = 8, 512, 256
TT = T // P
DC = D // P
H = 16
GH = 4
NG = H // GH
MLP = 4 * D
MC = MLP // P
SPLIT = 3
Q_PART = (0, 0, 1, 1, 0, 2)
K_PART = (0, 1, 0, 1, 2, 0)
HD = 16
STACK = HD * len(Q_PART)
HD1 = 64
INNER1 = H * HD1
DI = 2 * D
IC = DI // P
NS = 32
DTR = D // 16
DPU = P // NS
UB = NS // DPU
NB = P // NS
TAPS = 4
HID = (int(2 / 3 * 2 * D) + 63) // 64 * 64
HC = HID // P

MOD0, MOD1, MOD2, MOD3 = 0, 4 * DC, 10 * DC, 16 * DC
MODS = 22 * DC


class Semaphores:

    def __init__(self, pool, names):
        assert len(set(names)) == len(names) <= len(pool)
        self.range = range(pool[0].num, pool[0].num + len(pool))
        assert [s.num for s in pool] == list(self.range)
        self.of = dict(zip(names, pool))

    def __getitem__(self, name):
        return self.of[name]


LN_SEMS = ["stats", "aggr", "var_eps", "rstd", "xn", "hT_filled", "hT"]


class Norm:

    def __init__(self, sb, S, x, cur, ident, half, banks, eps):
        self.S, self.x, self.cur, self.ident, self.half, self.banks, self.eps = S, x, cur, ident, half, banks, eps
        self.st = sb("ln_stats", [P, TT, 6], FP32)
        self.mv = sb("ln_mean_var", [P, TT, 2], FP32)
        self.ve = sb("ln_var_eps", [P, TT], FP32)
        self.rs = sb("ln_rstd", [P, TT], FP32)
        self.xn = sb("ln_xn", [P, TT, D], FP32)
        self.hT = sb("ln_hT", [P, DC, T], FP32)

    def vector(self, nc, dve, b, n):
        S = self.S
        for t in range(TT):
            nc.vector.bn_stats(self.st[:, t, :], self.x(b)[:, t, :]).then_inc(S["stats"], 1)
        dve.wait_ge(S["stats"], TT * (n + 1))
        for t in range(TT):
            nc.vector.bn_aggr(self.mv[:, t, :], self.st[:, t, :]).then_inc(S["aggr"], 1)
        dve.wait_ge(S["rstd"], n + 1)
        for t in range(TT):
            nc.vector.tensor_scalar(self.xn[:, t, :], self.x(b)[:, t, :], self.mv[:, t, 0:1], self.rs[:, t:t + 1],
                                    ALU.subtract, ALU.mult).then_inc(S["xn"], 1)

    def gpsimd(self, nc, pool, n):
        S = self.S
        pool.wait_ge(S["aggr"], TT * (n + 1))
        nc.gpsimd.tensor_scalar(self.ve[:, :], self.mv[:, :, 1], self.eps, None, ALU.add).then_inc(S["var_eps"], 1)
        pool.wait_ge(S["var_eps"], n + 1)
        nc.gpsimd.tensor_tensor(self.rs[:, :], self.ve[:, :], self.half[:, :], ALU.pow).then_inc(S["rstd"], 1)

    def tensor(self, nc, pe, n):
        S = self.S
        pe.wait_ge(S["xn"], TT * (n + 1))
        for c in range(DC):
            for t in range(TT):
                last = nc.tensor.transpose(self.banks[c][:, t * P:(t + 1) * P], self.xn[:, t, c * P:(c + 1) * P],
                                           self.ident[:, :])
            last.then_inc(S["hT_filled"], 1)

    def scalar(self, nc, act, n, scale, shift):
        S = self.S
        for c in range(DC):
            act.wait_ge(S["hT_filled"], DC * n + c + 1)
            nc.scalar.activation(self.hT[:, c, :], self.banks[c][:, :], ACT.Identity,
                                 bias=self.cur[:, shift + c:shift + c + 1],
                                 scale=self.cur[:, scale + c:scale + c + 1]).then_inc(S["hT"], 1)


class Gates:

    def __init__(self, sb, S, cur, ident, ones, bank, columns, rows=None):
        self.S, self.cur, self.ident, self.ones, self.bank, self.columns = S, cur, ident, ones, bank, columns
        self.diag = sb("gate_diag", [P, len(columns), D], FP32)
        self.rows = sb("gate_rows", [P, len(columns), D], FP32) if rows is None else rows

    def vector(self, nc, dve):
        for k, column in enumerate(self.columns):
            for c in range(DC):
                nc.vector.tensor_scalar(self.diag[:, k, c * P:(c + 1) * P], self.ident[:, :],
                                        self.cur[:, column + c:column + c + 1], None,
                                        ALU.mult).then_inc(self.S["gate_diag"], 1)

    def tensor(self, nc, pe):
        pe.wait_ge(self.S["gate_diag"], DC * len(self.columns))
        for k in range(len(self.columns)):
            last = nc.tensor.matmul(self.bank[:, k * D:(k + 1) * D], self.ones[:, :], self.diag[:, k, :],
                                    start=True, stop=True)
        last.then_inc(self.S["gate_filled"], 1)

    def scalar(self, nc, act):
        act.wait_ge(self.S["gate_filled"], 1)
        nc.scalar.activation(self.rows[:, :, :].rearrange("p k n -> p (k n)"), self.bank[:, 0:len(self.columns) * D],
                             ACT.Copy).then_inc(self.S["gate_rows"], 1)


def residual(nc, dve, S, banks, bias, gate, tmp, x_b, n, filled):
    steps = (bias is not None) + (gate is not None) + 1
    for k in range(2):
        done = 2 * steps * n + steps * k
        dve.wait_ge(S[filled], k + 1)
        y = banks[k][:, :].rearrange("p (t n) -> p t n", t=2)
        over = lambda row: row.unsqueeze(1).broadcast_to([P, 2, D])
        rows = [(row, op) for row, op in ((bias, ALU.add), (gate, ALU.mult)) if row is not None]
        for n_row, (row, op) in enumerate(rows):
            nc.vector.tensor_tensor(tmp[:, k, :, :], tmp[:, k, :, :] if n_row else y, over(row), op)\
                .then_inc(S["res"], 1)
            dve.wait_ge(S["res"], done + n_row + 1)
        x = x_b[:, 2 * k:2 * k + 2, :]
        nc.vector.tensor_tensor(x, x, tmp[:, k, :, :], ALU.add).then_inc(S["res"], 1)
    dve.wait_ge(S["res"], 2 * steps * (n + 1))


def mlp_tensor(nc, pe, S, banks, hT, w1, w2, g, n_hT):
    pe.wait_ge(S["hT"], n_hT)
    for j in range(MC):
        if j >= 4:
            pe.wait_ge(S["gelu"], j - 3)
        for c in range(DC):
            last = nc.tensor.matmul(banks[2 + j % 4][:, :], w1[:, c, j * P:(j + 1) * P], hT[:, c, :],
                                    start=(c == 0), stop=(c == DC - 1))
        last.then_inc(S["up_filled"], 1)
    pe.wait_ge(S["gelu"], MC)
    for t in range(TT):
        for j in range(MC):
            last = nc.tensor.matmul(banks[6 + t // 2][:, (t % 2) * D:(t % 2 + 1) * D], g[:, j, t * P:(t + 1) * P],
                                    w2[:, j, :], start=(j == 0), stop=(j == MC - 1))
        if t % 2:
            last.then_inc(S["down_filled"], 1)


def mlp_scalar(nc, act, S, banks, b1, g, func):
    for j in range(MC):
        act.wait_ge(S["up_filled"], j + 1)
        nc.scalar.activation(g[:, j, :], banks[2 + j % 4][:, :], func, bias=b1[:, j:j + 1]).then_inc(S["gelu"], 1)


def modulation(nc, consts, io):
    ident, ones, mod = consts["ident"], consts["ones"], consts["mod"]
    with ExitStack() as ctx:
        sb = lambda n, s, d: ctx.enter_context(nc.sbuf_tensor(n, s, d))
        w = sb("mod_w", [P, DC, MODS * P], FP32)
        bias = sb("mod_bias", [P, MODS], FP32)
        nw = sb("mod_norm_w", [P, 2 * DC], FP32)
        nb = sb("mod_norm_b", [P, 2 * DC], FP32)
        cT = sb("mod_cT", [P, DC, B], FP32)
        scT = sb("mod_silu_cT", [P, DC, B], FP32)
        acc = ctx.enter_context(nc.psum_tensor("mod_acc", [P, MODS, B], FP32))
        s_in = ctx.enter_context(nc.semaphore("mod_in"))
        s_w = [ctx.enter_context(nc.semaphore(f"mod_w{n}")) for n in range(2)]
        s_x = ctx.enter_context(nc.semaphore("mod_x"))
        s_sc = ctx.enter_context(nc.semaphore("mod_silu"))
        s_mm = ctx.enter_context(nc.semaphore("mod_filled"))
        s_v = ctx.enter_context(nc.semaphore("mod_steps"))
        s_c = ctx.enter_context(nc.semaphore("mod_consts"))
        half_cols = MODS // 2 * P
        with nc.Block() as block:

            @block.sync
            def _(sp):
                sp.dma_start(cT[:, :, :], io["condT"].rearrange("(c p) b -> p c b", p=P)).then_inc(s_in, 16)
                sp.dma_start(bias[:, :], io["mod_b"]).then_inc(s_in, 16)
                sp.dma_start(nw[:, :], io["norm_w"]).then_inc(s_in, 16)
                sp.dma_start(nb[:, :], io["norm_b"]).then_inc(s_in, 16)
                wv = io["mod_w"].rearrange("(c p) n -> p c n", p=P)
                for n in range(2):
                    sp.dma_start(w[:, :, n * half_cols:(n + 1) * half_cols],
                                 wv[:, :, n * half_cols:(n + 1) * half_cols]).then_inc(s_w[n], 16)
                sp.dma_start(consts["x"][:, :, :, :].rearrange("p b t d -> p (b t) d"),
                             io["x"].rearrange("b (t p) d -> p (b t) d", p=P)).then_inc(s_x, 16)
                sp.wait_ge(s_x, 16)

            @block.gpsimd
            def _(pool):
                nc.gpsimd.memset(ident[:, :], 0.0).then_inc(s_c, 1)
                pool.wait_ge(s_c, 1)
                nc.gpsimd.affine_select(out=ident[:, :], in_=ident[:, :], compare_op=ALU.not_equal, fill=1.0,
                                        base=0, pattern=[[-1, P]], channel_multiplier=1).then_inc(s_c, 1)
                nc.gpsimd.memset(ones[:, :], 1.0).then_inc(s_c, 1)
                nc.gpsimd.memset(consts["half"][:, :], -0.5).then_inc(s_c, 1)

            @block.scalar
            def _(act):
                act.wait_ge(s_in, 64)
                nc.scalar.activation(scT[:, :, :], cT[:, :, :], ACT.Silu).then_inc(s_sc, 1)

            @block.tensor
            def _(pe):
                pe.wait_ge(s_in, 64)
                pe.wait_ge(s_sc, 1)
                for m in range(MODS):
                    if m % (MODS // 2) == 0:
                        pe.wait_ge(s_w[m // (MODS // 2)], 16)
                    c_in = cT if m < MOD1 else scT
                    for c in range(DC):
                        last = nc.tensor.matmul(acc[:, m, :], w[:, c, m * P:(m + 1) * P], c_in[:, c, :],
                                                start=(c == 0), stop=(c == DC - 1))
                last.then_inc(s_mm, 1)

            @block.vector
            def _(dve):
                dve.wait_ge(s_mm, 1)
                done = [0]

                def step(instruction):
                    instruction.then_inc(s_v, 1)
                    done[0] += 1

                step(nc.vector.tensor_tensor(mod[:, :, :].rearrange("p b m -> p m b"), acc[:, :, :],
                                             bias[:, :].unsqueeze(2).broadcast_to([P, MODS, B]), ALU.add))
                dve.wait_ge(s_v, done[0])
                scales = [MOD0, MOD0 + 2 * DC] + [m + k * DC for m in (MOD1, MOD2, MOD3) for k in (1, 4)]
                for col in scales:
                    step(nc.vector.tensor_scalar(mod[:, :, col:col + DC], mod[:, :, col:col + DC], 1.0, None, ALU.add))
                dve.wait_ge(s_v, done[0])
                for k in range(2):
                    for c in range(DC):
                        sh, sc = MOD3 + 3 * k * DC + c, MOD3 + (3 * k + 1) * DC + c
                        n = k * DC + c
                        step(nc.vector.scalar_tensor_tensor(mod[:, :, sh], mod[:, :, sc], nb[:, n:n + 1],
                                                            mod[:, :, sh], ALU.mult, ALU.add))
                        dve.wait_ge(s_v, done[0])
                        step(nc.vector.tensor_scalar(mod[:, :, sc], mod[:, :, sc], nw[:, n:n + 1], None, ALU.mult))
    nc.all_engine_barrier()


def narrow_attention_layer(nc, consts, io, tag, mod0, eps, masked):
    ident, ones, mod = consts["ident"], consts["ones"], consts["mod"]
    x = consts["x"]
    gated = masked
    k_max = STACK + (1 if masked else 0)
    k_all = k_max + 2
    if masked:
        scale1, shift1, gate1, scale2, shift2, gate2 = DC, 0, 2 * DC, 4 * DC, 3 * DC, 5 * DC
    else:
        scale1, shift1, gate1, scale2, shift2, gate2 = 0, DC, None, 2 * DC, 3 * DC, None
    n_mod = 6 * DC if gated else 4 * DC
    TILES = H * TT
    GT = GH * TT
    LEAD = 28
    SLOTS = 3 * GH
    CH = H // DC
    with ExitStack() as ctx:
        def sb(name, shape, dt):
            return ctx.enter_context(nc.sbuf_tensor(f"{tag}_{name}", shape, dt))

        wq, wk, wv = (sb(f"w{n}", [P, DC, D], FP32) for n in "qkv")
        wo = sb("wo", [P, NG, D], FP32)
        w1 = sb("w1", [P, DC, MLP], FP32)
        w2 = sb("w2", [P, MC, D], FP32)
        bqk = sb("bqk", [P, 2 * DC], FP32)
        bv, bo, b2 = (sb(n, [P, D], FP32) for n in ("bv", "bo", "b2"))
        b1 = sb("b1", [P, MC], FP32)
        cur = sb("cur", [P, n_mod], FP32)
        qk = sb("qk", [P, 2 * DC, T], FP32)
        parts = sb("parts", [P, 2 * DC, SPLIT, T], BF16)
        qs = sb("q_stack", [k_all, H, T], BF16)
        ks = sb("k_stack", [k_all, H, T], BF16)
        va = sb("v_and_ones", [P, TT, H, 2 * HD], FP32)
        mx = sb("row_max", [P, NG, TT, GH], FP32)
        mrow = sb("max_rows", [GH, 2, T], BF16)
        probs = sb("probs", [P, SLOTS, T], FP32)
        oT = sb("oT", [P, NG, T], FP32)
        rec = sb("rec", [P, T], FP32)
        sel_sum = sb("sel_sum", [P, NG, H], FP32)
        sel_head = sb("sel_head", [P, NG, P], FP32)
        g = sb("g", [P, MC, T], FP32)
        tmp = sb("res_tmp", [P, 2, 2, D], FP32)
        pm = sb("q_valid", [P, T], FP32) if masked else None
        scratch = nc.dram_tensor(f"{tag}_parts_dram", (DC, 2, P, SPLIT, T), BF16, kind="Internal").ap()
        psum = ctx.enter_context(nc.psum_tensor(f"{tag}_psum", [P, 8, T], FP32))
        bank = [psum[:, n, :] for n in range(8)]
        pair = lambda n: psum[:, 2 + 2 * (n // 2 % 2):4 + 2 * (n // 2 % 2), :]
        S = Semaphores(consts["pool"], LN_SEMS + [
            "cur", "gate_diag", "gate_filled", "gate_rows", "qk_filled", "v_filled", "qk", "part1", "rest", "part2",
            "part3", "v", "parts_out0", "parts_out1", "parts_out2", "parts_out3", "stacks0", "stacks1", "mask_in", "max_filled", "max_taken",
            "maxT_filled", "max_part1", "max_part2", "max_rows", "st_filled", "exp", "av", "oT", "sum_filled", "rec",
            "head_filled", "oT_norm", "y_filled", "res", "up_filled", "gelu", "down_filled"])
        s_w, s_i, s_p, s_a = consts["init_sems"]
        norm = Norm(sb, S, lambda b: x[:, bass.ds(b, 1), :, :].rearrange("p b t d -> p (b t) d"), cur, ident,
                    consts["half"], bank, eps)
        gates = Gates(sb, S, cur, ident, ones, bank[7], [gate1, gate2]) if gated else None

        with nc.Block() as block:

            @block.sync
            def _(sp):
                n = 0
                for to, of in ((wq, "wq"), (wk, "wk"), (wv, "wv"), (w1, "w1"), (w2, "w2")):
                    sp.dma_start(to[:, :, :], io[tag + of].rearrange("(c p) n -> p c n", p=P)).then_inc(s_w, 16)
                    n += 1
                for to, of in ((bv, "bv"), (bo, "bo"), (b2, "b2")):
                    sp.dma_start(to[:, :], io[tag + of].unsqueeze(0).broadcast_to([P, D])).then_inc(s_w, 16)
                    n += 1
                sp.dma_start(b1[:, :], io[tag + "b1"]).then_inc(s_w, 16)
                sp.dma_start(bqk[:, 0:DC], io[tag + "bq"]).then_inc(s_w, 16)
                sp.dma_start(bqk[:, DC:2 * DC], io[tag + "bk"]).then_inc(s_w, 16)
                sp.wait_ge(s_i, 1)
                wo_v = io[tag + "wo"].rearrange("(g j d) n -> j d g n", j=GH, d=HD)
                for j in range(GH):
                    sp.dma_start(wo[j * 2 * HD:j * 2 * HD + HD, :, :], wo_v[j]).then_inc(s_w, 16)
                sp.wait_ge(s_w, 16 * (n + 3 + GH))

            @block.vector
            def _(dve):
                nc.vector.memset(wo[:, :, :], 0.0).then_inc(s_i, 1)
                nc.vector.memset(rec[:, :], 0.0).then_inc(s_i, 1)
                nc.vector.memset(va[:, :, :, HD:2 * HD], 1.0).then_inc(s_i, 1)
                nc.vector.memset(ks[STACK:k_all, :, :], 1.0).then_inc(s_i, 1)

            @block.gpsimd
            def _(pool):
                nc.gpsimd.memset(sel_sum[:, :, :], 0.0).then_inc(s_p, 1)
                nc.gpsimd.memset(sel_head[:, :, :], 0.0).then_inc(s_p, 1)
                pool.wait_ge(s_p, 2)
                for gg in range(NG):
                    nc.gpsimd.affine_select(
                        out=sel_sum[:, gg, gg * GH:(gg + 1) * GH], in_=sel_sum[:, gg, gg * GH:(gg + 1) * GH],
                        compare_op=ALU.not_equal, fill=1.0, base=-HD, pattern=[[-2 * HD, GH]], channel_multiplier=1)
                    nc.gpsimd.affine_select(
                        out=sel_head[:, gg, :].rearrange("p (j r) -> p j r", j=GH),
                        in_=sel_head[:, gg, :].rearrange("p (j r) -> p j r", j=GH),
                        compare_op=ALU.not_equal, fill=1.0, base=-gg * GH, pattern=[[-1, GH], [0, 2 * HD]],
                        channel_multiplier=1)

        nc.all_engine_barrier(sems_to_clear=range(s_w.num, s_a.num + 1))

        with nc.Fori(0, B) as b:
            x_b = x[:, bass.ds(b, 1), :, :].rearrange("p b t d -> p (b t) d")
            with nc.Block() as block:

                @block.sync
                def _(sp):
                    if masked:
                        valid, valid16, bar16 = io["valid"], io["valid16"], io["bar16"]
                        sp.dma_start(pm[:, :], valid[bass.ds(b, 1), :].broadcast_to([P, T])).then_inc(S["mask_in"], 16)
                        row = lambda a: a[bass.ds(b, 1), :].unsqueeze(1).broadcast_to([1, H, T])
                        sp.dma_start(qs[STACK:STACK + 1, :, :], row(valid16)).then_inc(S["mask_in"], 16)
                        sp.dma_start(ks[STACK:STACK + 1, :, :], row(bar16)).then_inc(S["mask_in"], 16)
                    for m in range(2 * DC):
                        sp.wait_ge(S["part3"], m + 1)
                        sp.dma_start(scratch[m // 2, m % 2, :, :, :], parts[:, m, :, :])\
                            .then_inc(S[f"parts_out{m}"], 16)
                        if m % 2:
                            c = m // 2
                            for which, stack, part in ((0, qs, Q_PART), (1, ks, K_PART)):
                                sp.wait_ge(S[f"parts_out{2 * c + which}"], 16)
                                for s, p_ in enumerate(part):
                                    of = scratch[c, which, :, p_, :].rearrange("(h d) t -> d h t", d=HD)
                                    sp.dma_start(stack[s * HD:(s + 1) * HD, c * CH:(c + 1) * CH, :], of)\
                                        .then_inc(S[f"stacks{c}"], 16)
                    for gg in range(NG):
                        sp.wait_ge(S["max_part2"], gg + 1)
                        for k in range(2):
                            sp.dma_start(qs[k_max + k:k_max + k + 1, gg * GH:(gg + 1) * GH, :],
                                         mrow[:, k, :]).then_inc(S["max_rows"], 16)
                        sp.wait_ge(S["max_rows"], 32 * (gg + 1))

                @block.gpsimd
                def _(pool):
                    norm.gpsimd(nc, pool, 0)
                    norm.gpsimd(nc, pool, 1)

                @block.vector
                def _(dve):
                    nc.vector.tensor_copy(cur[:, :], mod[:, bass.ds(b, 1), mod0:mod0 + n_mod]
                                          .rearrange("p b m -> p (b m)")).then_inc(S["cur"], 1)
                    norm.vector(nc, dve, b, 0)
                    if gated:
                        dve.wait_ge(S["cur"], 1)
                        gates.vector(nc, dve)
                    if masked:
                        dve.wait_ge(S["mask_in"], 48)
                    for c in range(DC):
                        for m in (2 * c, 2 * c + 1):
                            dve.wait_ge(S["qk_filled"], m + 1)
                            b_col = bqk[:, (m % 2) * DC + c:(m % 2) * DC + c + 1]
                            if masked and m % 2 == 0:
                                nc.vector.scalar_tensor_tensor(qk[:, m, :], bank[2 + m], b_col, pm[:, :],
                                                               ALU.add, ALU.mult).then_inc(S["qk"], 1)
                            else:
                                nc.vector.tensor_scalar(qk[:, m, :], bank[2 + m], b_col, None,
                                                        ALU.add).then_inc(S["qk"], 1)
                        for m in (2 * c, 2 * c + 1):
                            dve.wait_ge(S["part1"], m + 1)
                            nc.vector.tensor_tensor(qk[:, m, :], qk[:, m, :], parts[:, m, 0, :],
                                                    ALU.subtract).then_inc(S["rest"], 1)
                        for m in (2 * c, 2 * c + 1):
                            dve.wait_ge(S["part2"], m + 1)
                            nc.vector.tensor_tensor(parts[:, m, 2, :], qk[:, m, :], parts[:, m, 1, :],
                                                    ALU.subtract).then_inc(S["part3"], 1)
                    for k in range(2):
                        dve.wait_ge(S["v_filled"], k + 1)
                        nc.vector.tensor_tensor(
                            va[:, 2 * k:2 * k + 2, :, 0:HD],
                            bank[6 + k].rearrange("p (t h d) -> p t h d", t=2, h=H),
                            bv[:, :].rearrange("p (h d) -> p h d", h=H).unsqueeze(1).broadcast_to([P, 2, H, HD]),
                            ALU.add).then_inc(S["v"], 1)

                    def take_max(n):
                        dve.wait_ge(S["max_filled"], n + 1)
                        h, t = n // TT, n % TT
                        nc.vector.tensor_reduce(mx[:, h // GH, t, h % GH:h % GH + 1], bank[n % 2], AX.X, ALU.max)\
                            .then_inc(S["max_taken"], 1)

                    def max_rows(gg):
                        dve.wait_ge(S["maxT_filled"], gg + 1)
                        if gg:
                            dve.wait_ge(S["max_rows"], 32 * gg)
                        nc.vector.tensor_scalar(mrow[:, 0, :], bank[6][0:GH, :], -1.0, None,
                                                ALU.mult).then_inc(S["max_part1"], 1)
                        dve.wait_ge(S["max_part1"], gg + 1)
                        nc.vector.scalar_tensor_tensor(mrow[:, 1, :], bank[6][0:GH, :], -1.0, mrow[:, 0, :],
                                                       ALU.mult, ALU.subtract).then_inc(S["max_part2"], 1)

                    for n in range(TILES + 2 * GT + LEAD):
                        if n < TILES:
                            take_max(n)
                        if n % GT == 3 and GT < n < TILES + GT:
                            max_rows(n // GT - 1)
                        gg, at = divmod(n - LEAD - GT - 6, GT)
                        if at == 0 and 0 <= gg < NG:
                            dve.wait_ge(S["av"], TT * (gg + 1))
                            nc.vector.tensor_copy(oT[:, gg, :], bank[7]).then_inc(S["oT"], 1)
                    dve.wait_ge(S["sum_filled"], 1)
                    nc.vector.reciprocal(rec[0:H, :], bank[6][0:H, :]).then_inc(S["rec"], 1)
                    for gg in range(NG):
                        dve.wait_ge(S["head_filled"], gg + 1)
                        nc.vector.tensor_tensor(oT[:, gg, :], oT[:, gg, :], bank[gg],
                                                ALU.mult).then_inc(S["oT_norm"], 1)
                    if gated:
                        dve.wait_ge(S["gate_rows"], 1)
                    residual(nc, dve, S, bank[4:6], bo[:, :], gates.rows[:, 0, :] if gated else None, tmp, x_b, 0,
                             "y_filled")
                    norm.vector(nc, dve, b, 1)
                    residual(nc, dve, S, bank[6:8], b2[:, :], gates.rows[:, 1, :] if gated else None, tmp, x_b, 1,
                             "down_filled")

                @block.scalar
                def _(act):
                    act.wait_ge(S["cur"], 1)
                    norm.scalar(nc, act, 0, scale1, shift1)
                    if gated:
                        gates.scalar(nc, act)
                    for c in range(DC):
                        for m in (2 * c, 2 * c + 1):
                            act.wait_ge(S["qk"], m + 1)
                            nc.scalar.activation(parts[:, m, 0, :], qk[:, m, :], ACT.Copy).then_inc(S["part1"], 1)
                        for m in (2 * c, 2 * c + 1):
                            act.wait_ge(S["rest"], m + 1)
                            nc.scalar.activation(parts[:, m, 1, :], qk[:, m, :], ACT.Copy).then_inc(S["part2"], 1)
                    for n in range(0, TILES, 2):
                        act.wait_ge(S["st_filled"], n // 2 + 1)
                        if n >= SLOTS:
                            act.wait_ge(S["av"], (n - SLOTS) // GH + 1)
                        nc.scalar.activation(probs[:, n % SLOTS:n % SLOTS + 2, :], pair(n), ACT.Exp,
                                             scale=float(HD) ** -0.5).then_inc(S["exp"], 1)
                    norm.scalar(nc, act, 1, scale2, shift2)
                    mlp_scalar(nc, act, S, bank, b1, g, ACT.Gelu_apprx_tanh if masked else ACT.Gelu)

                @block.tensor
                def _(pe):
                    norm.tensor(nc, pe, 0)
                    if gated:
                        gates.tensor(nc, pe)
                    pe.wait_ge(S["hT"], DC)
                    for m in range(2 * DC):
                        w = (wq, wk)[m % 2]
                        for c in range(DC):
                            last = nc.tensor.matmul(bank[2 + m], w[:, c, m // 2 * P:(m // 2 + 1) * P],
                                                    norm.hT[:, c, :], start=(c == 0), stop=(c == DC - 1))
                        last.then_inc(S["qk_filled"], 1)
                    if gated:
                        pe.wait_ge(S["gate_rows"], 1)
                    for t in range(TT):
                        for c in range(DC):
                            last = nc.tensor.matmul(bank[6 + t // 2][:, (t % 2) * D:(t % 2 + 1) * D],
                                                    norm.hT[:, c, t * P:(t + 1) * P], wv[:, c, :],
                                                    start=(c == 0), stop=(c == DC - 1))
                        if t % 2:
                            last.then_inc(S["v_filled"], 1)

                    def scores(n):
                        h, t = n // TT, n % TT
                        if h % CH == 0 and t == 0:
                            pe.wait_ge(S[f"stacks{h // CH}"], 16 * 2 * len(Q_PART))
                        if n >= 2:
                            pe.wait_ge(S["max_taken"], n - 1)
                        nc.tensor.matmul(bank[n % 2], qs[0:k_max, h, t * P:(t + 1) * P], ks[0:k_max, h, :],
                                         start=True, stop=True).then_inc(S["max_filled"], 1)

                    def max_rows(gg):
                        pe.wait_ge(S["max_taken"], GT * (gg + 1))
                        if gg:
                            pe.wait_ge(S["max_part2"], gg)
                        else:
                            pe.wait_ge(S["v"], 2)
                        for t in range(TT):
                            last = nc.tensor.transpose(bank[6][0:GH, t * P:(t + 1) * P], mx[:, gg, t, :], ident[:, :])
                        last.then_inc(S["maxT_filled"], 1)

                    def scores_T(n):
                        if n % GT == 0:
                            pe.wait_ge(S["max_rows"], 32 * (n // GT + 1))
                        if n >= 4:
                            pe.wait_ge(S["exp"], n // 2 - 1)
                        for i in range(2):
                            gg, k, j = n // GT, n // GH % TT, n % GH + i
                            last = nc.tensor.matmul(pair(n)[:, i, :], ks[0:k_all, gg * GH + j, k * P:(k + 1) * P],
                                                    qs[0:k_all, gg * GH + j, :], start=True, stop=True)
                        last.then_inc(S["st_filled"], 1)

                    def values(q):
                        gg, k = q // TT, q % TT
                        if k == 0 and gg:
                            pe.wait_ge(S["oT"], gg)
                        pe.wait_ge(S["exp"], 2 * (q + 1))
                        for j in range(GH):
                            last = nc.tensor.matmul(bank[7][2 * HD * j:2 * HD * (j + 1), :],
                                                    va[:, k, gg * GH + j, :], probs[:, (GH * q + j) % SLOTS, :],
                                                    start=(k == 0), stop=(k == TT - 1))
                        last.then_inc(S["av"], 1)

                    if masked:
                        pe.wait_ge(S["mask_in"], 48)
                    for n in range(TILES + GT + LEAD):
                        if n < TILES:
                            scores(n)
                        if n % GT == 2 and GT < n < TILES + GT:
                            max_rows(n // GT - 1)
                        m = n - LEAD - 1
                        if m >= 0 and m % 2 == 0 and m < TILES:
                            scores_T(m)
                        if m > GH and m % GH == 2 and m < TILES + GH:
                            values(m // GH - 1)
                    pe.wait_ge(S["oT"], NG)
                    pe.wait_ge(S["max_part2"], NG)
                    for gg in range(NG):
                        last = nc.tensor.matmul(bank[6][0:H, :], sel_sum[:, gg, :], oT[:, gg, :],
                                                start=(gg == 0), stop=(gg == NG - 1))
                    last.then_inc(S["sum_filled"], 1)
                    pe.wait_ge(S["rec"], 1)
                    for gg in range(NG):
                        nc.tensor.matmul(bank[gg], sel_head[:, gg, :], rec[:, :], start=True, stop=True)\
                            .then_inc(S["head_filled"], 1)
                    pe.wait_ge(S["oT_norm"], NG)
                    for t in range(TT):
                        for gg in range(NG):
                            last = nc.tensor.matmul(bank[4 + t // 2][:, (t % 2) * D:(t % 2 + 1) * D],
                                                    oT[:, gg, t * P:(t + 1) * P], wo[:, gg, :],
                                                    start=(gg == 0), stop=(gg == NG - 1))
                        if t % 2:
                            last.then_inc(S["y_filled"], 1)
                    norm.tensor(nc, pe, 1)
                    mlp_tensor(nc, pe, S, bank, norm.hT, w1, w2, g, 2 * DC)

            nc.all_engine_barrier(sems_to_clear=S.range)


def wide_attention_layer(nc, consts, io, tag, mod0, eps):
    ident, ones, mod, x = consts["ident"], consts["ones"], consts["mod"], consts["x"]
    shift1, scale1, gate1, shift2, scale2, gate2 = (k * DC for k in range(6))
    n_mod = 6 * DC
    PG = GH // 2
    GW = GH * HD1
    with ExitStack() as ctx:
        def sb(name, shape, dt):
            return ctx.enter_context(nc.sbuf_tensor(f"{tag}_{name}", shape, dt))

        wq, wk, wv = (sb(f"w{n}", [P, DC, INNER1], FP32) for n in "qkv")
        wo = sb("wo", [P, INNER1 // P, D], FP32)
        w1 = sb("w1", [P, DC, MLP], FP32)
        w2 = sb("w2", [P, MC, D], FP32)
        bo, b2 = (sb(n, [P, D], FP32) for n in ("bo", "b2"))
        b1 = sb("b1", [P, MC], FP32)
        cur = sb("cur", [P, n_mod], FP32)
        qz = sb("q_heads", [P, 2, GH, T], FP32)
        kz = sb("k_heads", [P, 2, GH, T], FP32)
        v = sb("v", [P, 2, TT, GW], FP32)
        mx = sb("row_max", [P, NG, TT, GH], FP32)
        mrow = sb("max_rows", [GH, T], FP32)
        probs = sb("probs", [P, 2 * GH, T], FP32)
        oT = sb("oT", [P, INNER1 // P, T], FP32)
        rec = sb("rec", [P, T], FP32)
        sel = sb("sel_pair", [P, PG, P], FP32)
        g = sb("g", [P, MC, T], FP32)
        tmp = sb("res_tmp", [P, 2, 2, D], FP32)
        bank = [ctx.enter_context(nc.psum_tensor(f"{tag}_bank{n}", [P, T], FP32)) for n in range(8)]
        S = Semaphores(consts["pool"], LN_SEMS + [
            "cur", "gate_diag", "gate_filled", "gate_rows", "proj_filled", "proj", "no_max", "max_filled", "max_taken",
            "maxT_filled", "max_neg", "max_rows", "st_filled", "exp", "av", "oT", "rec", "head_filled", "oT_norm",
            "y_filled", "res", "up_filled", "gelu", "down_filled"])
        s_w, s_i, s_p, s_a = consts["init_sems"]
        norm = Norm(sb, S, lambda b: x[:, bass.ds(b, 1), :, :].rearrange("p b t d -> p (b t) d"), cur, ident,
                    consts["half"], bank, eps)
        gates = Gates(sb, S, cur, ident, ones, bank[7], [gate1, gate2])
        own = lambda j: slice(HD1 * (j % 2), HD1 * (j % 2) + HD1)
        aux = lambda j: HD1 * (1 - j % 2)

        with nc.Block() as block:

            @block.sync
            def _(sp):
                n = 0
                for to, of in ((wq, "wq"), (wk, "wk"), (wv, "wv"), (wo, "wo"), (w1, "w1"), (w2, "w2")):
                    sp.dma_start(to[:, :, :], io[tag + of].rearrange("(c p) n -> p c n", p=P)).then_inc(s_w, 16)
                    n += 1
                for to, of in ((bo, "bo"), (b2, "b2")):
                    sp.dma_start(to[:, :], io[tag + of].unsqueeze(0).broadcast_to([P, D])).then_inc(s_w, 16)
                    n += 1
                sp.dma_start(b1[:, :], io[tag + "b1"]).then_inc(s_w, 16)
                sp.wait_ge(s_w, 16 * (n + 1))

            @block.vector
            def _(dve):
                nc.vector.memset(qz[:, :, :, :], 0.0).then_inc(s_i, 1)
                nc.vector.memset(kz[:, :, :, :], 0.0).then_inc(s_i, 1)
                dve.wait_ge(s_i, 2)
                for j in range(GH):
                    nc.vector.memset(kz[aux(j):aux(j) + 1, :, j, :], 1.0).then_inc(s_i, 1)

            @block.gpsimd
            def _(pool):
                nc.gpsimd.memset(sel[:, :, :], 0.0).then_inc(s_p, 1)
                pool.wait_ge(s_p, 1)
                view = sel[:, :, :].rearrange("p q (a r) -> p q a r", a=2)
                nc.gpsimd.affine_select(out=view, in_=view, compare_op=ALU.not_equal, fill=1.0, base=0,
                                        pattern=[[-HD1, PG], [-HD1 // 2, 2], [0, HD1]], channel_multiplier=1)

        nc.all_engine_barrier(sems_to_clear=range(s_w.num, s_a.num + 1))

        with nc.Fori(0, B) as b:
            x_b = x[:, bass.ds(b, 1), :, :].rearrange("p b t d -> p (b t) d")
            PROJ = 2 * PG + 2
            PRING = (7, 0, 1)
            with nc.Block() as block:

                @block.sync
                def _(sp):
                    for gg in range(NG):
                        sp.wait_ge(S["max_neg"], gg + 1)
                        for j in range(GH):
                            sp.dma_start(qz[aux(j):aux(j) + 1, gg % 2, j, :], mrow[j:j + 1, :])\
                                .then_inc(S["max_rows"], 16)
                        sp.wait_ge(S["max_rows"], 16 * GH * (gg + 1))

                @block.gpsimd
                def _(pool):
                    norm.gpsimd(nc, pool, 0)
                    pool.wait_ge(S["rstd"], 1)
                    for gg in range(NG):
                        if gg >= 2:
                            pool.wait_ge(S["st_filled"], GH * TT * (gg - 1))
                        for j in range(GH):
                            if gg or j:
                                pool.wait_ge(S["no_max"], gg * GH + j)
                            nc.gpsimd.memset(qz[aux(j):aux(j) + 1, gg % 2, j, :], 0.0).then_inc(S["no_max"], 1)
                    norm.gpsimd(nc, pool, 1)

                @block.vector
                def _(dve):
                    nc.vector.tensor_copy(cur[:, :], mod[:, bass.ds(b, 1), mod0:mod0 + n_mod]
                                          .rearrange("p b m -> p (b m)")).then_inc(S["cur"], 1)
                    norm.vector(nc, dve, b, 0)
                    dve.wait_ge(S["cur"], 1)
                    gates.vector(nc, dve)

                    def take_max(gg, j):
                        for t in range(TT):
                            n = (gg * GH + j) * TT + t
                            dve.wait_ge(S["max_filled"], n + 1)
                            nc.vector.tensor_reduce(mx[:, gg, t, j:j + 1], bank[n % 2][:, :], AX.X, ALU.max)\
                                .then_inc(S["max_taken"], 1)

                    def max_rows(gg):
                        dve.wait_ge(S["maxT_filled"], gg + 1)
                        if gg:
                            dve.wait_ge(S["max_rows"], 16 * GH * gg)
                        nc.vector.tensor_scalar(mrow[:, :], bank[7][0:GH, :], -1.0, None,
                                                ALU.mult).then_inc(S["max_neg"], 1)

                    def normalise(gg, p):
                        dve.wait_ge(S["head_filled"], PG * gg + p + 1)
                        dve.wait_ge(S["oT"], PG * gg + p + 1)
                        nc.vector.tensor_tensor(oT[:, PG * gg + p, :], oT[:, PG * gg + p, :], bank[7][:, :],
                                                ALU.mult).then_inc(S["oT_norm"], 1)

                    for j in range(GH):
                        take_max(0, j)
                    max_rows(0)
                    for gg in range(NG):
                        for k in range(TT):
                            if gg + 1 < NG:
                                take_max(gg + 1, k)
                            if gg and 1 <= k <= PG:
                                normalise(gg - 1, k - 1)
                        if gg + 1 < NG:
                            max_rows(gg + 1)
                        dve.wait_ge(S["av"], TT * (gg + 1))
                        nc.vector.reciprocal(rec[:, :], bank[6][:, :]).then_inc(S["rec"], 1)
                    for p in range(PG):
                        normalise(NG - 1, p)
                    dve.wait_ge(S["gate_rows"], 1)
                    residual(nc, dve, S, bank[4:6], bo[:, :], gates.rows[:, 0, :], tmp, x_b, 0, "y_filled")
                    norm.vector(nc, dve, b, 1)
                    residual(nc, dve, S, bank[6:8], b2[:, :], gates.rows[:, 1, :], tmp, x_b, 1, "down_filled")

                @block.scalar
                def _(act):
                    act.wait_ge(S["cur"], 1)
                    norm.scalar(nc, act, 0, scale1, shift1)
                    gates.scalar(nc, act)

                    def projected(gg):
                        for m in range(PROJ):
                            n = gg * PROJ + m
                            act.wait_ge(S["proj_filled"], n + 1)
                            src = bank[PRING[m % 3]]
                            if m < 2 * PG:
                                to, pair = (qz, kz)[m // PG], m % PG
                                for j in (2 * pair, 2 * pair + 1):
                                    nc.scalar.activation(to[own(j), gg % 2, j, :], src[own(j), :],
                                                         ACT.Copy).then_inc(S["proj"], 1)
                            else:
                                t = 2 * (m - 2 * PG)
                                nc.scalar.activation(v[:, gg % 2, t:t + 2, :].rearrange("p t n -> p (t n)"), src[:, :],
                                                     ACT.Copy).then_inc(S["proj"], 2)

                    projected(0)
                    for gg in range(NG):
                        for k in range(TT):
                            if gg + 1 < NG and k == 0:
                                projected(gg + 1)
                            for j in range(GH):
                                n = (gg * TT + k) * GH + j
                                act.wait_ge(S["st_filled"], n + 1)
                                if n >= 2 * GH:
                                    act.wait_ge(S["av"], n // GH - 1)
                                nc.scalar.activation(probs[:, n % (2 * GH), :], bank[2 + n % 2][:, :], ACT.Exp,
                                                     scale=float(HD1) ** -0.5).then_inc(S["exp"], 1)
                        act.wait_ge(S["av"], TT * (gg + 1))
                        for p in range(PG):
                            nc.scalar.activation(oT[:, PG * gg + p, :], bank[4 + p][:, :],
                                                 ACT.Copy).then_inc(S["oT"], 1)
                    norm.scalar(nc, act, 1, scale2, shift2)
                    mlp_scalar(nc, act, S, bank, b1, g, ACT.Gelu)

                @block.tensor
                def _(pe):
                    norm.tensor(nc, pe, 0)
                    gates.tensor(nc, pe)
                    pe.wait_ge(S["hT"], DC)
                    pe.wait_ge(S["gate_rows"], 1)

                    def project(gg):
                        for m in range(PROJ):
                            if m == 0 and gg:
                                pe.wait_ge(S["max_neg"], gg)
                            if m == 0 and gg >= 3:
                                pe.wait_ge(S["oT_norm"], PG * (gg - 2))
                            if m == 1 and gg:
                                pe.wait_ge(S["max_taken"], TT * GH * gg)
                            if m >= 3:
                                pe.wait_ge(S["proj"], 2 * (gg * PROJ + m - 2))
                            to = bank[PRING[m % 3]]
                            if m < 2 * PG:
                                w, cols = (wq, wk)[m // PG], gg * GW + (m % PG) * P
                                for c in range(DC):
                                    last = nc.tensor.matmul(to[:, :], w[:, c, cols:cols + P], norm.hT[:, c, :],
                                                            start=(c == 0), stop=(c == DC - 1))
                            else:
                                for u in range(2):
                                    t = 2 * (m - 2 * PG) + u
                                    for c in range(DC):
                                        last = nc.tensor.matmul(to[:, u * GW:(u + 1) * GW],
                                                                norm.hT[:, c, t * P:(t + 1) * P],
                                                                wv[:, c, gg * GW:(gg + 1) * GW],
                                                                start=(c == 0), stop=(c == DC - 1))
                            last.then_inc(S["proj_filled"], 1)

                    def scores(gg, j):
                        if j == 0:
                            pe.wait_ge(S["proj"], 2 * PROJ * (gg + 1))
                            pe.wait_ge(S["no_max"], GH * (gg + 1))
                        for t in range(TT):
                            n = (gg * GH + j) * TT + t
                            if n >= 2:
                                pe.wait_ge(S["max_taken"], n - 1)
                            nc.tensor.matmul(bank[n % 2][:, :], qz[:, gg % 2, j, t * P:(t + 1) * P],
                                             kz[:, gg % 2, j, :], start=True, stop=True).then_inc(S["max_filled"], 1)

                    def max_rows(gg):
                        pe.wait_ge(S["max_taken"], TT * GH * (gg + 1))
                        if gg >= 2:
                            pe.wait_ge(S["oT_norm"], PG * (gg - 1))
                        for t in range(TT):
                            last = nc.tensor.transpose(bank[7][0:GH, t * P:(t + 1) * P], mx[:, gg, t, :], ident[:, :])
                        last.then_inc(S["maxT_filled"], 1)

                    def scores_T(gg, k):
                        for j in range(GH):
                            n = (gg * TT + k) * GH + j
                            if n >= 2:
                                pe.wait_ge(S["exp"], n - 1)
                            nc.tensor.matmul(bank[2 + n % 2][:, :], kz[:, gg % 2, j, k * P:(k + 1) * P],
                                             qz[:, gg % 2, j, :], start=True, stop=True).then_inc(S["st_filled"], 1)

                    def values(gg, k):
                        if k == 0 and gg:
                            pe.wait_ge(S["oT"], PG * gg)
                            pe.wait_ge(S["rec"], gg)
                        pe.wait_ge(S["exp"], GH * (gg * TT + k + 1))
                        slot = lambda j: ((gg * TT + k) * GH + j) % (2 * GH)
                        for j in range(GH):
                            nc.tensor.matmul(bank[4 + j // 2][own(j), :], v[:, gg % 2, k, j * HD1:(j + 1) * HD1],
                                             probs[:, slot(j), :], start=(k == 0), stop=(k == TT - 1))
                        for j in range(GH):
                            last = nc.tensor.matmul(bank[6][32 * j:32 * (j + 1), :], ones[:, 0:32],
                                                    probs[:, slot(j), :], start=(k == 0), stop=(k == TT - 1))
                        last.then_inc(S["av"], 1)

                    def spread(gg, p):
                        pe.wait_ge(S["rec"], gg + 1)
                        if p:
                            pe.wait_ge(S["oT_norm"], PG * gg + p)
                        nc.tensor.matmul(bank[7][:, :], sel[:, p, :], rec[:, :], start=True, stop=True)\
                            .then_inc(S["head_filled"], 1)

                    project(0)
                    for j in range(GH):
                        scores(0, j)
                    max_rows(0)
                    for gg in range(NG):
                        for k in range(TT):
                            if gg + 1 < NG and k == 0:
                                project(gg + 1)
                            if gg + 1 < NG:
                                scores(gg + 1, k)
                            if k == 0:
                                pe.wait_ge(S["max_rows"], 16 * GH * (gg + 1))
                            scores_T(gg, k)
                            if gg and 1 <= k <= PG:
                                spread(gg - 1, k - 1)
                            if k:
                                values(gg, k - 1)
                        if gg + 1 < NG:
                            max_rows(gg + 1)
                        values(gg, TT - 1)
                    for p in range(PG):
                        spread(NG - 1, p)
                    pe.wait_ge(S["oT"], PG * NG)
                    pe.wait_ge(S["oT_norm"], PG * NG)
                    for t in range(TT):
                        for c in range(INNER1 // P):
                            last = nc.tensor.matmul(bank[4 + t // 2][:, (t % 2) * D:(t % 2 + 1) * D],
                                                    oT[:, c, t * P:(t + 1) * P], wo[:, c, :],
                                                    start=(c == 0), stop=(c == INNER1 // P - 1))
                        if t % 2:
                            last.then_inc(S["y_filled"], 1)
                    norm.tensor(nc, pe, 1)
                    mlp_tensor(nc, pe, S, bank, norm.hT, w1, w2, g, 2 * DC)

            nc.all_engine_barrier(sems_to_clear=S.range)


def mask_rows(nc, io):
    with ExitStack() as ctx:
        sb = lambda n, s, d: ctx.enter_context(nc.sbuf_tensor(n, s, d))
        m8, v32 = sb("mask_u8", [B, T], U8), sb("mask_f32", [B, T], FP32)
        v16, bar = sb("mask_bf16", [B, T], BF16), sb("mask_bar", [B, T], BF16)
        s_in = ctx.enter_context(nc.semaphore("mask_in"))
        s_v = ctx.enter_context(nc.semaphore("mask_steps"))
        s_out = ctx.enter_context(nc.semaphore("mask_out"))
        with nc.Block() as block:

            @block.sync
            def _(sp):
                sp.dma_start(m8[:, :], io["mask"]).then_inc(s_in, 16)
                sp.wait_ge(s_v, 3)
                sp.dma_start(io["valid"], v32[:, :]).then_inc(s_out, 16)
                sp.dma_start(io["valid16"], v16[:, :]).then_inc(s_out, 16)
                sp.dma_start(io["bar16"], bar[:, :]).then_inc(s_out, 16)
                sp.wait_ge(s_out, 48)

            @block.vector
            def _(dve):
                dve.wait_ge(s_in, 16)
                nc.vector.tensor_copy(v32[:, :], m8[:, :]).then_inc(s_v, 1)
                nc.vector.tensor_copy(v16[:, :], m8[:, :]).then_inc(s_v, 1)
                nc.vector.tensor_scalar(bar[:, :], m8[:, :], 1.0, 1e9, ALU.subtract, ALU.mult).then_inc(s_v, 1)
    nc.all_engine_barrier()


def mamba_layer(nc, consts, io, tag, mod0, eps):
    ident, ones, mod, x = consts["ident"], consts["ones"], consts["mod"], consts["x"]
    shift1, scale1, gate1, shift2, scale2, gate2 = (k * DC for k in range(6))
    n_mod = 6 * DC
    PAD = TAPS - 1
    UNITS = IC * UB * NB
    SLOTS = 2 * NB
    XP_BANKS = (0, 1, 6, 7, 2, 3)
    RING = 3
    with ExitStack() as ctx:
        def sb(name, shape, dt, where=ctx):
            return where.enter_context(nc.sbuf_tensor(f"{tag}_{name}", shape, dt))

        win = sb("win", [P, DC, 2 * DI], FP32)
        x_dt = sb("xproj_dt", [P, IC, P], FP32)
        x_b4 = sb("xproj_b", [P, IC, DPU, NS], FP32)
        x_c4 = sb("xproj_c", [P, IC, DPU, NS], FP32)
        dtw = sb("dtw", [P, DI], FP32)
        wout = sb("wout", [P, IC, D], FP32)
        w1, w2 = sb("w1", [P, DC, HID], FP32), sb("w2", [P, DC, HID], FP32)
        w3 = sb("w3", [P, HC, D], FP32)
        cw = sb("conv_w", [P, IC, TAPS], FP32)
        cb, dtb, dp = (sb(n, [P, IC], FP32) for n in ("conv_b", "dtb", "dp"))
        a_log = sb("a_log", [P, UNITS], FP32)
        a_neg = sb("a_neg", [P, UNITS], FP32)
        spread = sb("spread", [SPLIT * NS, UB, P], BF16)
        gather = sb("gather", [P, UB * NS], FP32)
        cur = sb("cur", [P, n_mod], FP32)
        sz = sb("silu_z", [P, IC, T], FP32)
        xs = sb("xs", [P, IC, 2, T], FP32)
        b_rep, c_rep = sb("b_rep", [P, 2, T], FP32), sb("c_rep", [P, 2, T], FP32)
        y = sb("y", [P, T], FP32)
        S = Semaphores(consts["pool"], LN_SEMS + [
            "cur", "gate_diag", "gate_filled", "gate_rows", "pads", "in_filled", "in_taken", "tap0", "taps", "xs",
            "xp_filled", "xp", "dt_filled", "abs", "exp_abs", "ln", "relu", "dt", "dtx", "part1", "rest",
            "part2", "part3", "parts_out0", "parts_out1", "parts_out2", "parts_out3", "stacks", "scan_pads", "e_filled", "x_filled",
            "decay", "bx", "scan", "hc", "y_sum", "combine", "y_filled", "res", "up1_filled", "up2_filled", "silu",
            "prod", "down_filled"])
        s_w, s_i, s_p, s_a = consts["init_sems"]
        psum = ctx.enter_context(nc.psum_tensor(f"{tag}_psum", [P, 8, T], FP32))
        bank = [psum[:, n, :] for n in range(8)]
        dt_psum = psum[:, 0:2, :]
        x_psum = lambda i: psum[:, 2 * (i % 2) + 2:2 * (i % 2) + 4, :]
        y_psum = psum[:, 6:8, :]
        scratch = nc.dram_tensor(f"{tag}_parts_dram", (IC, SPLIT, P, 2, 2, T), BF16, kind="Internal").ap()
        gate_rows = sb("gate_rows", [P, 2, D], FP32)
        with ExitStack() as early:
            sb_early = lambda name, shape, dt: sb(name, shape, dt, early)
            norm = Norm(sb_early, S, lambda b: x[:, bass.ds(b, 1), :, :].rearrange("p b t d -> p (b t) d"), cur, ident,
                        consts["half"], bank, eps)
            gates = Gates(sb_early, S, cur, ident, ones, bank[7], [gate1, gate2], gate_rows)
            tmp = sb("res_tmp", [P, 2, 2, D], FP32, early)
            hid = sb("hid", [P, HC, T], FP32, early)
            xp = sb("x_padded", [P, IC, T + 2 * PAD], FP32, early)
            dtl = sb("dt_low", [P, 2, T], FP32, early)
            lg = sb("softplus", [P, IC, 2, T], FP32, early)
            dd = sb("dt_and_dtx", [P, 2, 2, 2, T], FP32, early)
            parts = sb("parts", [P, 2, SPLIT, 2, 2, T], BF16, early)
        stack = sb("stack", [SPLIT * NS, 2, NB, 2, 2, T], BF16)
        decay = sb("decay", [P, RING, 2, T + 1], FP32)
        bx = sb("bx", [P, RING, 2, T + 1], FP32)
        h = sb("h", [P, RING, 2, T + 1], FP32)
        hc = sb("hc", [P, SLOTS, 2, T], FP32)

        with nc.Block() as block:

            @block.sync
            def _(sp):
                n = 0
                for to, of in ((win, "win"), (wout, "wout"), (w1, "w1"), (w2, "w2"), (w3, "w3")):
                    sp.dma_start(to[:, :, :], io[tag + of].rearrange("(c p) n -> p c n", p=P)).then_inc(s_w, 16)
                    n += 1
                xpv = io[tag + "xp"].rearrange("(c p) n -> p c n", p=P)
                for r in range(DPU):
                    sp.dma_start(x_b4[:, :, r, :], xpv[:, :, DTR:DTR + NS]).then_inc(s_w, 16)
                    sp.dma_start(x_c4[:, :, r, :], xpv[:, :, DTR + NS:DTR + 2 * NS]).then_inc(s_w, 16)
                    n += 2
                sp.dma_start(cw[:, :, :], io[tag + "conv_w"].rearrange("(c p) k -> p c k", p=P)).then_inc(s_w, 16)
                for to, of in ((cb, "conv_b"), (dtb, "dtb"), (dp, "dp")):
                    sp.dma_start(to[:, :], io[tag + of]).then_inc(s_w, 16)
                sp.wait_ge(s_i, 2)
                sp.dma_start(x_dt[:, :, 0:DTR], xpv[:, :, 0:DTR]).then_inc(s_w, 16)
                sp.dma_start(dtw[0:DTR, :], io[tag + "dtw"]).then_inc(s_w, 16)
                sp.wait_ge(s_w, 16 * (n + 6))

            @block.vector
            def _(dve):
                nc.vector.memset(x_dt[:, :, :], 0.0).then_inc(s_i, 1)
                nc.vector.memset(dtw[:, :], 0.0).then_inc(s_i, 1)
                nc.vector.memset(gather[:, :], 0.0).then_inc(s_i, 1)
                dve.wait_ge(s_i, 3)
                for a in range(DPU):
                    nc.vector.memset(gather[NS * a:NS * (a + 1), a::NS + DPU], 1.0).then_inc(s_i, 1)
                dve.wait_ge(s_a, 17)
                nc.vector.tensor_scalar(a_neg[:, :], a_neg[:, :], -1.0, None, ALU.mult).then_inc(s_i, 1)

            @block.scalar
            def _(act):
                act.dma_start(a_log[:, :], io[tag + "alog"]).then_inc(s_a, 16)
                act.wait_ge(s_a, 16)
                nc.scalar.activation(a_neg[:, :], a_log[:, :], ACT.Exp).then_inc(s_a, 1)

            @block.gpsimd
            def _(pool):
                nc.gpsimd.memset(spread[:, :, :], 0.0).then_inc(s_p, 1)
                view = spread[:, :, :].rearrange("p u (a n) -> p u a n", a=DPU)
                for j in range(SPLIT):
                    pool.wait_ge(s_p, j + 1)
                    nc.gpsimd.affine_select(out=view, in_=view, compare_op=ALU.not_equal, fill=1.0, base=-NS * j,
                                            pattern=[[-DPU, UB], [-1, DPU], [0, NS]],
                                            channel_multiplier=1).then_inc(s_p, 1)

        nc.all_engine_barrier(sems_to_clear=range(s_w.num, s_a.num + 1))

        with nc.Fori(0, B) as b:
            x_of_b = x[:, bass.ds(b, 1), :, :].rearrange("p b t d -> p (b t) d")
            with nc.Block() as block:

                @block.sync
                def _(sp):
                    def parts_out(c):
                        sp.wait_ge(S["part3"], c + 1)
                        sp.dma_start(scratch[c].rearrange("s p q w t -> p s (q w t)"),
                                     parts[:, c % 2, :, :, :, :].rearrange("p s q w t -> p s (q w t)"))\
                            .then_inc(S[f"parts_out{c}"], 16)

                    parts_out(0)
                    parts_out(1)
                    for c in range(IC):
                        sp.wait_ge(S[f"parts_out{c}"], 16)
                        if c >= 2:
                            sp.wait_ge(S["x_filled"], UB * NB * (c - 1))
                        for j in range(SPLIT):
                            sp.dma_start(stack[NS * j:NS * (j + 1), c % 2, :, :, :, :]
                                         .rearrange("d k q w t -> d k (q w t)"),
                                         scratch[c, j].rearrange("(k d) q w t -> d k (q w t)", d=NS))\
                                .then_inc(S["stacks"], 16)
                        sp.wait_ge(S["stacks"], 16 * SPLIT * (c + 1))
                        if c + 2 < IC:
                            parts_out(c + 2)

                @block.gpsimd
                def _(pool):
                    nc.gpsimd.memset(xp[:, :, 0:PAD], 0.0).then_inc(S["pads"], 1)
                    pool.wait_ge(S["pads"], 1)
                    nc.gpsimd.memset(xp[:, :, PAD + T:], 0.0).then_inc(S["pads"], 1)
                    pool.wait_ge(S["pads"], 2)
                    norm.gpsimd(nc, pool, 0)
                    pool.wait_ge(S["part3"], IC)
                    nc.gpsimd.memset(decay[:, :, :, T:], 0.0).then_inc(S["scan_pads"], 1)
                    nc.gpsimd.memset(bx[:, :, :, T:], 0.0).then_inc(S["scan_pads"], 1)
                    for i in range(UNITS):
                        pool.wait_ge(S["scan"], i + 1)
                        if i >= SLOTS:
                            pool.wait_ge(S["y_sum"], 2 * (i // NB - 1))
                        nc.gpsimd.tensor_tensor(hc[:, i % SLOTS, :, :], h[:, i % RING, :, 0:T], c_rep[:, :, :],
                                                ALU.mult).then_inc(S["hc"], 1)
                    norm.gpsimd(nc, pool, 1)

                @block.vector
                def _(dve):
                    nc.vector.tensor_copy(cur[:, :], mod[:, bass.ds(b, 1), mod0:mod0 + n_mod]
                                          .rearrange("p b m -> p (b m)")).then_inc(S["cur"], 1)
                    norm.vector(nc, dve, b, 0)
                    dve.wait_ge(S["cur"], 1)
                    gates.vector(nc, dve)
                    dve.wait_ge(S["pads"], 2)
                    for c in range(IC):
                        for j in range(1, TAPS):
                            for w in range(2):
                                if j == 1:
                                    dve.wait_ge(S["tap0"], 2 * c + w + 1)
                                else:
                                    dve.wait_ge(S["taps"], 2 * ((TAPS - 1) * c + j - 2) + w + 1)
                                src = xp[:, c, j:j + T] if w == 0 else xp[:, c, T + 2 * PAD - 1 - j:2 * PAD - 1 - j:-1]
                                nc.vector.scalar_tensor_tensor(xs[:, c, w, :], src, cw[:, c, j:j + 1], xs[:, c, w, :],
                                                               ALU.mult, ALU.add).then_inc(S["taps"], 1)

                    def dt_and_dtx(c):
                        dve.wait_ge(S["abs"], c + 1)
                        if c >= 2:
                            dve.wait_ge(S["part3"], c - 1)
                        nc.vector.tensor_scalar(dd[:, c % 2, 0, :, :], psum[:, 2 * c:2 * c + 2, :], dtb[:, c:c + 1],
                                                0.0, ALU.add, ALU.max).then_inc(S["relu"], 1)
                        dve.wait_ge(S["ln"], c + 1)
                        dve.wait_ge(S["relu"], c + 1)
                        nc.vector.tensor_tensor(dd[:, c % 2, 0, :, :], dd[:, c % 2, 0, :, :], lg[:, c, :, :],
                                                ALU.add).then_inc(S["dt"], 1)
                        dve.wait_ge(S["dt"], c + 1)
                        nc.vector.tensor_tensor(dd[:, c % 2, 1, :, :], dd[:, c % 2, 0, :, :], xs[:, c, :, :],
                                                ALU.mult).then_inc(S["dtx"], 1)

                    def rest(c):
                        dve.wait_ge(S["part1"], c + 1)
                        nc.vector.tensor_tensor(dd[:, c % 2, :, :, :], dd[:, c % 2, :, :, :],
                                                parts[:, c % 2, 0, :, :, :], ALU.subtract).then_inc(S["rest"], 1)

                    def part3(c):
                        dve.wait_ge(S["part2"], c + 1)
                        nc.vector.tensor_tensor(parts[:, c % 2, 2, :, :, :], dd[:, c % 2, :, :, :],
                                                parts[:, c % 2, 1, :, :, :], ALU.subtract).then_inc(S["part3"], 1)

                    dt_and_dtx(0)
                    dt_and_dtx(1)
                    for c in range(0, IC, 2):
                        rest(c)
                        rest(c + 1)
                        for k in (c, c + 1):
                            part3(k)
                            if k + 2 < IC:
                                dt_and_dtx(k + 2)
                    dve.wait_ge(S["xp"], 6)

                    def scan_unit(i):
                        dve.wait_ge(S["decay"], i + 1)
                        dve.wait_ge(S["bx"], i + 1)
                        if i >= RING:
                            dve.wait_ge(S["hc"], i - RING + 1)
                        if i == 0:
                            for k in range(IC):
                                dve.wait_ge(S[f"parts_out{k}"], 16)
                        both = lambda ring: ring[:, i % RING, :, :].rearrange("p w t -> p (w t)")
                        nc.vector.tensor_tensor_scan(both(h), both(decay), both(bx), 0.0,
                                                     ALU.mult, ALU.add).then_inc(S["scan"], 1)

                    def combine(c):
                        dve.wait_ge(S["y_sum"], 2 * UB * (c + 1))
                        steps = (
                            lambda: nc.vector.scalar_tensor_tensor(y[:, :], xs[:, c, 0, :], dp[:, c:c + 1], y_psum[:, 0, :],
                                                                   ALU.mult, ALU.add),
                            lambda: nc.vector.scalar_tensor_tensor(y[:, :], xs[:, c, 1, ::-1], dp[:, c:c + 1], y[:, :],
                                                                   ALU.mult, ALU.add),
                            lambda: nc.vector.tensor_tensor(y[:, :], y_psum[:, 1, ::-1], y[:, :], ALU.add),
                            lambda: nc.vector.tensor_tensor(sz[:, c, :], y[:, :], sz[:, c, :], ALU.mult))
                        for k, step in enumerate(steps):
                            if c or k:
                                dve.wait_ge(S["combine"], len(steps) * c + k)
                            step().then_inc(S["combine"], 1)

                    per_chunk = UB * NB
                    dve.wait_ge(S["scan_pads"], 2)
                    for i in range(UNITS + 1):
                        if i < UNITS:
                            dve.wait_ge(S["x_filled"], i + 1)
                            if i >= RING:
                                dve.wait_ge(S["scan"], i - RING + 1)
                            nc.vector.tensor_tensor(bx[:, i % RING, :, 0:T], x_psum(i), b_rep[:, :, :],
                                                    ALU.mult).then_inc(S["bx"], 1)
                        if i:
                            scan_unit(i - 1)
                        if i > per_chunk and i % per_chunk == 5:
                            combine(i // per_chunk - 1)
                    combine(IC - 1)
                    dve.wait_ge(S["gate_rows"], 1)
                    residual(nc, dve, S, bank[0:2], None, gates.rows[:, 0, :], tmp, x_of_b, 0, "y_filled")
                    norm.vector(nc, dve, b, 1)
                    for j in range(HC):
                        dve.wait_ge(S["silu"], j + 1)
                        dve.wait_ge(S["up2_filled"], j + 1)
                        nc.vector.tensor_tensor(hid[:, j, :], hid[:, j, :], bank[5 + j], ALU.mult)\
                            .then_inc(S["prod"], 1)
                    residual(nc, dve, S, bank[0:2], None, gates.rows[:, 1, :], tmp, x_of_b, 1, "down_filled")

                @block.scalar
                def _(act):
                    act.wait_ge(S["cur"], 1)
                    norm.scalar(nc, act, 0, scale1, shift1)
                    gates.scalar(nc, act)
                    act.wait_ge(S["pads"], 2)
                    for c in range(IC):
                        act.wait_ge(S["in_filled"], c + 1)
                        nc.scalar.activation(xp[:, c, PAD:PAD + T], bank[2 + c], ACT.Copy).then_inc(S["in_taken"], 1)
                        act.wait_ge(S["in_taken"], c + 1)
                        for w in range(2):
                            src = xp[:, c, 0:T] if w == 0 else xp[:, c, T + 2 * PAD - 1:2 * PAD - 1:-1]
                            nc.scalar.activation(xs[:, c, w, :], src, ACT.Identity, bias=cb[:, c:c + 1],
                                                 scale=cw[:, c, 0:1]).then_inc(S["tap0"], 1)
                    for c in range(IC):
                        act.wait_ge(S["in_filled"], IC + c + 1)
                        nc.scalar.activation(sz[:, c, :], bank[2 + c], ACT.Silu).then_inc(S["in_taken"], 1)
                        for w in range(2):
                            act.wait_ge(S["taps"], 2 * ((TAPS - 1) * c + TAPS - 2) + w + 1)
                            nc.scalar.activation(xs[:, c, w, :], xs[:, c, w, :], ACT.Silu).then_inc(S["xs"], 1)
                    for n, to in enumerate((dtl, dtl, b_rep, b_rep, c_rep, c_rep)):
                        act.wait_ge(S["xp_filled"], n + 1)
                        nc.scalar.activation(to[:, n % 2, :], bank[XP_BANKS[n]], ACT.Copy).then_inc(S["xp"], 1)
                    for c in range(IC):
                        act.wait_ge(S["dt_filled"], c + 1)
                        nc.scalar.activation(lg[:, c, :, :], psum[:, 2 * c:2 * c + 2, :], ACT.Abs,
                                             bias=dtb[:, c:c + 1]).then_inc(S["abs"], 1)
                    for c in range(IC):
                        act.wait_ge(S["abs"], c + 1)
                        nc.scalar.activation(lg[:, c, :, :], lg[:, c, :, :], ACT.Exp, scale=-1.0)\
                            .then_inc(S["exp_abs"], 1)
                    for c in range(IC):
                        act.wait_ge(S["exp_abs"], c + 1)
                        nc.scalar.activation(lg[:, c, :, :], lg[:, c, :, :], ACT.Ln, bias=1.0).then_inc(S["ln"], 1)
                    for c0 in range(0, IC, 2):
                        for c in (c0, c0 + 1):
                            act.wait_ge(S["dtx"], c + 1)
                            if c >= 2:
                                act.wait_ge(S[f"parts_out{c - 2}"], 16)
                            nc.scalar.activation(parts[:, c % 2, 0, :, :, :], dd[:, c % 2, :, :, :], ACT.Copy)\
                                .then_inc(S["part1"], 1)
                        for c in (c0, c0 + 1):
                            act.wait_ge(S["rest"], c + 1)
                            nc.scalar.activation(parts[:, c % 2, 1, :, :, :], dd[:, c % 2, :, :, :], ACT.Copy)\
                                .then_inc(S["part2"], 1)
                    act.wait_ge(S["part3"], IC)
                    for i in range(UNITS):
                        unit = (i // (UB * NB)) * UB * NB + (i % NB) * UB + (i // NB) % UB
                        act.wait_ge(S["e_filled"], i + 1)
                        if i >= RING:
                            act.wait_ge(S["scan"], i - RING + 1)
                        nc.scalar.activation(decay[:, i % RING, :, 0:T], dt_psum, ACT.Exp, scale=a_neg[:, unit:unit + 1])\
                            .then_inc(S["decay"], 1)
                    norm.scalar(nc, act, 1, scale2, shift2)
                    for j in range(HC):
                        act.wait_ge(S["up1_filled"], j + 1)
                        nc.scalar.activation(hid[:, j, :], bank[2 + j], ACT.Silu).then_inc(S["silu"], 1)

                @block.tensor
                def _(pe):
                    norm.tensor(nc, pe, 0)
                    gates.tensor(nc, pe)
                    pe.wait_ge(S["hT"], DC)
                    for m in range(2 * IC):
                        if m >= 4:
                            pe.wait_ge(S["in_taken"], m - 3)
                        for c in range(DC):
                            last = nc.tensor.matmul(bank[2 + m % 4], win[:, c, m * P:(m + 1) * P], norm.hT[:, c, :],
                                                    start=(c == 0), stop=(c == DC - 1))
                        last.then_inc(S["in_filled"], 1)
                    pe.wait_ge(S["gate_rows"], 1)
                    for c in range(IC):
                        pe.wait_ge(S["xs"], 2 * (c + 1))
                        for n, w in enumerate((x_dt, x_dt, x_b4, x_b4, x_c4, x_c4)):
                            if c == 0 and XP_BANKS[n] in (2, 3):
                                pe.wait_ge(S["in_taken"], IC + XP_BANKS[n] - 1)
                            stat = w[:, c, :] if w is x_dt else w[:, c, :, :].rearrange("p a n -> p (a n)")
                            last = nc.tensor.matmul(bank[XP_BANKS[n]], stat, xs[:, c, n % 2, :],
                                                    start=(c == 0), stop=(c == IC - 1))
                            if c == IC - 1:
                                last.then_inc(S["xp_filled"], 1)
                    pe.wait_ge(S["xp"], 6)
                    pe.wait_ge(S["in_taken"], 2 * IC)
                    for c in range(IC):
                        for w in range(2):
                            last = nc.tensor.matmul(bank[2 * c + w], dtw[:, c * P:(c + 1) * P], dtl[:, w, :],
                                                    start=True, stop=True)
                        last.then_inc(S["dt_filled"], 1)
                    pe.wait_ge(S["relu"], IC)
                    pe.wait_ge(S["abs"], IC)

                    def y_sum(k, w):
                        c, u = k // UB, k % UB
                        if u == 0 and c:
                            pe.wait_ge(S["combine"], 4 * c)
                        pe.wait_ge(S["hc"], NB * (k + 1))
                        for j in range(NB):
                            last = nc.tensor.matmul(y_psum[NS * j:NS * (j + 1), w, :],
                                                    gather[:, NS * u:NS * (u + 1)],
                                                    hc[:, (NB * k + j) % SLOTS, w, :],
                                                    start=(u == 0), stop=(u == UB - 1))
                        last.then_inc(S["y_sum"], 1)

                    for i in range(UNITS):
                        c, u, j = i // (UB * NB), (i // NB) % UB, i % NB
                        if i % (UB * NB) == 0:
                            pe.wait_ge(S["stacks"], 16 * SPLIT * (c + 1))
                        if i:
                            pe.wait_ge(S["decay"], i)
                        for w in range(2):
                            last = nc.tensor.matmul(dt_psum[:, w, :], spread[:, u, :], stack[:, c % 2, j, 0, w, :],
                                                    start=True, stop=True)
                        last.then_inc(S["e_filled"], 1)
                        if i >= 2:
                            pe.wait_ge(S["bx"], i - 1)
                        for w in range(2):
                            last = nc.tensor.matmul(x_psum(i)[:, w, :], spread[:, u, :], stack[:, c % 2, j, 1, w, :],
                                                    start=True, stop=True)
                        last.then_inc(S["x_filled"], 1)
                        if i % 2 and i > NB + 2:
                            y_sum((i - 3) // NB - 1, (i - 3) % NB // 2)
                    for i in range(UNITS + 1, UNITS + 6, 2):
                        y_sum((i - 3) // NB - 1, (i - 3) % NB // 2)
                    pe.wait_ge(S["combine"], 4 * IC)
                    for t in range(TT):
                        for c in range(IC):
                            last = nc.tensor.matmul(bank[t // 2][:, (t % 2) * D:(t % 2 + 1) * D],
                                                    sz[:, c, t * P:(t + 1) * P], wout[:, c, :],
                                                    start=(c == 0), stop=(c == IC - 1))
                        if t % 2:
                            last.then_inc(S["y_filled"], 1)
                    norm.tensor(nc, pe, 1)
                    pe.wait_ge(S["hT"], 2 * DC)
                    for base, w, filled in ((2, w1, "up1_filled"), (5, w2, "up2_filled")):
                        for j in range(HC):
                            for c in range(DC):
                                last = nc.tensor.matmul(bank[base + j], w[:, c, j * P:(j + 1) * P], norm.hT[:, c, :],
                                                        start=(c == 0), stop=(c == DC - 1))
                            last.then_inc(S[filled], 1)
                    pe.wait_ge(S["prod"], HC)
                    for t in range(TT):
                        for j in range(HC):
                            last = nc.tensor.matmul(bank[t // 2][:, (t % 2) * D:(t % 2 + 1) * D],
                                                    hid[:, j, t * P:(t + 1) * P], w3[:, j, :],
                                                    start=(j == 0), stop=(j == HC - 1))
                        if t % 2:
                            last.then_inc(S["down_filled"], 1)

            nc.all_engine_barrier(sems_to_clear=S.range)


_INPUTS = {
    "x": lambda a: a["x"],
    "condT": lambda a: a["cond_1024"].T,
    "mask": lambda a: a["mask_BxS_bk1"],
    "mod_w": lambda a: _join(1, a["L0_cond_Wln1"], a["L0_cond_Wln2"], a["L1_cond_W_mod"], a["L2_cond_ada_w"].T,
                             a["L3_cond_adaln1_W"], a["L3_cond_adaln2_W"]),
    "mod_b": lambda a: _columns(_join(0, a["L0_cond_bln1"], a["L0_cond_bln2"], a["L1_cond_b_mod"], a["L2_cond_ada_b"],
                                      a["L3_cond_adaln1_b"], a["L3_cond_adaln2_b"])),
    "norm_w": lambda a: _columns(_join(0, a["L3_cond_norm1_w"], a["L3_cond_norm2_w"])),
    "norm_b": lambda a: _columns(_join(0, a["L3_cond_norm1_b"], a["L3_cond_norm2_b"])),
    "l0_wq": lambda a: a["L0_cond_Wq"], "l0_wk": lambda a: a["L0_cond_Wk"], "l0_wv": lambda a: a["L0_cond_Wv"],
    "l0_wo": lambda a: a["L0_cond_Wo"], "l0_w1": lambda a: a["L0_cond_W1"], "l0_w2": lambda a: a["L0_cond_W2"],
    "l0_bq": lambda a: _columns(a["L0_cond_bq"]), "l0_bk": lambda a: _columns(a["L0_cond_bk"]), "l0_bv": lambda a: a["L0_cond_bv"],
    "l0_bo": lambda a: a["L0_cond_bo"], "l0_b1": lambda a: _columns(a["L0_cond_b1"]), "l0_b2": lambda a: a["L0_cond_b2"],
    "l1_wq": lambda a: a["L1_cond_W_qkv"][:, 0:INNER1], "l1_wk": lambda a: a["L1_cond_W_qkv"][:, INNER1:2 * INNER1],
    "l1_wv": lambda a: a["L1_cond_W_qkv"][:, 2 * INNER1:], "l1_wo": lambda a: a["L1_cond_W_out"],
    "l1_bo": lambda a: a["L1_cond_b_out"], "l1_w1": lambda a: a["L1_cond_W1"], "l1_b1": lambda a: _columns(a["L1_cond_b1"]),
    "l1_w2": lambda a: a["L1_cond_W2"], "l1_b2": lambda a: a["L1_cond_b2"],
    "l2_wq": lambda a: a["L2_cond_qkv_w"][0:D].T, "l2_wk": lambda a: a["L2_cond_qkv_w"][D:2 * D].T,
    "l2_wv": lambda a: a["L2_cond_qkv_w"][2 * D:].T, "l2_wo": lambda a: a["L2_cond_proj_w"].T,
    "l2_w1": lambda a: a["L2_cond_fc1_w"].T, "l2_w2": lambda a: a["L2_cond_fc2_w"].T,
    "l2_bq": lambda a: _columns(a["L2_cond_qkv_b"][0:D]), "l2_bk": lambda a: _columns(a["L2_cond_qkv_b"][D:2 * D]),
    "l2_bv": lambda a: a["L2_cond_qkv_b"][2 * D:], "l2_bo": lambda a: a["L2_cond_proj_b"],
    "l2_b1": lambda a: _columns(a["L2_cond_fc1_b"]), "l2_b2": lambda a: a["L2_cond_fc2_b"],
    "l3_win": lambda a: a["L3_cond_in_proj_W"], "l3_conv_w": lambda a: a["L3_cond_conv_w"].reshape(DI, TAPS),
    "l3_conv_b": lambda a: _columns(a["L3_cond_conv_b"]), "l3_xp": lambda a: a["L3_cond_x_proj_W"],
    "l3_dtw": lambda a: a["L3_cond_dt_proj_W"], "l3_dtb": lambda a: _columns(a["L3_cond_dt_proj_b"]),
    "l3_alog": lambda a: _columns(a["L3_cond_A_log"]), "l3_dp": lambda a: _columns(a["L3_cond_Dp"]),
    "l3_wout": lambda a: a["L3_cond_out_proj_W"], "l3_w1": lambda a: a["L3_cond_w1"],
    "l3_w2": lambda a: a["L3_cond_w2"], "l3_w3": lambda a: a["L3_cond_w3"],
}


def _columns(v):
    return v.reshape(-1, P).T


def _join(axis, *arrays):
    import numpy as np
    return np.concatenate(arrays, axis=axis)


LAYERS = 4
BODY_SEMS = 56


def program(nc, io, out):
    for name, dt in (("valid", FP32), ("valid16", BF16), ("bar16", BF16)):
        io[name] = nc.dram_tensor(f"{name}_dram", (B, T), dt, kind="Internal").ap()
    with ExitStack() as ctx:
        sb = lambda n, s, d: ctx.enter_context(nc.sbuf_tensor(n, s, d))
        consts = {"x": sb("x_sb", [P, B, TT, D], FP32), "ident": sb("ident", [P, P], FP32),
                  "ones": sb("ones", [P, P], FP32), "mod": sb("mod", [P, B, MODS], FP32),
                  "half": sb("minus_half", [P, TT], FP32)}
        consts["init_sems"] = [ctx.enter_context(nc.semaphore(n)) for n in ("weights", "init", "init_sel", "init_a")]
        consts["pool"] = [ctx.enter_context(nc.semaphore(f"body{n}")) for n in range(BODY_SEMS)]
        modulation(nc, consts, io)
        if LAYERS >= 1:
            narrow_attention_layer(nc, consts, io, "l0_", MOD0, 1e-5, masked=False)
        if LAYERS >= 2:
            wide_attention_layer(nc, consts, io, "l1_", MOD1, 1e-5)
        if LAYERS >= 3:
            mask_rows(nc, io)
            narrow_attention_layer(nc, consts, io, "l2_", MOD2, 1e-6, masked=True)
        if LAYERS >= 4:
            mamba_layer(nc, consts, io, "l3_", MOD3, 1e-5)
        store(nc, consts, out)


def store(nc, consts, out):
    s_out = nc.alloc_semaphore("out")
    with nc.Block() as block:

        @block.sync
        def _(sp):
            sp.dma_start(out.rearrange("b (t p) d -> p (b t) d", p=P),
                         consts["x"][:, :, :, :].rearrange("p b t d -> p (b t) d")).then_inc(s_out, 16)
            sp.wait_ge(s_out, 16)


def kernel(**inputs):
    import numpy as np
    import concourse.bacc as bacc
    from concourse.bass_utils import run_bass_kernel_spmd

    nc = bacc.Bacc("TRN2", target_bir_lowering=False, num_devices=1)
    given = {k: np.asarray(v) for k, v in inputs.items()}
    arrays, io = {}, {}
    for name, lay in _INPUTS.items():
        a = np.ascontiguousarray(lay(given))
        arrays[f"in_{name}"] = a
        io[name] = nc.dram_tensor(f"in_{name}", a.shape, mybir.dt.from_np(a.dtype), kind="ExternalInput").ap()
    out = nc.dram_tensor("out_x", (B, T, D), FP32, kind="ExternalOutput").ap()
    program(nc, io, out)
    r = run_bass_kernel_spmd(nc, [arrays], core_ids=[0])
    return r.results[0]["out_x"]
```

```python
import concourse.bass as bass
from concourse import mybir
from contextlib import ExitStack

FP32 = mybir.dt.float32
FP32R = mybir.dt.float32r
BF16 = mybir.dt.bfloat16
U8 = mybir.dt.uint8
ALU = mybir.AluOpType
ACT = mybir.ActivationFunctionType
AX = mybir.AxisListType

P = 128
B, T, D = 8, 512, 256
TT = T // P
DC = D // P
H = 16
GH = 4
NG = H // GH
MLP = 4 * D
MC = MLP // P
SPLIT = 3
Q_PART = (0, 0, 1, 1, 0, 2)
K_PART = (0, 1, 0, 1, 2, 0)
HD = 16
STACK = HD * len(Q_PART)
HD1 = 64
INNER1 = H * HD1
DI = 2 * D
IC = DI // P
NS = 32
DTR = D // 16
DPU = P // NS
UB = NS // DPU
NB = P // NS
TAPS = 4
HID = (int(2 / 3 * 2 * D) + 63) // 64 * 64
HC = HID // P

MOD0, MOD1, MOD2, MOD3 = 0, 4 * DC, 10 * DC, 16 * DC
MODS = 22 * DC


class Semaphores:

    def __init__(self, pool, names):
        assert len(set(names)) == len(names) <= len(pool)
        self.range = range(pool[0].num, pool[0].num + len(pool))
        assert [s.num for s in pool] == list(self.range)
        self.of = dict(zip(names, pool))

    def __getitem__(self, name):
        return self.of[name]


LN_SEMS = ["cur_ahead", "stats", "aggr", "var_eps", "rstd", "xn", "hT_filled", "hT"]


class Norm:

    def __init__(self, sb, S, ident, half, eps):
        self.S, self.ident, self.half, self.eps = S, ident, half, eps
        self.st = sb("ln_stats", [P, 2, TT, 6], FP32)
        self.mv = sb("ln_mean_var", [P, 2, TT, 2], FP32)
        self.ve = sb("ln_var_eps", [P, 2, TT], FP32)
        self.rs = sb("ln_rstd", [P, 2, TT], FP32)
        self.xn = sb("ln_xn", [P, TT, D], FP32)

    def vector(self, nc, dve, x, n):
        S = self.S
        for t in range(TT):
            nc.vector.bn_stats(self.st[:, n, t, :], x[:, t, :]).then_inc(S["stats"], 1)
        dve.wait_ge(S["stats"], TT * (n + 1))
        for t in range(TT):
            nc.vector.bn_aggr(self.mv[:, n, t, :], self.st[:, n, t, :]).then_inc(S["aggr"], 1)
        dve.wait_ge(S["rstd"], n + 1)
        if n:
            dve.wait_ge(S["hT_filled"], DC * n)
        for t in range(TT):
            nc.vector.tensor_scalar(self.xn[:, t, :], x[:, t, :], self.mv[:, n, t, 0:1], self.rs[:, n, t:t + 1],
                                    ALU.subtract, ALU.mult).then_inc(S["xn"], 1)

    def gpsimd(self, nc, pool, n):
        S = self.S
        pool.wait_ge(S["aggr"], TT * (n + 1))
        nc.gpsimd.tensor_scalar(self.ve[:, n, :], self.mv[:, n, :, 1], self.eps, None, ALU.add)\
            .then_inc(S["var_eps"], 1)
        pool.wait_ge(S["var_eps"], n + 1)
        nc.gpsimd.tensor_tensor(self.rs[:, n, :], self.ve[:, n, :], self.half[:, :], ALU.pow).then_inc(S["rstd"], 1)

    def tensor(self, nc, pe, n, banks):
        S = self.S
        pe.wait_ge(S["xn"], TT * (n + 1))
        for c in range(DC):
            for t in range(TT):
                last = nc.tensor.transpose(banks[c][:, t * P:(t + 1) * P], self.xn[:, t, c * P:(c + 1) * P],
                                           self.ident[:, :])
            last.then_inc(S["hT_filled"], 1)

    def scalar(self, nc, act, n, banks, hT, cur, scale, shift):
        S = self.S
        for c in range(DC):
            act.wait_ge(S["hT_filled"], DC * n + c + 1)
            nc.scalar.activation(hT[:, c, :], banks[c], ACT.Identity, bias=cur[:, shift + c:shift + c + 1],
                                 scale=cur[:, scale + c:scale + c + 1]).then_inc(S["hT"], 1)


class NormAhead:

    def __init__(self, norm, consts, sb, hT, mod0, n_mod, scale, shift):
        self.norm, self.x, self.mod, self.hT = norm, consts["x"], consts["mod"], hT
        self.mod0, self.n_mod, self.scale, self.shift = mod0, n_mod, scale, shift
        self.cur = sb("cur_ahead", [P, n_mod], FP32)

    def vector(self, nc, dve, b, n):
        nc.vector.tensor_copy(self.cur[:, :], self.mod[:, bass.ds(b, 1), self.mod0:self.mod0 + self.n_mod]
                              .rearrange("p b m -> p (b m)")).then_inc(self.norm.S["cur_ahead"], 1)
        self.norm.vector(nc, dve, self.x[:, bass.ds(b, 1), :, :].rearrange("p b t d -> p (b t) d"), n)

    def scalar(self, nc, act, n, banks):
        act.wait_ge(self.norm.S["cur_ahead"], 1)
        self.norm.scalar(nc, act, n, banks, self.hT, self.cur, self.scale, self.shift)

    def first(self, nc, banks):
        with nc.Block() as block:

            @block.gpsimd
            def _(pool):
                self.norm.gpsimd(nc, pool, 0)

            @block.vector
            def _(dve):
                self.vector(nc, dve, 0, 0)

            @block.scalar
            def _(act):
                self.scalar(nc, act, 0, banks)

            @block.tensor
            def _(pe):
                self.norm.tensor(nc, pe, 0, banks)

        nc.all_engine_barrier(sems_to_clear=self.norm.S.range)


class Gates:

    def __init__(self, sb, S, cur, ident, ones, bank, columns, rows=None):
        self.S, self.cur, self.ident, self.ones, self.bank, self.columns = S, cur, ident, ones, bank, columns
        self.diag = sb("gate_diag", [P, len(columns), D], FP32)
        self.rows = sb("gate_rows", [P, len(columns), D], FP32) if rows is None else rows

    def vector(self, nc, dve):
        for k, column in enumerate(self.columns):
            for c in range(DC):
                nc.vector.tensor_scalar(self.diag[:, k, c * P:(c + 1) * P], self.ident[:, :],
                                        self.cur[:, column + c:column + c + 1], None,
                                        ALU.mult).then_inc(self.S["gate_diag"], 1)

    def tensor(self, nc, pe):
        pe.wait_ge(self.S["gate_diag"], DC * len(self.columns))
        for k in range(len(self.columns)):
            last = nc.tensor.matmul(self.bank[:, k * D:(k + 1) * D], self.ones[:, :], self.diag[:, k, :],
                                    start=True, stop=True)
        last.then_inc(self.S["gate_filled"], 1)

    def scalar(self, nc, act):
        act.wait_ge(self.S["gate_filled"], 1)
        nc.scalar.activation(self.rows[:, :, :].rearrange("p k n -> p (k n)"), self.bank[:, 0:len(self.columns) * D],
                             ACT.Copy).then_inc(self.S["gate_rows"], 1)


def residual(nc, dve, S, banks, bias, gate, tmp, x_b, n, filled):
    steps = (bias is not None) + (gate is not None) + 1
    for k in range(2):
        done = 2 * steps * n + steps * k
        dve.wait_ge(S[filled], k + 1)
        y = banks[k] if len(banks[k].shape) == 3 else banks[k].rearrange("p (t n) -> p t n", t=2)
        over = lambda row: row.unsqueeze(1).broadcast_to([P, 2, D])
        rows = [(row, op) for row, op in ((bias, ALU.add), (gate, ALU.mult)) if row is not None]
        for n_row, (row, op) in enumerate(rows):
            nc.vector.tensor_tensor(tmp[:, k, :, :], tmp[:, k, :, :] if n_row else y, over(row), op)\
                .then_inc(S["res"], 1)
            dve.wait_ge(S["res"], done + n_row + 1)
        x = x_b[:, 2 * k:2 * k + 2, :]
        nc.vector.tensor_tensor(x, x, tmp[:, k, :, :], ALU.add).then_inc(S["res"], 1)
    dve.wait_ge(S["res"], 2 * steps * (n + 1))


AHEAD_AT = 5


def mlp_tensor(nc, pe, S, banks, hT, w1, w2, g, norm, ahead=None):
    pe.wait_ge(S["hT"], DC)
    for j in range(MC):
        if j >= 4:
            pe.wait_ge(S["gelu"], j - 3)
        for c in range(DC):
            last = nc.tensor.matmul(banks[2 + j % 4], w1[:, c, j * P:(j + 1) * P], hT[:, c, :],
                                    start=(c == 0), stop=(c == DC - 1))
        last.then_inc(S["up_filled"], 1)
        if j + 1 == AHEAD_AT:
            norm.tensor(nc, pe, 1, banks[0:DC])
    if ahead is not None:
        pe.wait_ge(S["gelu"], MC)
        pe.wait_ge(S["hT"], 2 * DC)
        ahead()
    pe.wait_ge(S["gelu"], MC)
    for t in range(TT):
        for j in range(MC):
            last = nc.tensor.matmul(banks[6 + t // 2][:, (t % 2) * D:(t % 2 + 1) * D], g[:, j, t * P:(t + 1) * P],
                                    w2[:, j, :], start=(j == 0), stop=(j == MC - 1))
        if t % 2:
            last.then_inc(S["down_filled"], 1)


def mlp_scalar(nc, act, S, banks, b1, g, func, ahead):
    for j in range(MC):
        act.wait_ge(S["up_filled"], j + 1)
        nc.scalar.activation(g[:, j, :], banks[2 + j % 4], func, bias=b1[:, j:j + 1]).then_inc(S["gelu"], 1)
        if j + 1 == AHEAD_AT:
            ahead()


def modulation(nc, consts, io):
    ident, ones, mod = consts["ident"], consts["ones"], consts["mod"]
    with ExitStack() as ctx:
        sb = lambda n, s, d: ctx.enter_context(nc.sbuf_tensor(n, s, d))
        w = sb("mod_w", [P, DC, MODS * P], FP32)
        bias = sb("mod_bias", [P, MODS], FP32)
        nw = sb("mod_norm_w", [P, 2 * DC], FP32)
        nb = sb("mod_norm_b", [P, 2 * DC], FP32)
        cT = sb("mod_cT", [P, DC, B], FP32)
        scT = sb("mod_silu_cT", [P, DC, B], FP32)
        acc = ctx.enter_context(nc.psum_tensor("mod_acc", [P, MODS, B], FP32))
        s_in = ctx.enter_context(nc.semaphore("mod_in"))
        s_w = [ctx.enter_context(nc.semaphore(f"mod_w{n}")) for n in range(2)]
        s_x = ctx.enter_context(nc.semaphore("mod_x"))
        s_sc = ctx.enter_context(nc.semaphore("mod_silu"))
        s_mm = ctx.enter_context(nc.semaphore("mod_filled"))
        s_v = ctx.enter_context(nc.semaphore("mod_steps"))
        s_c = ctx.enter_context(nc.semaphore("mod_consts"))
        half_cols = MODS // 2 * P
        with nc.Block() as block:

            @block.sync
            def _(sp):
                sp.dma_start(cT[:, :, :], io["condT"].rearrange("(c p) b -> p c b", p=P)).then_inc(s_in, 16)
                sp.dma_start(bias[:, :], io["mod_b"]).then_inc(s_in, 16)
                sp.dma_start(nw[:, :], io["norm_w"]).then_inc(s_in, 16)
                sp.dma_start(nb[:, :], io["norm_b"]).then_inc(s_in, 16)
                wv = io["mod_w"].rearrange("(c p) n -> p c n", p=P)
                for n in range(2):
                    sp.dma_start(w[:, :, n * half_cols:(n + 1) * half_cols],
                                 wv[:, :, n * half_cols:(n + 1) * half_cols]).then_inc(s_w[n], 16)
                sp.dma_start(consts["x"][:, :, :, :].rearrange("p b t d -> p (b t) d"),
                             io["x"].rearrange("b (t p) d -> p (b t) d", p=P)).then_inc(s_x, 16)
                sp.wait_ge(s_x, 16)

            @block.gpsimd
            def _(pool):
                nc.gpsimd.memset(ident[:, :], 0.0).then_inc(s_c, 1)
                pool.wait_ge(s_c, 1)
                nc.gpsimd.affine_select(out=ident[:, :], in_=ident[:, :], compare_op=ALU.not_equal, fill=1.0,
                                        base=0, pattern=[[-1, P]], channel_multiplier=1).then_inc(s_c, 1)
                nc.gpsimd.memset(ones[:, :], 1.0).then_inc(s_c, 1)
                nc.gpsimd.memset(consts["half"][:, :], -0.5).then_inc(s_c, 1)

            @block.scalar
            def _(act):
                act.wait_ge(s_in, 64)
                nc.scalar.activation(scT[:, :, :], cT[:, :, :], ACT.Silu).then_inc(s_sc, 1)

            @block.tensor
            def _(pe):
                pe.wait_ge(s_in, 64)
                pe.wait_ge(s_sc, 1)
                for m in range(MODS):
                    if m % (MODS // 2) == 0:
                        pe.wait_ge(s_w[m // (MODS // 2)], 16)
                    c_in = cT if m < MOD1 else scT
                    for c in range(DC):
                        last = nc.tensor.matmul(acc[:, m, :], w[:, c, m * P:(m + 1) * P], c_in[:, c, :],
                                                start=(c == 0), stop=(c == DC - 1))
                last.then_inc(s_mm, 1)

            @block.vector
            def _(dve):
                dve.wait_ge(s_mm, 1)
                done = [0]

                def step(instruction):
                    instruction.then_inc(s_v, 1)
                    done[0] += 1

                step(nc.vector.tensor_tensor(mod[:, :, :].rearrange("p b m -> p m b"), acc[:, :, :],
                                             bias[:, :].unsqueeze(2).broadcast_to([P, MODS, B]), ALU.add))
                dve.wait_ge(s_v, done[0])
                scales = [MOD0, MOD0 + 2 * DC] + [m + k * DC for m in (MOD1, MOD2, MOD3) for k in (1, 4)]
                for col in scales:
                    step(nc.vector.tensor_scalar(mod[:, :, col:col + DC], mod[:, :, col:col + DC], 1.0, None, ALU.add))
                dve.wait_ge(s_v, done[0])
                for k in range(2):
                    for c in range(DC):
                        sh, sc = MOD3 + 3 * k * DC + c, MOD3 + (3 * k + 1) * DC + c
                        n = k * DC + c
                        step(nc.vector.scalar_tensor_tensor(mod[:, :, sh], mod[:, :, sc], nb[:, n:n + 1],
                                                            mod[:, :, sh], ALU.mult, ALU.add))
                        dve.wait_ge(s_v, done[0])
                        step(nc.vector.tensor_scalar(mod[:, :, sc], mod[:, :, sc], nw[:, n:n + 1], None, ALU.mult))
    nc.all_engine_barrier()


def narrow_attention_layer(nc, consts, io, tag, mod0, eps, masked):
    ident, ones, mod = consts["ident"], consts["ones"], consts["mod"]
    x = consts["x"]
    gated = masked
    k_max = STACK + (1 if masked else 0)
    k_all = k_max + 2
    if masked:
        scale1, shift1, gate1, scale2, shift2, gate2 = DC, 0, 2 * DC, 4 * DC, 3 * DC, 5 * DC
    else:
        scale1, shift1, gate1, scale2, shift2, gate2 = 0, DC, None, 2 * DC, 3 * DC, None
    n_mod = 6 * DC if gated else 4 * DC
    TILES = H * TT
    GT = GH * TT
    LEAD = 24
    SLOTS = 3 * GH
    CH = H // DC
    SUMS_AT = LEAD + (NG - 1) * GT + 8
    SPREADS_AT = (SUMS_AT + 6, SUMS_AT + 8, SUMS_AT + 11)
    with ExitStack() as ctx:
        def sb(name, shape, dt):
            return ctx.enter_context(nc.sbuf_tensor(f"{tag}_{name}", shape, dt))

        wq, wk, wv = (sb(f"w{n}", [P, DC, D], FP32) for n in "qkv")
        wo = sb("wo", [P, NG, D], FP32)
        w1 = sb("w1", [P, DC, MLP], FP32)
        w2 = sb("w2", [P, MC, D], FP32)
        bqk = sb("bqk", [P, 2 * DC], FP32)
        bv, bo, b2 = (sb(n, [P, D], FP32) for n in ("bv", "bo", "b2"))
        b1 = sb("b1", [P, MC], FP32)
        cur = sb("cur", [P, n_mod], FP32)
        qk = sb("qk", [P, 2 * DC, T], FP32)
        parts = sb("parts", [P, 2 * DC, SPLIT, T], BF16)
        qs = sb("q_stack", [k_all, H, T], BF16)
        ks = sb("k_stack", [k_all, H, T], BF16)
        va = sb("v_and_ones", [P, TT, H, 2 * HD], FP32)
        mx = sb("row_max", [P, NG, TT, GH], FP32)
        mrow = sb("max_rows", [GH, 2, T], BF16)
        probs = sb("probs", [P, SLOTS, T], FP32)
        oT = sb("oT", [P, NG, T], FP32)
        rec, rec_last = sb("rec", [P, T], FP32), sb("rec_last", [P, T], FP32)
        sel_sum = sb("sel_sum", [P, NG, H], FP32)
        sel_head = sb("sel_head", [P, NG, P], FP32)
        g = sb("g", [P, MC, T], FP32)
        tmp = sb("res_tmp", [P, 2, 2, D], FP32)
        pm = sb("q_valid", [P, T], FP32) if masked else None
        scratch = nc.dram_tensor(f"{tag}_parts_dram", (DC, 2, P, SPLIT, T), BF16, kind="Internal").ap()
        psum = ctx.enter_context(nc.psum_tensor(f"{tag}_psum", [P, 8, T], FP32))
        bank = [psum[:, n, :] for n in range(8)]
        RING0, SOLO = 4, LEAD - 4
        max_bank = lambda n: bank[n % RING0] if n < SOLO else bank[n % 2]
        pair = lambda n: psum[:, 2 + 2 * (n // 2 % 2):4 + 2 * (n // 2 % 2), :]
        S = Semaphores(consts["pool"], LN_SEMS + [
            "cur", "gate_diag", "gate_filled", "gate_rows", "qk_filled", "v_filled", "qk", "part1", "rest", "part2",
            "part3", "v", "parts_out0", "parts_out1", "parts_out2", "parts_out3", "stacks0", "stacks1", "valid_in", "mask_in", "max_filled", "max_taken",
            "maxT_filled", "max_part1", "max_part2", "max_rows", "st_filled", "exp", "av", "oT", "sum_filled", "rec",
            "head_filled", "oT_norm", "y_filled", "res", "up_filled", "gelu", "down_filled"])
        s_w, s_i, s_p, s_a = consts["init_sems"]
        norm = Norm(sb, S, ident, consts["half"], eps)
        hT, hT_mlp = sb("hT", [P, DC, T], FP32), sb("hT_mlp", [P, DC, T], FP32)
        ahead = NormAhead(norm, consts, sb, hT, mod0, n_mod, scale1, shift1)
        gates = Gates(sb, S, cur, ident, ones, bank[0], [gate1, gate2]) if gated else None

        with nc.Block() as block:

            @block.sync
            def _(sp):
                n = 0
                for to, of in ((wq, "wq"), (wk, "wk"), (wv, "wv"), (w1, "w1"), (w2, "w2")):
                    sp.dma_start(to[:, :, :], io[tag + of].rearrange("(c p) n -> p c n", p=P)).then_inc(s_w, 16)
                    n += 1
                for to, of in ((bv, "bv"), (bo, "bo"), (b2, "b2")):
                    sp.dma_start(to[:, :], io[tag + of].unsqueeze(0).broadcast_to([P, D])).then_inc(s_w, 16)
                    n += 1
                sp.dma_start(b1[:, :], io[tag + "b1"]).then_inc(s_w, 16)
                sp.dma_start(bqk[:, 0:DC], io[tag + "bq"]).then_inc(s_w, 16)
                sp.dma_start(bqk[:, DC:2 * DC], io[tag + "bk"]).then_inc(s_w, 16)
                sp.wait_ge(s_i, 1)
                wo_v = io[tag + "wo"].rearrange("(g j d) n -> j d g n", j=GH, d=HD)
                for j in range(GH):
                    sp.dma_start(wo[j * 2 * HD:j * 2 * HD + HD, :, :], wo_v[j]).then_inc(s_w, 16)
                sp.wait_ge(s_w, 16 * (n + 3 + GH))

            @block.vector
            def _(dve):
                nc.vector.memset(wo[:, :, :], 0.0).then_inc(s_i, 1)
                nc.vector.memset(rec[:, :], 0.0).then_inc(s_i, 1)
                nc.vector.memset(rec_last[:, :], 0.0).then_inc(s_i, 1)
                nc.vector.memset(va[:, :, :, HD:2 * HD], 1.0).then_inc(s_i, 1)
                nc.vector.memset(ks[STACK:k_all, :, :], 1.0).then_inc(s_i, 1)

            @block.gpsimd
            def _(pool):
                nc.gpsimd.memset(sel_sum[:, :, :], 0.0).then_inc(s_p, 1)
                nc.gpsimd.memset(sel_head[:, :, :], 0.0).then_inc(s_p, 1)
                pool.wait_ge(s_p, 2)
                for gg in range(NG):
                    nc.gpsimd.affine_select(
                        out=sel_sum[:, gg, gg * GH:(gg + 1) * GH], in_=sel_sum[:, gg, gg * GH:(gg + 1) * GH],
                        compare_op=ALU.not_equal, fill=1.0, base=-HD, pattern=[[-2 * HD, GH]], channel_multiplier=1)
                    nc.gpsimd.affine_select(
                        out=sel_head[:, gg, :].rearrange("p (j r) -> p j r", j=GH),
                        in_=sel_head[:, gg, :].rearrange("p (j r) -> p j r", j=GH),
                        compare_op=ALU.not_equal, fill=1.0, base=-gg * GH, pattern=[[-1, GH], [0, 2 * HD]],
                        channel_multiplier=1)

        nc.all_engine_barrier(sems_to_clear=range(s_w.num, s_a.num + 1))

        def valid_sync(sp, b):
            if masked:
                sp.dma_start(pm[:, :], io["valid"][bass.ds(b, 1), :].broadcast_to([P, T])).then_inc(S["valid_in"], 16)

        def qkv_sync(sp, b):
            for m in range(2 * DC):
                sp.wait_ge(S["part3"], m + 1)
                if masked and m == 0:
                    row = lambda a: a[bass.ds(b, 1), :].unsqueeze(1).broadcast_to([1, H, T])
                    sp.dma_start(qs[STACK:STACK + 1, :, :], row(io["valid16"])).then_inc(S["mask_in"], 16)
                    sp.dma_start(ks[STACK:STACK + 1, :, :], row(io["bar16"])).then_inc(S["mask_in"], 16)
                sp.dma_start(scratch[m // 2, m % 2, :, :, :], parts[:, m, :, :])\
                    .then_inc(S[f"parts_out{m}"], 16)
                if m % 2:
                    c = m // 2
                    for which, stack, part in ((0, qs, Q_PART), (1, ks, K_PART)):
                        sp.wait_ge(S[f"parts_out{2 * c + which}"], 16)
                        for s, p_ in enumerate(part):
                            of = scratch[c, which, :, p_, :].rearrange("(h d) t -> d h t", d=HD)
                            sp.dma_start(stack[s * HD:(s + 1) * HD, c * CH:(c + 1) * CH, :], of)\
                                .then_inc(S[f"stacks{c}"], 16)
            if masked:
                sp.wait_ge(S["mask_in"], 32)
            for c in range(DC):
                sp.wait_ge(S[f"stacks{c}"], 16 * 2 * len(Q_PART))

        def qkv_vector(dve):
            if masked:
                dve.wait_ge(S["valid_in"], 16)
            for c in range(DC):
                for m in (2 * c, 2 * c + 1):
                    dve.wait_ge(S["qk_filled"], m + 1)
                    b_col = bqk[:, (m % 2) * DC + c:(m % 2) * DC + c + 1]
                    if masked and m % 2 == 0:
                        nc.vector.scalar_tensor_tensor(qk[:, m, :], bank[2 + m], b_col, pm[:, :],
                                                       ALU.add, ALU.mult).then_inc(S["qk"], 1)
                    else:
                        nc.vector.tensor_scalar(qk[:, m, :], bank[2 + m], b_col, None,
                                                ALU.add).then_inc(S["qk"], 1)
                for m in (2 * c, 2 * c + 1):
                    dve.wait_ge(S["part1"], m + 1)
                    nc.vector.tensor_tensor(qk[:, m, :], qk[:, m, :], parts[:, m, 0, :],
                                            ALU.subtract).then_inc(S["rest"], 1)
                for m in (2 * c, 2 * c + 1):
                    dve.wait_ge(S["part2"], m + 1)
                    nc.vector.tensor_tensor(parts[:, m, 2, :], qk[:, m, :], parts[:, m, 1, :],
                                            ALU.subtract).then_inc(S["part3"], 1)
            for k in range(2):
                dve.wait_ge(S["v_filled"], k + 1)
                nc.vector.tensor_tensor(
                    va[:, 2 * k:2 * k + 2, :, 0:HD],
                    bank[k].rearrange("p (t h d) -> p t h d", t=2, h=H),
                    bv[:, :].rearrange("p (h d) -> p h d", h=H).unsqueeze(1).broadcast_to([P, 2, H, HD]),
                    ALU.add).then_inc(S["v"], 1)

        def qkv_scalar(act):
            for c in range(DC):
                for m in (2 * c, 2 * c + 1):
                    act.wait_ge(S["qk"], m + 1)
                    nc.scalar.activation(parts[:, m, 0, :], qk[:, m, :], ACT.Copy).then_inc(S["part1"], 1)
                for m in (2 * c, 2 * c + 1):
                    act.wait_ge(S["rest"], m + 1)
                    nc.scalar.activation(parts[:, m, 1, :], qk[:, m, :], ACT.Copy).then_inc(S["part2"], 1)

        def qkv_tensor(pe):
            for m in range(2 * DC):
                w = (wq, wk)[m % 2]
                for c in range(DC):
                    last = nc.tensor.matmul(bank[2 + m], w[:, c, m // 2 * P:(m // 2 + 1) * P],
                                            hT[:, c, :], start=(c == 0), stop=(c == DC - 1))
                last.then_inc(S["qk_filled"], 1)
            for t in range(TT):
                for c in range(DC):
                    last = nc.tensor.matmul(bank[t // 2][:, (t % 2) * D:(t % 2 + 1) * D],
                                            hT[:, c, t * P:(t + 1) * P], wv[:, c, :],
                                            start=(c == 0), stop=(c == DC - 1))
                if t % 2:
                    last.then_inc(S["v_filled"], 1)

        ahead.first(nc, bank[0:DC])
        with nc.Block() as block:

            @block.sync
            def _(sp):
                valid_sync(sp, 0)
                qkv_sync(sp, 0)

            @block.vector
            def _(dve):
                qkv_vector(dve)

            @block.scalar
            def _(act):
                qkv_scalar(act)

            @block.tensor
            def _(pe):
                qkv_tensor(pe)

        nc.all_engine_barrier(sems_to_clear=S.range)

        with nc.Fori(0, B) as b:
            nxt = (b + 1) % B
            x_b = x[:, bass.ds(b, 1), :, :].rearrange("p b t d -> p (b t) d")
            with nc.Block() as block:

                @block.sync
                def _(sp):
                    valid_sync(sp, nxt)
                    for gg in range(NG):
                        sp.wait_ge(S["max_part2"], gg + 1)
                        for k in range(2):
                            sp.dma_start(qs[k_max + k:k_max + k + 1, gg * GH:(gg + 1) * GH, :],
                                         mrow[:, k, :]).then_inc(S["max_rows"], 16)
                        sp.wait_ge(S["max_rows"], 32 * (gg + 1))
                    qkv_sync(sp, nxt)

                @block.gpsimd
                def _(pool):
                    norm.gpsimd(nc, pool, 0)
                    norm.gpsimd(nc, pool, 1)

                @block.vector
                def _(dve):
                    nc.vector.tensor_copy(cur[:, :], mod[:, bass.ds(b, 1), mod0:mod0 + n_mod]
                                          .rearrange("p b m -> p (b m)")).then_inc(S["cur"], 1)
                    if gated:
                        dve.wait_ge(S["cur"], 1)
                        gates.vector(nc, dve)
                    def take_max(n):
                        dve.wait_ge(S["max_filled"], n + 1)
                        h, t = n // TT, n % TT
                        nc.vector.tensor_reduce(mx[:, h // GH, t, h % GH:h % GH + 1], max_bank(n), AX.X,
                                                ALU.max)\
                            .then_inc(S["max_taken"], 1)

                    def max_rows(gg):
                        dve.wait_ge(S["maxT_filled"], gg + 1)
                        if gg:
                            dve.wait_ge(S["max_rows"], 32 * gg)
                        nc.vector.tensor_scalar(mrow[:, 0, :], bank[6][0:GH, :], -1.0, None,
                                                ALU.mult).then_inc(S["max_part1"], 1)
                        dve.wait_ge(S["max_part1"], gg + 1)
                        nc.vector.scalar_tensor_tensor(mrow[:, 1, :], bank[6][0:GH, :], -1.0, mrow[:, 0, :],
                                                       ALU.mult, ALU.subtract).then_inc(S["max_part2"], 1)

                    def normalise(gg):
                        dve.wait_ge(S["oT"], gg + 1)
                        dve.wait_ge(S["head_filled"], gg + 1)
                        nc.vector.tensor_tensor(oT[:, gg, :], oT[:, gg, :], bank[gg % 2],
                                                ALU.mult).then_inc(S["oT_norm"], 1)

                    for n in range(TILES + 2 * GT + LEAD):
                        if n < TILES:
                            take_max(n)
                        if n % GT == 3 and GT < n < TILES + GT:
                            max_rows(n // GT - 1)
                        gg, at = divmod(n - LEAD - GT - 6, GT)
                        if at == 0 and 0 <= gg < NG:
                            dve.wait_ge(S["av"], TT * (gg + 1))
                            nc.vector.tensor_copy(oT[:, gg, :], bank[7]).then_inc(S["oT"], 1)
                            if gg == NG - 2:
                                dve.wait_ge(S["sum_filled"], 1)
                                nc.vector.reciprocal(rec[0:H - GH, :], bank[6][0:H - GH, :]).then_inc(S["rec"], 1)
                                for done in range(NG - 1):
                                    normalise(done)
                    dve.wait_ge(S["sum_filled"], 2)
                    nc.vector.reciprocal(rec_last[0:GH, :], bank[6][0:GH, :]).then_inc(S["rec"], 1)
                    normalise(NG - 1)
                    if gated:
                        dve.wait_ge(S["gate_rows"], 1)
                    residual(nc, dve, S, [psum[:, 2:4, 0:D], psum[:, 4:6, 0:D]], bo[:, :], gates.rows[:, 0, :] if gated else None, tmp, x_b, 0,
                             "y_filled")
                    norm.vector(nc, dve, x_b, 0)
                    ahead.vector(nc, dve, nxt, 1)
                    qkv_vector(dve)
                    residual(nc, dve, S, bank[6:8], b2[:, :], gates.rows[:, 1, :] if gated else None, tmp, x_b, 1,
                             "down_filled")

                @block.scalar
                def _(act):
                    if gated:
                        gates.scalar(nc, act)
                    for n in range(0, TILES, 2):
                        act.wait_ge(S["st_filled"], n // 2 + 1)
                        if n >= SLOTS:
                            act.wait_ge(S["av"], (n - SLOTS) // GH + 1)
                        nc.scalar.activation(probs[:, n % SLOTS:n % SLOTS + 2, :], pair(n), ACT.Exp,
                                             scale=float(HD) ** -0.5).then_inc(S["exp"], 1)
                    act.wait_ge(S["cur"], 1)
                    norm.scalar(nc, act, 0, bank[0:DC], hT_mlp, cur, scale2, shift2)
                    mlp_scalar(nc, act, S, bank, b1, g, ACT.Gelu_apprx_tanh if masked else ACT.Gelu,
                               lambda: ahead.scalar(nc, act, 1, bank[0:DC]))
                    qkv_scalar(act)

                @block.tensor
                def _(pe):
                    def scores(n):
                        h, t = n // TT, n % TT
                        if n >= SOLO:
                            pe.wait_ge(S["max_taken"], n - 1)
                        elif n >= RING0:
                            pe.wait_ge(S["max_taken"], n - RING0 + 1)
                        nc.tensor.matmul(max_bank(n), qs[0:k_max, h, t * P:(t + 1) * P], ks[0:k_max, h, :],
                                         start=True, stop=True).then_inc(S["max_filled"], 1)

                    def max_rows(gg):
                        pe.wait_ge(S["max_taken"], GT * (gg + 1))
                        if gg:
                            pe.wait_ge(S["max_part2"], gg)
                        for t in range(TT):
                            last = nc.tensor.transpose(bank[6][0:GH, t * P:(t + 1) * P], mx[:, gg, t, :], ident[:, :])
                        last.then_inc(S["maxT_filled"], 1)

                    def scores_T(n):
                        if n == 0:
                            pe.wait_ge(S["max_taken"], SOLO)
                        if n % GT == 0:
                            pe.wait_ge(S["max_rows"], 32 * (n // GT + 1))
                        if n >= 4:
                            pe.wait_ge(S["exp"], n // 2 - 1)
                        for i in range(2):
                            gg, k, j = n // GT, n // GH % TT, n % GH + i
                            last = nc.tensor.matmul(pair(n)[:, i, :], ks[0:k_all, gg * GH + j, k * P:(k + 1) * P],
                                                    qs[0:k_all, gg * GH + j, :], start=True, stop=True)
                        last.then_inc(S["st_filled"], 1)

                    def values(q):
                        gg, k = q // TT, q % TT
                        if k == 0 and gg:
                            pe.wait_ge(S["oT"], gg)
                        pe.wait_ge(S["exp"], 2 * (q + 1))
                        for j in range(GH):
                            last = nc.tensor.matmul(bank[7][2 * HD * j:2 * HD * (j + 1), :],
                                                    va[:, k, gg * GH + j, :], probs[:, (GH * q + j) % SLOTS, :],
                                                    start=(k == 0), stop=(k == TT - 1))
                        last.then_inc(S["av"], 1)

                    def sums():
                        pe.wait_ge(S["oT"], NG - 1)
                        pe.wait_ge(S["max_part2"], NG)
                        for gg in range(NG - 1):
                            last = nc.tensor.matmul(bank[6][0:H - GH, :], sel_sum[:, gg, 0:H - GH], oT[:, gg, :],
                                                    start=(gg == 0), stop=(gg == NG - 2))
                        last.then_inc(S["sum_filled"], 1)

                    def spread(gg):
                        pe.wait_ge(S["rec"], 1)
                        if gg >= 2:
                            pe.wait_ge(S["oT_norm"], gg - 1)
                        else:
                            pe.wait_ge(S["max_taken"], TILES)
                        nc.tensor.matmul(bank[gg % 2], sel_head[:, gg, :], rec[:, :], start=True, stop=True)\
                            .then_inc(S["head_filled"], 1)

                    if gated:
                        gates.tensor(nc, pe)
                        pe.wait_ge(S["gate_rows"], 1)
                    for n in range(TILES + GT + LEAD):
                        if n < TILES:
                            scores(n)
                        if n % GT == 2 and GT < n < TILES + GT:
                            max_rows(n // GT - 1)
                        m = n - LEAD - 1
                        if m >= 0 and m % 2 == 0 and m < TILES:
                            scores_T(m)
                        if n == SUMS_AT:
                            sums()
                        if n in SPREADS_AT:
                            spread(SPREADS_AT.index(n))
                        if m > GH and m % GH == 3 and m < TILES + GH:
                            values(m // GH - 1)
                    def project_out(t, groups):
                        for gg in groups:
                            last = nc.tensor.matmul(psum[:, 2 + t, 0:D], oT[:, gg, t * P:(t + 1) * P], wo[:, gg, :],
                                                    start=(gg == 0), stop=(gg == NG - 1))
                        return last

                    pe.wait_ge(S["exp"], TILES // 2)
                    pe.wait_ge(S["oT_norm"], NG - 1)
                    project_out(0, range(NG - 1))
                    pe.wait_ge(S["oT"], NG)
                    pe.wait_ge(S["rec"], 1)
                    nc.tensor.matmul(bank[6][0:GH, :], sel_sum[:, 0, 0:GH], oT[:, NG - 1, :],
                                     start=True, stop=True).then_inc(S["sum_filled"], 1)
                    for t in range(1, TT):
                        project_out(t, range(NG - 1))
                    pe.wait_ge(S["rec"], 2)
                    nc.tensor.matmul(bank[(NG - 1) % 2], sel_head[:, 0, :], rec_last[:, :],
                                     start=True, stop=True).then_inc(S["head_filled"], 1)
                    pe.wait_ge(S["oT_norm"], NG)
                    for t in range(TT):
                        last = project_out(t, (NG - 1,))
                        if t % 2:
                            last.then_inc(S["y_filled"], 1)
                    norm.tensor(nc, pe, 0, bank[0:DC])
                    mlp_tensor(nc, pe, S, bank, hT_mlp, w1, w2, g, norm, lambda: qkv_tensor(pe))

            nc.all_engine_barrier(sems_to_clear=S.range)


def wide_attention_layer(nc, consts, io, tag, mod0, eps):
    ident, ones, mod, x = consts["ident"], consts["ones"], consts["mod"], consts["x"]
    shift1, scale1, gate1, shift2, scale2, gate2 = (k * DC for k in range(6))
    n_mod = 6 * DC
    PG = GH // 2
    TILES = H * TT
    GT = GH * TT
    SLOTS = 2 * GH
    PROJ = 2 * PG + 2
    PRING = (7, 0, 1)
    PROJ_AT = ((0, 1, 2), (3,), (4,), (5,))
    SCORES_AT, AT_ONCE, MAX_AT, SPREAD_AT = 4, 2, 12, (7, 9)
    GW = GH * HD1
    with ExitStack() as ctx:
        def sb(name, shape, dt, where=ctx):
            return where.enter_context(nc.sbuf_tensor(f"{tag}_{name}", shape, dt))

        wq, wk, wv = (sb(f"w{n}", [P, DC, INNER1], FP32) for n in "qkv")
        wo = sb("wo", [P, INNER1 // P, D], FP32)
        w1 = sb("w1", [P, DC, MLP], FP32)
        w2 = sb("w2", [P, MC, D], FP32)
        bo, b2 = (sb(n, [P, D], FP32) for n in ("bo", "b2"))
        b1 = sb("b1", [P, MC], FP32)
        cur = sb("cur", [P, n_mod], FP32)
        q_max = sb("q_and_max", [P, 2, GH, T], FP32R)
        low_ones = sb("low_and_ones", [P, 2, GH, T], FP32R)
        heads_in = sb("heads_in", [P, 2, T], FP32)
        v = sb("v", [P, 2, TT, GW], FP32)
        mx = sb("row_max", [P, NG, TT, GH], FP32)
        mrow = sb("max_rows", [GH, 2, T], FP32R)
        mneg = sb("max_negated", [GH, T], FP32)
        oT = sb("oT", [P, INNER1 // P, T], FP32)
        rec = sb("rec", [P, T], FP32)
        sel = sb("sel_pair", [P, PG, P], FP32)
        hT = sb("ln_hT", [P, DC, T], FP32)
        gate_rows = sb("gate_rows", [P, 2, D], FP32)
        psum = ctx.enter_context(nc.psum_tensor(f"{tag}_psum", [P, 8, T], FP32))
        bank = [psum[:, n, :] for n in range(8)]
        S = Semaphores(consts["pool"], LN_SEMS + [
            "cur", "gate_diag", "gate_filled", "gate_rows", "proj_filled", "proj", "copied", "high", "low", "no_max",
            "max_filled", "max_taken", "maxT_filled", "max_neg", "max_high", "max_low", "max_rows", "st_filled", "exp",
            "sums", "av", "oT", "rec", "head_filled", "oT_norm", "y_filled", "res", "up_filled", "gelu", "down_filled"])
        s_w, s_i, s_p, s_a = consts["init_sems"]
        with ExitStack() as outside:
            sb_out = lambda name, shape, dt: sb(name, shape, dt, outside)
            norm = Norm(sb_out, S, ident, consts["half"], eps)
            hT_mlp = sb_out("hT_mlp", [P, DC, T], FP32)
            ahead = NormAhead(norm, consts, sb_out, hT, mod0, n_mod, scale1, shift1)
            gates = Gates(sb_out, S, cur, ident, ones, bank[2], [gate1, gate2], gate_rows)
            g = sb_out("g", [P, MC, T], FP32)
            tmp = sb_out("res_tmp", [P, 2, 2, D], FP32)
        probs = sb("probs", [P, SLOTS, T], FP32)
        q_low = sb("q_and_low", [P, 2, GH, T], FP32R)
        k_twice = sb("k_twice", [P, 2, GH, T], FP32R)
        full = lambda a: a.bitcast(FP32)
        FIRST = 4
        max_bank = lambda n: bank[n % FIRST] if n < GT else bank[n % 2]
        own = lambda j: slice(HD1 * (j % 2), HD1 * (j % 2) + HD1)
        other = lambda j: own(j + 1)
        aux = lambda j: HD1 * (1 - j % 2)

        with nc.Block() as block:

            @block.sync
            def _(sp):
                n = 0
                for to, of in ((wq, "wq"), (wk, "wk"), (wv, "wv"), (wo, "wo"), (w1, "w1"), (w2, "w2")):
                    sp.dma_start(to[:, :, :], io[tag + of].rearrange("(c p) n -> p c n", p=P)).then_inc(s_w, 16)
                    n += 1
                for to, of in ((bo, "bo"), (b2, "b2")):
                    sp.dma_start(to[:, :], io[tag + of].unsqueeze(0).broadcast_to([P, D])).then_inc(s_w, 16)
                    n += 1
                sp.dma_start(b1[:, :], io[tag + "b1"]).then_inc(s_w, 16)
                sp.wait_ge(s_w, 16 * (n + 1))

            @block.vector
            def _(dve):
                nc.vector.memset(full(q_max[:, :, :, :]), 0.0).then_inc(s_i, 1)
                nc.vector.memset(full(low_ones[:, :, :, :]), 0.0).then_inc(s_i, 1)
                dve.wait_ge(s_i, 2)
                for j in range(GH):
                    nc.vector.memset(full(low_ones[aux(j):aux(j) + 2, :, j, :]), 1.0).then_inc(s_i, 1)

            @block.gpsimd
            def _(pool):
                nc.gpsimd.memset(sel[:, :, :], 0.0).then_inc(s_p, 1)
                pool.wait_ge(s_p, 1)
                view = sel[:, :, :].rearrange("p q (a r) -> p q a r", a=2)
                nc.gpsimd.affine_select(out=view, in_=view, compare_op=ALU.not_equal, fill=1.0, base=0,
                                        pattern=[[-HD1, PG], [-HD1 // 2, 2], [0, HD1]], channel_multiplier=1)

        nc.all_engine_barrier(sems_to_clear=range(s_w.num, s_a.num + 1))

        ahead.first(nc, bank[0:DC])

        with nc.Fori(0, B) as b:
            nxt = (b + 1) % B
            x_b = x[:, bass.ds(b, 1), :, :].rearrange("p b t d -> p (b t) d")
            with nc.Block() as block:

                @block.sync
                def _(sp):
                    for gg in range(NG):
                        for k, ready in enumerate(("max_high", "max_low")):
                            sp.wait_ge(S[ready], gg + 1)
                            for j in range(GH):
                                sp.dma_start(full(q_max[aux(j) + k:aux(j) + k + 1, gg % 2, j, :]), full(mrow[j:j + 1, k, :]))\
                                    .then_inc(S["max_rows"], 16)
                        sp.wait_ge(S["max_rows"], 32 * GH * (gg + 1))

                @block.gpsimd
                def _(pool):
                    for gg in range(NG):
                        if gg >= 2:
                            pool.wait_ge(S["st_filled"], GH * TT * (gg - 1))
                        for j in range(GH):
                            if gg or j:
                                pool.wait_ge(S["no_max"], gg * GH + j)
                            nc.gpsimd.memset(full(q_max[aux(j):aux(j) + 2, gg % 2, j, :]), 0.0).then_inc(S["no_max"], 1)
                    norm.gpsimd(nc, pool, 0)
                    norm.gpsimd(nc, pool, 1)

                @block.vector
                def _(dve):
                    nc.vector.tensor_copy(cur[:, :], mod[:, bass.ds(b, 1), mod0:mod0 + n_mod]
                                          .rearrange("p b m -> p (b m)")).then_inc(S["cur"], 1)
                    dve.wait_ge(S["cur"], 1)
                    gates.vector(nc, dve)

                    def high_and_low(gg, m):
                        n, n_qk = gg * PROJ + m, gg * 2 * PG + m
                        dve.wait_ge(S["proj"], n + 1)
                        of = heads_in[:, n_qk % 2, :]
                        to_high = q_max if m < PG else k_twice
                        heads = (2 * (m % PG), 2 * (m % PG) + 1)
                        for j in heads:
                            nc.vector.tensor_copy(to_high[own(j), gg % 2, j, :], of[own(j), :])\
                                .then_inc(S["high"], 1)
                        dve.wait_ge(S["high"], 2 * (n_qk + 1))
                        for j in heads:
                            to_low = q_low[other(j), gg % 2, j, :] if m < PG else low_ones[own(j), gg % 2, j, :]
                            nc.vector.tensor_tensor(to_low, of[own(j), :], full(to_high[own(j), gg % 2, j, :]),
                                                    ALU.subtract).then_inc(S["low"], 1)

                    def take_max(n):
                        dve.wait_ge(S["max_filled"], n + 1)
                        h, t = n // TT, n % TT
                        nc.vector.tensor_reduce(mx[:, h // GH, t, h % GH:h % GH + 1], max_bank(n), AX.X,
                                                ALU.max).then_inc(S["max_taken"], 1)

                    def max_rows(gg):
                        dve.wait_ge(S["maxT_filled"], gg + 1)
                        if gg:
                            dve.wait_ge(S["max_rows"], 32 * GH * gg)
                        nc.vector.tensor_scalar(mneg[:, :], bank[7][0:GH, :], -1.0, None,
                                                ALU.mult).then_inc(S["max_neg"], 1)
                        dve.wait_ge(S["max_neg"], gg + 1)
                        nc.vector.tensor_copy(mrow[:, 0, :], mneg[:, :]).then_inc(S["max_high"], 1)
                        dve.wait_ge(S["max_high"], gg + 1)
                        nc.vector.tensor_tensor(mrow[:, 1, :], mneg[:, :], full(mrow[:, 0, :]),
                                                ALU.subtract).then_inc(S["max_low"], 1)

                    def reciprocal(gg):
                        dve.wait_ge(S["sums"], TT * (gg + 1))
                        nc.vector.reciprocal(rec[:, :], bank[6]).then_inc(S["rec"], 1)

                    def normalise(gg, p):
                        dve.wait_ge(S["head_filled"], PG * gg + p + 1)
                        dve.wait_ge(S["oT"], PG * gg + p + 1)
                        nc.vector.tensor_tensor(oT[:, PG * gg + p, :], oT[:, PG * gg + p, :], bank[7],
                                                ALU.mult).then_inc(S["oT_norm"], 1)

                    for m in range(2 * PG):
                        high_and_low(0, m)
                    for n in range(GT):
                        take_max(n)
                    max_rows(0)
                    for n in range(TILES):
                        gg, s = n // GT, n % GT
                        if gg + 1 < NG:
                            for m in PROJ_AT[s] if s < len(PROJ_AT) else ():
                                if m < 2 * PG:
                                    high_and_low(gg + 1, m)
                        if gg and s == 2:
                            reciprocal(gg - 1)
                        if gg + 1 < NG and s >= SCORES_AT:
                            for tile in range(AT_ONCE * (s - SCORES_AT), min(AT_ONCE * (s - SCORES_AT + 1), GT)):
                                take_max(GT * (gg + 1) + tile)
                        if gg and s - 1 in SPREAD_AT:
                            normalise(gg - 1, SPREAD_AT.index(s - 1))
                        if gg + 1 < NG and s == MAX_AT:
                            max_rows(gg + 1)
                    reciprocal(NG - 1)
                    for p in range(PG):
                        normalise(NG - 1, p)
                    dve.wait_ge(S["gate_rows"], 1)
                    residual(nc, dve, S, [psum[:, 0:2, 0:D], psum[:, 2:4, 0:D]], bo[:, :], gates.rows[:, 0, :], tmp, x_b, 0, "y_filled")
                    norm.vector(nc, dve, x_b, 0)
                    ahead.vector(nc, dve, nxt, 1)
                    residual(nc, dve, S, bank[6:8], b2[:, :], gates.rows[:, 1, :], tmp, x_b, 1, "down_filled")

                @block.scalar
                def _(act):
                    def projected(gg, m):
                        act.wait_ge(S["proj_filled"], gg * PROJ + m + 1)
                        src = bank[PRING[m % 3]]
                        if m < 2 * PG:
                            n_qk = gg * 2 * PG + m
                            if n_qk >= 2:
                                act.wait_ge(S["low"], 2 * (n_qk - 1))
                            nc.scalar.activation(heads_in[:, n_qk % 2, :], src, ACT.Copy).then_inc(S["proj"], 1)
                        else:
                            t = 2 * (m - 2 * PG)
                            nc.scalar.activation(v[:, gg % 2, t:t + 2, :].rearrange("p t n -> p (t n)"), src,
                                                 ACT.Copy).then_inc(S["proj"], 1)

                    def second_copies(gg, m):
                        if m < 2 * PG:
                            act.wait_ge(S["high"], 2 * (gg * 2 * PG + m + 1))
                            for j in (2 * (m % PG), 2 * (m % PG) + 1):
                                to, of = (q_low[own(j)], q_max) if m < PG else (k_twice[other(j)], k_twice)
                                nc.scalar.activation(to[:, gg % 2, j, :], of[own(j), gg % 2, j, :],
                                                     ACT.Copy).then_inc(S["copied"], 1)

                    def heads_out(gg):
                        act.wait_ge(S["av"], TT * (gg + 1))
                        for p in range(PG):
                            nc.scalar.activation(oT[:, PG * gg + p, :], bank[4 + p],
                                                 ACT.Copy).then_inc(S["oT"], 1)

                    for m in range(PROJ):
                        projected(0, m)
                        if m:
                            second_copies(0, m - 1)
                    gates.scalar(nc, act)
                    for n in range(TILES):
                        gg, s = n // GT, n % GT
                        projections = PROJ_AT[s] if gg + 1 < NG and s < len(PROJ_AT) else ()
                        if s == 0:
                            for m in projections:
                                projected(gg + 1, m)
                                second_copies(gg + 1, m)
                        if gg and s == 5:
                            heads_out(gg - 1)
                        act.wait_ge(S["st_filled"], n + 1)
                        if n >= SLOTS:
                            act.wait_ge(S["av"], (n - SLOTS) // GH + 1)
                        nc.scalar.activation(probs[:, n % SLOTS, :], bank[2 + n % 2], ACT.Exp,
                                             scale=float(HD1) ** -0.5).then_inc(S["exp"], 1)
                        if s:
                            for m in projections:
                                projected(gg + 1, m)
                                second_copies(gg + 1, m)
                    heads_out(NG - 1)
                    act.wait_ge(S["cur"], 1)
                    norm.scalar(nc, act, 0, bank[0:DC], hT_mlp, cur, scale2, shift2)
                    mlp_scalar(nc, act, S, bank, b1, g, ACT.Gelu, lambda: ahead.scalar(nc, act, 1, bank[0:DC]))

                @block.tensor
                def _(pe):

                    def project(gg, m):
                        if m == 0 and gg:
                            pe.wait_ge(S["max_neg"], gg)
                        if m == 1 and gg:
                            pe.wait_ge(S["max_taken"], GT * gg)
                        if m >= 3:
                            pe.wait_ge(S["proj"], gg * PROJ + m - 2)
                        to = bank[PRING[m % 3]]
                        if m < 2 * PG:
                            w, cols = (wq, wk)[m // PG], gg * GW + (m % PG) * P
                            for c in range(DC):
                                last = nc.tensor.matmul(to, w[:, c, cols:cols + P], hT[:, c, :],
                                                        start=(c == 0), stop=(c == DC - 1))
                        else:
                            for u in range(2):
                                t = 2 * (m - 2 * PG) + u
                                for c in range(DC):
                                    last = nc.tensor.matmul(to[:, u * GW:(u + 1) * GW],
                                                            hT[:, c, t * P:(t + 1) * P],
                                                            wv[:, c, gg * GW:(gg + 1) * GW],
                                                            start=(c == 0), stop=(c == DC - 1))
                        last.then_inc(S["proj_filled"], 1)

                    def scores(n):
                        h, t = n // TT, n % TT
                        gg, j = h // GH, h % GH
                        if n % GT == 0:
                            pe.wait_ge(S["copied"], 4 * PG * (gg + 1))
                            pe.wait_ge(S["proj"], PROJ * (gg + 1))
                            pe.wait_ge(S["low"], 4 * PG * (gg + 1))
                            pe.wait_ge(S["no_max"], GH * (gg + 1))
                        if n >= GT:
                            pe.wait_ge(S["max_taken"], n - 1)
                        elif n >= FIRST:
                            pe.wait_ge(S["max_taken"], n - FIRST + 1)
                        for i, (q_, k_) in enumerate(((q_low, k_twice), (q_max, low_ones))):
                            last = nc.tensor.matmul(max_bank(n), q_[:, gg % 2, j, t * P:(t + 1) * P],
                                                    k_[:, gg % 2, j, :], start=(i == 0), stop=(i == 1))
                        last.then_inc(S["max_filled"], 1)

                    def max_rows(gg):
                        pe.wait_ge(S["max_taken"], GT * (gg + 1))
                        if gg >= 2:
                            pe.wait_ge(S["oT_norm"], PG * (gg - 1))
                        for t in range(TT):
                            last = nc.tensor.transpose(bank[7][0:GH, t * P:(t + 1) * P], mx[:, gg, t, :], ident[:, :])
                        last.then_inc(S["maxT_filled"], 1)

                    def scores_T(n):
                        gg, k, j = n // GT, n // GH % TT, n % GH
                        if n % GT == 0:
                            pe.wait_ge(S["max_rows"], 32 * GH * (gg + 1))
                        if n >= 2:
                            pe.wait_ge(S["exp"], n - 1)
                        for i, (q_, k_) in enumerate(((q_low, k_twice), (q_max, low_ones))):
                            last = nc.tensor.matmul(bank[2 + n % 2], k_[:, gg % 2, j, k * P:(k + 1) * P],
                                                    q_[:, gg % 2, j, :], start=(i == 0), stop=(i == 1))
                        last.then_inc(S["st_filled"], 1)

                    def values(q, part):
                        gg, k = q // TT, q % TT
                        slot = lambda j: (q * GH + j) % SLOTS
                        if part == 0:
                            if k == 0 and gg:
                                pe.wait_ge(S["rec"], gg)
                            pe.wait_ge(S["exp"], GH * (q + 1))
                            for j in range(GH):
                                last = nc.tensor.matmul(bank[6][32 * j:32 * (j + 1), :], ones[:, 0:32],
                                                        probs[:, slot(j), :], start=(k == 0), stop=(k == TT - 1))
                            last.then_inc(S["sums"], 1)
                        else:
                            if k == 0 and gg and part == 1:
                                pe.wait_ge(S["oT"], PG * gg)
                            for j in (2 * (part - 1), 2 * (part - 1) + 1):
                                last = nc.tensor.matmul(bank[3 + part][own(j), :], v[:, gg % 2, k, j * HD1:(j + 1) * HD1],
                                                        probs[:, slot(j), :], start=(k == 0), stop=(k == TT - 1))
                            if part == PG:
                                last.then_inc(S["av"], 1)

                    def spread(gg, p):
                        pe.wait_ge(S["rec"], gg + 1)
                        if p == 0:
                            pe.wait_ge(S["proj"], PROJ * min(gg + 3, NG))
                        if p:
                            pe.wait_ge(S["oT_norm"], PG * gg + p)
                        nc.tensor.matmul(bank[7], sel[:, p, :], rec[:, :], start=True, stop=True)\
                            .then_inc(S["head_filled"], 1)

                    for m in range(PROJ):
                        project(0, m)
                    gates.tensor(nc, pe)
                    pe.wait_ge(S["gate_rows"], 1)
                    for n in range(GT):
                        scores(n)
                    max_rows(0)
                    for n in range(TILES):
                        gg, s = n // GT, n % GT
                        if gg + 1 < NG and s < len(PROJ_AT):
                            for m in PROJ_AT[s]:
                                project(gg + 1, m)
                        if gg + 1 < NG and s >= SCORES_AT:
                            for tile in range(AT_ONCE * (s - SCORES_AT), min(AT_ONCE * (s - SCORES_AT + 1), GT)):
                                scores(GT * (gg + 1) + tile)
                        if gg + 1 < NG and s == MAX_AT:
                            max_rows(gg + 1)
                        scores_T(n)
                        if gg and s in SPREAD_AT:
                            spread(gg - 1, SPREAD_AT.index(s))
                        for part in {1: (0,), 2: (1, 2)}.get(n % GH, ()) if n > GH else ():
                            values(n // GH - 1, part)
                    for part in range(PG + 1):
                        values(TILES // GH - 1, part)
                    def project_out(t, pairs):
                        for c in pairs:
                            last = nc.tensor.matmul(psum[:, t, 0:D], oT[:, c, t * P:(t + 1) * P], wo[:, c, :],
                                                    start=(c == 0), stop=(c == PG * NG - 1))
                        return last

                    pe.wait_ge(S["max_taken"], TILES)
                    pe.wait_ge(S["exp"], TILES)
                    pe.wait_ge(S["oT_norm"], PG * (NG - 1))
                    for t in range(TT):
                        if t >= TT - PG:
                            spread(NG - 1, t - (TT - PG))
                        project_out(t, range(PG * (NG - 1)))
                    pe.wait_ge(S["oT_norm"], PG * NG)
                    for t in range(TT):
                        last = project_out(t, range(PG * (NG - 1), PG * NG))
                        if t % 2:
                            last.then_inc(S["y_filled"], 1)
                    norm.tensor(nc, pe, 0, bank[0:DC])
                    mlp_tensor(nc, pe, S, bank, hT_mlp, w1, w2, g, norm)

            nc.all_engine_barrier(sems_to_clear=S.range)


def mask_rows(nc, io):
    with ExitStack() as ctx:
        sb = lambda n, s, d: ctx.enter_context(nc.sbuf_tensor(n, s, d))
        m8, v32 = sb("mask_u8", [B, T], U8), sb("mask_f32", [B, T], FP32)
        v16, bar = sb("mask_bf16", [B, T], BF16), sb("mask_bar", [B, T], BF16)
        s_in = ctx.enter_context(nc.semaphore("mask_in"))
        s_v = ctx.enter_context(nc.semaphore("mask_steps"))
        s_out = ctx.enter_context(nc.semaphore("mask_out"))
        with nc.Block() as block:

            @block.sync
            def _(sp):
                sp.dma_start(m8[:, :], io["mask"]).then_inc(s_in, 16)
                sp.wait_ge(s_v, 3)
                sp.dma_start(io["valid"], v32[:, :]).then_inc(s_out, 16)
                sp.dma_start(io["valid16"], v16[:, :]).then_inc(s_out, 16)
                sp.dma_start(io["bar16"], bar[:, :]).then_inc(s_out, 16)
                sp.wait_ge(s_out, 48)

            @block.vector
            def _(dve):
                dve.wait_ge(s_in, 16)
                nc.vector.tensor_copy(v32[:, :], m8[:, :]).then_inc(s_v, 1)
                nc.vector.tensor_copy(v16[:, :], m8[:, :]).then_inc(s_v, 1)
                nc.vector.tensor_scalar(bar[:, :], m8[:, :], 1.0, 1e9, ALU.subtract, ALU.mult).then_inc(s_v, 1)
    nc.all_engine_barrier()


def mamba_layer(nc, consts, io, tag, mod0, eps):
    ident, ones, mod, x = consts["ident"], consts["ones"], consts["mod"], consts["x"]
    shift1, scale1, gate1, shift2, scale2, gate2 = (k * DC for k in range(6))
    n_mod = 6 * DC
    PAD = TAPS - 1
    UNITS = IC * UB * NB
    SLOTS = 2 * NB
    XP_BANKS = (6, 7, 4, 5, 2, 3)
    RING = 3
    with ExitStack() as ctx:
        def sb(name, shape, dt, where=ctx):
            return where.enter_context(nc.sbuf_tensor(f"{tag}_{name}", shape, dt))

        win = sb("win", [P, DC, 2 * DI], FP32)
        x_dt = sb("xproj_dt", [P, IC, P], FP32)
        x_b4 = sb("xproj_b", [P, IC, DPU, NS], FP32)
        x_c4 = sb("xproj_c", [P, IC, DPU, NS], FP32)
        dtw = sb("dtw", [P, DI], FP32)
        wout = sb("wout", [P, IC, D], FP32)
        w1, w2 = sb("w1", [P, DC, HID], FP32), sb("w2", [P, DC, HID], FP32)
        w3 = sb("w3", [P, HC, D], FP32)
        cw = sb("conv_w", [P, IC, TAPS], FP32)
        cb, dtb, dp = (sb(n, [P, IC], FP32) for n in ("conv_b", "dtb", "dp"))
        a_log = sb("a_log", [P, UNITS], FP32)
        a_neg = sb("a_neg", [P, UNITS], FP32)
        spread = sb("spread", [SPLIT * NS, UB, P], BF16)
        gather = sb("gather", [P, UB * NS], FP32)
        cur = sb("cur", [P, n_mod], FP32)
        sz = sb("silu_z", [P, IC, T], FP32)
        xs = sb("xs", [P, IC, 2, T], FP32)
        b_rep, c_rep = sb("b_rep", [P, 2, T], FP32), sb("c_rep", [P, 2, T], FP32)
        y = sb("y", [P, T], FP32)
        S = Semaphores(consts["pool"], LN_SEMS + [
            "cur", "gate_diag", "gate_filled", "gate_rows", "pads", "in_filled", "in_taken", "tap0", "taps", "xs",
            "xp_filled", "xp", "dt_filled", "abs", "exp_abs", "ln", "relu", "dt", "dtx", "part1", "rest",
            "part2", "part3", "parts_out0", "parts_out1", "parts_out2", "parts_out3", "stacks", "late_stacks", "scan_pads", "e_filled", "x_filled",
            "decay", "bx", "scan", "hc", "y_sum", "combine", "y_filled", "res", "up_filled", "silu",
            "prod", "down_filled"])
        s_w, s_i, s_p, s_a = consts["init_sems"]
        psum = ctx.enter_context(nc.psum_tensor(f"{tag}_psum", [P, 8, T], FP32))
        bank = [psum[:, n, :] for n in range(8)]
        dt_psum = psum[:, 0:2, :]
        dt_banks = lambda c: psum[:, 2 * (c % 2):2 * (c % 2) + 2, :]
        up_bank = lambda j, k: bank[4 + 2 * (j % 2) + k]
        x_psum = lambda i: psum[:, 2 * (i % 2) + 2:2 * (i % 2) + 4, :]
        y_psum = psum[:, 6:8, :]
        scratch = nc.dram_tensor(f"{tag}_parts_dram", (IC, SPLIT, P, 2, 2, T), BF16, kind="Internal").ap()
        gate_rows = sb("gate_rows", [P, 2, D], FP32)
        with ExitStack() as early:
            sb_early = lambda name, shape, dt: sb(name, shape, dt, early)
            norm = Norm(sb_early, S, ident, consts["half"], eps)
            hT, hT_mlp = sb("hT", [P, DC, T], FP32, early), sb("hT_mlp", [P, DC, T], FP32, early)
            ahead = NormAhead(norm, consts, sb_early, hT, mod0, n_mod, scale1, shift1)
            gates = Gates(sb_early, S, cur, ident, ones, bank[1], [gate1, gate2], gate_rows)
            tmp = sb("res_tmp", [P, 2, 2, D], FP32, early)
            hid = sb("hid", [P, HC, T], FP32, early)
            xp = sb("x_padded", [P, IC, T + 2 * PAD], FP32, early)
            dtl = sb("dt_low", [P, 2, T], FP32, early)
            lg = sb("softplus", [P, IC, 2, T], FP32, early)
            dd = sb("dt_and_dtx", [P, 2, 2, 2, T], FP32, early)
            parts = sb("parts", [P, 2, SPLIT, 2, 2, T], BF16, early)
        stack = sb("stack", [SPLIT * NS, 2, NB, 2, 2, T], BF16)
        decay = sb("decay", [P, RING, 2, T + 1], FP32)
        bx = sb("bx", [P, RING, 2, T + 1], FP32)
        h = sb("h", [P, RING, 2, T + 1], FP32)
        hc = sb("hc", [P, SLOTS, 2, T], FP32)

        with nc.Block() as block:

            @block.sync
            def _(sp):
                n = 0
                for to, of in ((win, "win"), (wout, "wout"), (w1, "w1"), (w2, "w2"), (w3, "w3")):
                    sp.dma_start(to[:, :, :], io[tag + of].rearrange("(c p) n -> p c n", p=P)).then_inc(s_w, 16)
                    n += 1
                xpv = io[tag + "xp"].rearrange("(c p) n -> p c n", p=P)
                for r in range(DPU):
                    sp.dma_start(x_b4[:, :, r, :], xpv[:, :, DTR:DTR + NS]).then_inc(s_w, 16)
                    sp.dma_start(x_c4[:, :, r, :], xpv[:, :, DTR + NS:DTR + 2 * NS]).then_inc(s_w, 16)
                    n += 2
                sp.dma_start(cw[:, :, :], io[tag + "conv_w"].rearrange("(c p) k -> p c k", p=P)).then_inc(s_w, 16)
                for to, of in ((cb, "conv_b"), (dtb, "dtb"), (dp, "dp")):
                    sp.dma_start(to[:, :], io[tag + of]).then_inc(s_w, 16)
                sp.wait_ge(s_i, 2)
                sp.dma_start(x_dt[:, :, 0:DTR], xpv[:, :, 0:DTR]).then_inc(s_w, 16)
                sp.dma_start(dtw[0:DTR, :], io[tag + "dtw"]).then_inc(s_w, 16)
                sp.wait_ge(s_w, 16 * (n + 6))

            @block.vector
            def _(dve):
                nc.vector.memset(x_dt[:, :, :], 0.0).then_inc(s_i, 1)
                nc.vector.memset(dtw[:, :], 0.0).then_inc(s_i, 1)
                nc.vector.memset(gather[:, :], 0.0).then_inc(s_i, 1)
                dve.wait_ge(s_i, 3)
                for a in range(DPU):
                    nc.vector.memset(gather[NS * a:NS * (a + 1), a::NS + DPU], 1.0).then_inc(s_i, 1)
                dve.wait_ge(s_a, 17)
                nc.vector.tensor_scalar(a_neg[:, :], a_neg[:, :], -1.0, None, ALU.mult).then_inc(s_i, 1)

            @block.scalar
            def _(act):
                act.dma_start(a_log[:, :], io[tag + "alog"]).then_inc(s_a, 16)
                act.wait_ge(s_a, 16)
                nc.scalar.activation(a_neg[:, :], a_log[:, :], ACT.Exp).then_inc(s_a, 1)

            @block.gpsimd
            def _(pool):
                nc.gpsimd.memset(spread[:, :, :], 0.0).then_inc(s_p, 1)
                view = spread[:, :, :].rearrange("p u (a n) -> p u a n", a=DPU)
                for j in range(SPLIT):
                    pool.wait_ge(s_p, j + 1)
                    nc.gpsimd.affine_select(out=view, in_=view, compare_op=ALU.not_equal, fill=1.0, base=-NS * j,
                                            pattern=[[-DPU, UB], [-1, DPU], [0, NS]],
                                            channel_multiplier=1).then_inc(s_p, 1)

        nc.all_engine_barrier(sems_to_clear=range(s_w.num, s_a.num + 1))

        def stack_in(sp, c, loaded):
            for j in range(SPLIT):
                sp.dma_start(stack[NS * j:NS * (j + 1), c % 2, :, :, :, :].rearrange("d k q w t -> d k (q w t)"),
                             scratch[c, j].rearrange("(k d) q w t -> d k (q w t)", d=NS)).then_inc(loaded, 16)

        def between_sync(sp, end):
            parts_out(sp, (0, 1))
            if end:
                sp.wait_ge(S["res"], 8)
            for c in range(2):
                sp.wait_ge(S[f"parts_out{c}"], 16 * SPLIT)
                stack_in(sp, c, S["stacks"])
            parts_out(sp, (2, 3))
            sp.wait_ge(S["stacks"], 16 * SPLIT * 2)
            for c in range(2, IC):
                sp.wait_ge(S[f"parts_out{c}"], 16 * SPLIT)

        def parts_out(sp, chunks):
            for j in range(SPLIT):
                for c in chunks:
                    sp.wait_ge(S[f"part{j + 1}"], c + 1)
                    sp.dma_start(scratch[c, j].rearrange("p q w t -> p (q w t)"),
                                 parts[:, c % 2, j, :, :, :].rearrange("p q w t -> p (q w t)"))\
                        .then_inc(S[f"parts_out{c}"], 16)

        def between_gpsimd(pool, end):
            norm.gpsimd(nc, pool, 0)
            nc.gpsimd.memset(xp[:, :, 0:PAD], 0.0).then_inc(S["pads"], 1)
            pool.wait_ge(S["pads"], 1)
            nc.gpsimd.memset(xp[:, :, PAD + T:], 0.0).then_inc(S["pads"], 1)
            if end:
                norm.gpsimd(nc, pool, 1)

        def between_vector(dve, x_end, nxt, combine):
            end = x_end is not None
            if end:
                dve.wait_ge(S["cur"], 1)
                gates.vector(nc, dve)
            ahead.vector(nc, dve, nxt, 0)
            if end:
                combine(IC - 1)
            dve.wait_ge(S["pads"], 2)
            for c in range(IC):
                for j in range(1, TAPS):
                    for w in range(2):
                        if j == 1:
                            dve.wait_ge(S["tap0"], 2 * c + w + 1)
                        else:
                            dve.wait_ge(S["taps"], 2 * ((TAPS - 1) * c + j - 2) + w + 1)
                        src = xp[:, c, j:j + T] if w == 0 else xp[:, c, T + 2 * PAD - 1 - j:2 * PAD - 1 - j:-1]
                        nc.vector.scalar_tensor_tensor(xs[:, c, w, :], src, cw[:, c, j:j + 1], xs[:, c, w, :],
                                                       ALU.mult, ALU.add).then_inc(S["taps"], 1)

            if end:
                dve.wait_ge(S["gate_rows"], 1)
                residual(nc, dve, S, bank[0:2], None, gates.rows[:, 0, :], tmp, x_end, 0, "y_filled")
                norm.vector(nc, dve, x_end, 1)

            def dt_and_dtx(c):
                dve.wait_ge(S["abs"], c + 1)
                if c >= 2:
                    dve.wait_ge(S["part3"], c - 1)
                nc.vector.tensor_scalar(dd[:, c % 2, 0, :, :], dt_banks(c), dtb[:, c:c + 1],
                                        0.0, ALU.add, ALU.max).then_inc(S["relu"], 1)
                dve.wait_ge(S["ln"], c + 1)
                dve.wait_ge(S["relu"], c + 1)
                nc.vector.tensor_tensor(dd[:, c % 2, 0, :, :], dd[:, c % 2, 0, :, :], lg[:, c, :, :],
                                        ALU.add).then_inc(S["dt"], 1)
                dve.wait_ge(S["dt"], c + 1)
                nc.vector.tensor_tensor(dd[:, c % 2, 1, :, :], dd[:, c % 2, 0, :, :], xs[:, c, :, :],
                                        ALU.mult).then_inc(S["dtx"], 1)

            def rest(c):
                dve.wait_ge(S["part1"], c + 1)
                nc.vector.tensor_tensor(dd[:, c % 2, :, :, :], dd[:, c % 2, :, :, :],
                                        parts[:, c % 2, 0, :, :, :], ALU.subtract).then_inc(S["rest"], 1)

            def part3(c):
                dve.wait_ge(S["part2"], c + 1)
                nc.vector.tensor_tensor(parts[:, c % 2, 2, :, :, :], dd[:, c % 2, :, :, :],
                                        parts[:, c % 2, 1, :, :, :], ALU.subtract).then_inc(S["part3"], 1)

            def prod(j):
                if end:
                    dve.wait_ge(S["silu"], j + 1)
                    dve.wait_ge(S["up_filled"], j + 1)
                    nc.vector.tensor_tensor(hid[:, j, :], hid[:, j, :], up_bank(j, 1), ALU.mult).then_inc(S["prod"], 1)

            dt_and_dtx(0)
            dt_and_dtx(1)
            prod(0)
            rest(0)
            prod(1)
            rest(1)
            part3(0)
            prod(2)
            part3(1)
            if end:
                residual(nc, dve, S, bank[6:8], None, gates.rows[:, 1, :], tmp, x_end, 1, "down_filled")
            dt_and_dtx(2)
            dt_and_dtx(3)
            rest(2)
            rest(3)
            part3(2)
            part3(3)

        def between_scalar(act, end):
            if end:
                gates.scalar(nc, act)
            ahead.scalar(nc, act, 0, bank[2:2 + DC])
            act.wait_ge(S["pads"], 2)
            if end:
                act.wait_ge(S["combine"], 4 * IC)
            for c in range(IC):
                act.wait_ge(S["in_filled"], c + 1)
                nc.scalar.activation(xp[:, c, PAD:PAD + T], bank[2 + c], ACT.Copy).then_inc(S["in_taken"], 1)
                act.wait_ge(S["in_taken"], c + 1)
                for w in range(2):
                    src = xp[:, c, 0:T] if w == 0 else xp[:, c, T + 2 * PAD - 1:2 * PAD - 1:-1]
                    nc.scalar.activation(xs[:, c, w, :], src, ACT.Identity, bias=cb[:, c:c + 1],
                                         scale=cw[:, c, 0:1]).then_inc(S["tap0"], 1)

            def silu_z():
                for c in range(IC):
                    act.wait_ge(S["in_filled"], IC + c + 1)
                    nc.scalar.activation(sz[:, c, :], bank[2 + c], ACT.Silu).then_inc(S["in_taken"], 1)

            for c in range(IC):
                if c == 2:
                    silu_z()
                for w in range(2):
                    act.wait_ge(S["taps"], 2 * ((TAPS - 1) * c + TAPS - 2) + w + 1)
                    nc.scalar.activation(xs[:, c, w, :], xs[:, c, w, :], ACT.Silu).then_inc(S["xs"], 1)
            if end:
                norm.scalar(nc, act, 1, bank[0:DC], hT_mlp, cur, scale2, shift2)
            for n, to in enumerate((dtl, dtl, b_rep, b_rep, c_rep, c_rep)):
                act.wait_ge(S["xp_filled"], n + 1)
                nc.scalar.activation(to[:, n % 2, :], bank[XP_BANKS[n]], ACT.Copy).then_inc(S["xp"], 1)

            def ln_exp(chunks):
                for c in chunks:
                    act.wait_ge(S["dt_filled"], c + 1)
                    nc.scalar.activation(lg[:, c, :, :], dt_banks(c), ACT.Abs, bias=dtb[:, c:c + 1])\
                        .then_inc(S["abs"], 1)
                for c in chunks:
                    act.wait_ge(S["abs"], c + 1)
                    nc.scalar.activation(lg[:, c, :, :], lg[:, c, :, :], ACT.Exp, scale=-1.0).then_inc(S["exp_abs"], 1)
                for c in chunks:
                    act.wait_ge(S["exp_abs"], c + 1)
                    nc.scalar.activation(lg[:, c, :, :], lg[:, c, :, :], ACT.Ln, bias=1.0).then_inc(S["ln"], 1)

            def part1(c):
                act.wait_ge(S["dtx"], c + 1)
                if c >= 2:
                    act.wait_ge(S[f"parts_out{c - 2}"], 16 * SPLIT)
                nc.scalar.activation(parts[:, c % 2, 0, :, :, :], dd[:, c % 2, :, :, :], ACT.Copy)\
                    .then_inc(S["part1"], 1)

            def part2(c):
                act.wait_ge(S["rest"], c + 1)
                nc.scalar.activation(parts[:, c % 2, 1, :, :, :], dd[:, c % 2, :, :, :], ACT.Copy)\
                    .then_inc(S["part2"], 1)

            def silu_up(j):
                if end:
                    act.wait_ge(S["up_filled"], j + 1)
                    nc.scalar.activation(hid[:, j, :], up_bank(j, 0), ACT.Silu).then_inc(S["silu"], 1)

            ln_exp((0, 1))
            silu_up(0)
            part1(0)
            silu_up(1)
            part1(1)
            part2(0)
            silu_up(2)
            part2(1)
            ln_exp((2, 3))
            part1(2)
            part1(3)
            part2(2)
            part2(3)

        def between_tensor(pe, end):
            if end:
                pe.wait_ge(S["decay"], UNITS)
                gates.tensor(nc, pe)
                pe.wait_ge(S["bx"], UNITS)
            norm.tensor(nc, pe, 0, bank[2:2 + DC])
            pe.wait_ge(S["hT"], DC)

            def project_in(m):
                if m >= IC:
                    pe.wait_ge(S["in_taken"], m - IC + 1)
                for c in range(DC):
                    last = nc.tensor.matmul(bank[2 + m % 4], win[:, c, m * P:(m + 1) * P], hT[:, c, :],
                                            start=(c == 0), stop=(c == DC - 1))
                last.then_inc(S["in_filled"], 1)

            for m in range(IC):
                project_in(m)
            if end:
                pe.wait_ge(S["gate_rows"], 1)
                pe.wait_ge(S["combine"], 4 * IC)
                for t in range(TT):
                    for c in range(IC):
                        last = nc.tensor.matmul(bank[t // 2][:, (t % 2) * D:(t % 2 + 1) * D],
                                                sz[:, c, t * P:(t + 1) * P], wout[:, c, :],
                                                start=(c == 0), stop=(c == IC - 1))
                    if t % 2:
                        last.then_inc(S["y_filled"], 1)
            for m in range(IC, 2 * IC):
                project_in(m)
            pe.wait_ge(S["in_taken"], 2 * IC)
            for c in range(IC):
                if c == 2 and end:
                    norm.tensor(nc, pe, 1, bank[0:DC])
                pe.wait_ge(S["xs"], 2 * (c + 1))
                for n, w in enumerate((x_dt, x_dt, x_b4, x_b4, x_c4, x_c4)):
                    stat = w[:, c, :] if w is x_dt else w[:, c, :, :].rearrange("p a n -> p (a n)")
                    last = nc.tensor.matmul(bank[XP_BANKS[n]], stat, xs[:, c, n % 2, :],
                                            start=(c == 0), stop=(c == IC - 1))
                    if c == IC - 1:
                        last.then_inc(S["xp_filled"], 1)
            pe.wait_ge(S["xp"], 6)
            if end:
                pe.wait_ge(S["hT"], 2 * DC)

            def dt(c):
                if c >= 2:
                    pe.wait_ge(S["relu"], c - 1)
                    pe.wait_ge(S["abs"], c - 1)
                for w in range(2):
                    last = nc.tensor.matmul(dt_banks(c)[:, w, :], dtw[:, c * P:(c + 1) * P], dtl[:, w, :],
                                            start=True, stop=True)
                last.then_inc(S["dt_filled"], 1)

            dt(0)
            dt(1)
            if end:
                for j in range(HC):
                    if j >= 2:
                        pe.wait_ge(S["prod"], j - 1)
                    for k, w in enumerate((w1, w2)):
                        for c in range(DC):
                            last = nc.tensor.matmul(up_bank(j, k), w[:, c, j * P:(j + 1) * P], hT_mlp[:, c, :],
                                                    start=(c == 0), stop=(c == DC - 1))
                    last.then_inc(S["up_filled"], 1)
            dt(2)
            dt(3)
            if end:
                pe.wait_ge(S["prod"], HC)
                for t in range(TT):
                    for j in range(HC):
                        last = nc.tensor.matmul(bank[6 + t // 2][:, (t % 2) * D:(t % 2 + 1) * D],
                                                hid[:, j, t * P:(t + 1) * P], w3[:, j, :],
                                                start=(j == 0), stop=(j == HC - 1))
                    if t % 2:
                        last.then_inc(S["down_filled"], 1)

        with nc.Block() as block:

            @block.sync
            def _(sp):
                between_sync(sp, False)

            @block.gpsimd
            def _(pool):
                between_gpsimd(pool, False)

            @block.vector
            def _(dve):
                between_vector(dve, None, 0, None)

            @block.scalar
            def _(act):
                between_scalar(act, False)

            @block.tensor
            def _(pe):
                between_tensor(pe, False)

        nc.all_engine_barrier(sems_to_clear=S.range)

        with nc.Fori(0, B) as b:
            nxt = (b + 1) % B
            x_of_b = x[:, bass.ds(b, 1), :, :].rearrange("p b t d -> p (b t) d")
            with nc.Block() as block:

                @block.sync
                def _(sp):
                    for c in range(2, IC):
                        sp.wait_ge(S["x_filled"], UB * NB * (c - 1))
                        stack_in(sp, c, S["late_stacks"])
                        sp.wait_ge(S["late_stacks"], 16 * SPLIT * (c - 1))
                    between_sync(sp, True)

                @block.gpsimd
                def _(pool):
                    nc.gpsimd.memset(decay[:, :, :, T:], 0.0).then_inc(S["scan_pads"], 1)
                    nc.gpsimd.memset(bx[:, :, :, T:], 0.0).then_inc(S["scan_pads"], 1)
                    for i in range(UNITS):
                        pool.wait_ge(S["scan"], i + 1)
                        if i >= SLOTS:
                            pool.wait_ge(S["y_sum"], 2 * (i // NB - 1))
                        nc.gpsimd.tensor_tensor(hc[:, i % SLOTS, :, :], h[:, i % RING, :, 0:T], c_rep[:, :, :],
                                                ALU.mult).then_inc(S["hc"], 1)
                    between_gpsimd(pool, True)

                @block.vector
                def _(dve):
                    nc.vector.tensor_copy(cur[:, :], mod[:, bass.ds(b, 1), mod0:mod0 + n_mod]
                                          .rearrange("p b m -> p (b m)")).then_inc(S["cur"], 1)

                    def scan_unit(i):
                        dve.wait_ge(S["decay"], i + 1)
                        dve.wait_ge(S["bx"], i + 1)
                        if i >= RING:
                            dve.wait_ge(S["hc"], i - RING + 1)
                        both = lambda ring: ring[:, i % RING, :, :].rearrange("p w t -> p (w t)")
                        nc.vector.tensor_tensor_scan(both(h), both(decay), both(bx), 0.0,
                                                     ALU.mult, ALU.add).then_inc(S["scan"], 1)

                    def combine(c):
                        dve.wait_ge(S["y_sum"], 2 * UB * (c + 1))
                        steps = (
                            lambda: nc.vector.scalar_tensor_tensor(y[:, :], xs[:, c, 0, :], dp[:, c:c + 1], y_psum[:, 0, :],
                                                                   ALU.mult, ALU.add),
                            lambda: nc.vector.scalar_tensor_tensor(y[:, :], xs[:, c, 1, ::-1], dp[:, c:c + 1], y[:, :],
                                                                   ALU.mult, ALU.add),
                            lambda: nc.vector.tensor_tensor(y[:, :], y_psum[:, 1, ::-1], y[:, :], ALU.add),
                            lambda: nc.vector.tensor_tensor(sz[:, c, :], y[:, :], sz[:, c, :], ALU.mult))
                        for k, step in enumerate(steps):
                            if c or k:
                                dve.wait_ge(S["combine"], len(steps) * c + k)
                            step().then_inc(S["combine"], 1)

                    per_chunk = UB * NB
                    dve.wait_ge(S["scan_pads"], 2)
                    for i in range(UNITS + 1):
                        if i < UNITS:
                            dve.wait_ge(S["x_filled"], i + 1)
                            if i >= RING:
                                dve.wait_ge(S["scan"], i - RING + 1)
                            nc.vector.tensor_tensor(bx[:, i % RING, :, 0:T], x_psum(i), b_rep[:, :, :],
                                                    ALU.mult).then_inc(S["bx"], 1)
                        if i:
                            scan_unit(i - 1)
                        if i > per_chunk and i % per_chunk == 5:
                            combine(i // per_chunk - 1)
                    between_vector(dve, x_of_b, nxt, combine)

                @block.scalar
                def _(act):
                    for i in range(UNITS):
                        unit = (i // (UB * NB)) * UB * NB + (i % NB) * UB + (i // NB) % UB
                        act.wait_ge(S["e_filled"], i + 1)
                        if i >= RING:
                            act.wait_ge(S["scan"], i - RING + 1)
                        nc.scalar.activation(decay[:, i % RING, :, 0:T], dt_psum, ACT.Exp, scale=a_neg[:, unit:unit + 1])\
                            .then_inc(S["decay"], 1)
                    act.wait_ge(S["cur"], 1)
                    between_scalar(act, True)

                @block.tensor
                def _(pe):
                    def y_sum(k, w):
                        c, u = k // UB, k % UB
                        if u == 0 and c:
                            pe.wait_ge(S["combine"], 4 * c)
                        pe.wait_ge(S["hc"], NB * (k + 1))
                        for j in range(NB):
                            last = nc.tensor.matmul(y_psum[NS * j:NS * (j + 1), w, :],
                                                    gather[:, NS * u:NS * (u + 1)],
                                                    hc[:, (NB * k + j) % SLOTS, w, :],
                                                    start=(u == 0), stop=(u == UB - 1))
                        last.then_inc(S["y_sum"], 1)

                    for i in range(UNITS):
                        c, u, j = i // (UB * NB), (i // NB) % UB, i % NB
                        if i % (UB * NB) == 0 and c >= 2:
                            pe.wait_ge(S["late_stacks"], 16 * SPLIT * (c - 1))
                        if i:
                            pe.wait_ge(S["decay"], i)
                        for w in range(2):
                            last = nc.tensor.matmul(dt_psum[:, w, :], spread[:, u, :], stack[:, c % 2, j, 0, w, :],
                                                    start=True, stop=True)
                        last.then_inc(S["e_filled"], 1)
                        if i >= 2:
                            pe.wait_ge(S["bx"], i - 1)
                        for w in range(2):
                            last = nc.tensor.matmul(x_psum(i)[:, w, :], spread[:, u, :], stack[:, c % 2, j, 1, w, :],
                                                    start=True, stop=True)
                        last.then_inc(S["x_filled"], 1)
                        if i % 2 and i > NB + 2:
                            y_sum((i - 3) // NB - 1, (i - 3) % NB // 2)
                    for i in range(UNITS + 1, UNITS + 6, 2):
                        y_sum((i - 3) // NB - 1, (i - 3) % NB // 2)
                    between_tensor(pe, True)

            nc.all_engine_barrier(sems_to_clear=S.range)


_INPUTS = {
    "x": lambda a: a["x"],
    "condT": lambda a: a["cond_1024"].T,
    "mask": lambda a: a["mask_BxS_bk1"],
    "mod_w": lambda a: _join(1, a["L0_cond_Wln1"], a["L0_cond_Wln2"], a["L1_cond_W_mod"], a["L2_cond_ada_w"].T,
                             a["L3_cond_adaln1_W"], a["L3_cond_adaln2_W"]),
    "mod_b": lambda a: _columns(_join(0, a["L0_cond_bln1"], a["L0_cond_bln2"], a["L1_cond_b_mod"], a["L2_cond_ada_b"],
                                      a["L3_cond_adaln1_b"], a["L3_cond_adaln2_b"])),
    "norm_w": lambda a: _columns(_join(0, a["L3_cond_norm1_w"], a["L3_cond_norm2_w"])),
    "norm_b": lambda a: _columns(_join(0, a["L3_cond_norm1_b"], a["L3_cond_norm2_b"])),
    "l0_wq": lambda a: a["L0_cond_Wq"], "l0_wk": lambda a: a["L0_cond_Wk"], "l0_wv": lambda a: a["L0_cond_Wv"],
    "l0_wo": lambda a: a["L0_cond_Wo"], "l0_w1": lambda a: a["L0_cond_W1"], "l0_w2": lambda a: a["L0_cond_W2"],
    "l0_bq": lambda a: _columns(a["L0_cond_bq"]), "l0_bk": lambda a: _columns(a["L0_cond_bk"]), "l0_bv": lambda a: a["L0_cond_bv"],
    "l0_bo": lambda a: a["L0_cond_bo"], "l0_b1": lambda a: _columns(a["L0_cond_b1"]), "l0_b2": lambda a: a["L0_cond_b2"],
    "l1_wq": lambda a: a["L1_cond_W_qkv"][:, 0:INNER1], "l1_wk": lambda a: a["L1_cond_W_qkv"][:, INNER1:2 * INNER1],
    "l1_wv": lambda a: a["L1_cond_W_qkv"][:, 2 * INNER1:], "l1_wo": lambda a: a["L1_cond_W_out"],
    "l1_bo": lambda a: a["L1_cond_b_out"], "l1_w1": lambda a: a["L1_cond_W1"], "l1_b1": lambda a: _columns(a["L1_cond_b1"]),
    "l1_w2": lambda a: a["L1_cond_W2"], "l1_b2": lambda a: a["L1_cond_b2"],
    "l2_wq": lambda a: a["L2_cond_qkv_w"][0:D].T, "l2_wk": lambda a: a["L2_cond_qkv_w"][D:2 * D].T,
    "l2_wv": lambda a: a["L2_cond_qkv_w"][2 * D:].T, "l2_wo": lambda a: a["L2_cond_proj_w"].T,
    "l2_w1": lambda a: a["L2_cond_fc1_w"].T, "l2_w2": lambda a: a["L2_cond_fc2_w"].T,
    "l2_bq": lambda a: _columns(a["L2_cond_qkv_b"][0:D]), "l2_bk": lambda a: _columns(a["L2_cond_qkv_b"][D:2 * D]),
    "l2_bv": lambda a: a["L2_cond_qkv_b"][2 * D:], "l2_bo": lambda a: a["L2_cond_proj_b"],
    "l2_b1": lambda a: _columns(a["L2_cond_fc1_b"]), "l2_b2": lambda a: a["L2_cond_fc2_b"],
    "l3_win": lambda a: a["L3_cond_in_proj_W"], "l3_conv_w": lambda a: a["L3_cond_conv_w"].reshape(DI, TAPS),
    "l3_conv_b": lambda a: _columns(a["L3_cond_conv_b"]), "l3_xp": lambda a: a["L3_cond_x_proj_W"],
    "l3_dtw": lambda a: a["L3_cond_dt_proj_W"], "l3_dtb": lambda a: _columns(a["L3_cond_dt_proj_b"]),
    "l3_alog": lambda a: _columns(a["L3_cond_A_log"]), "l3_dp": lambda a: _columns(a["L3_cond_Dp"]),
    "l3_wout": lambda a: a["L3_cond_out_proj_W"], "l3_w1": lambda a: a["L3_cond_w1"],
    "l3_w2": lambda a: a["L3_cond_w2"], "l3_w3": lambda a: a["L3_cond_w3"],
}


def _columns(v):
    return v.reshape(-1, P).T


def _join(axis, *arrays):
    import numpy as np
    return np.concatenate(arrays, axis=axis)


BODY_SEMS = 60


def program(nc, io, out):
    for name, dt in (("valid", FP32), ("valid16", BF16), ("bar16", BF16)):
        io[name] = nc.dram_tensor(f"{name}_dram", (B, T), dt, kind="Internal").ap()
    with ExitStack() as ctx:
        sb = lambda n, s, d: ctx.enter_context(nc.sbuf_tensor(n, s, d))
        consts = {"x": sb("x_sb", [P, B, TT, D], FP32), "ident": sb("ident", [P, P], FP32),
                  "ones": sb("ones", [P, P], FP32), "mod": sb("mod", [P, B, MODS], FP32),
                  "half": sb("minus_half", [P, TT], FP32)}
        consts["init_sems"] = [ctx.enter_context(nc.semaphore(n)) for n in ("weights", "init", "init_sel", "init_a")]
        consts["pool"] = [ctx.enter_context(nc.semaphore(f"body{n}")) for n in range(BODY_SEMS)]
        modulation(nc, consts, io)
        narrow_attention_layer(nc, consts, io, "l0_", MOD0, 1e-5, masked=False)
        wide_attention_layer(nc, consts, io, "l1_", MOD1, 1e-5)
        mask_rows(nc, io)
        narrow_attention_layer(nc, consts, io, "l2_", MOD2, 1e-6, masked=True)
        mamba_layer(nc, consts, io, "l3_", MOD3, 1e-5)
        store(nc, consts, out)


def store(nc, consts, out):
    s_out = nc.alloc_semaphore("out")
    with nc.Block() as block:

        @block.sync
        def _(sp):
            sp.dma_start(out.rearrange("b (t p) d -> p (b t) d", p=P),
                         consts["x"][:, :, :, :].rearrange("p b t d -> p (b t) d")).then_inc(s_out, 16)
            sp.wait_ge(s_out, 16)


def kernel(**inputs):
    import numpy as np
    import concourse.bacc as bacc
    from concourse.bass_utils import run_bass_kernel_spmd

    nc = bacc.Bacc("TRN2", target_bir_lowering=False, num_devices=1)
    given = {k: np.asarray(v) for k, v in inputs.items()}
    arrays, io = {}, {}
    for name, lay in _INPUTS.items():
        a = np.ascontiguousarray(lay(given))
        arrays[f"in_{name}"] = a
        io[name] = nc.dram_tensor(f"in_{name}", a.shape, mybir.dt.from_np(a.dtype), kind="ExternalInput").ap()
    out = nc.dram_tensor("out_x", (B, T, D), FP32, kind="ExternalOutput").ap()
    program(nc, io, out)
    r = run_bass_kernel_spmd(nc, [arrays], core_ids=[0])
    return r.results[0]["out_x"]
```
